# Optimizing a Trainium2 kernel written in Bass

```python
import numpy as np
import jax
import jax.numpy as jnp

def _softmax(x, axis=-1):
    return jax.nn.softmax(x, axis=axis)

def _gelu(x):
    return jax.nn.gelu(x, approximate=True)

def _silu(x):
    return jax.nn.silu(x)

def _sigmoid(x):
    return jax.nn.sigmoid(x)

def _layernorm(x, axis=-1, eps=1e-05):
    m = jnp.mean(x, axis=axis, keepdims=True)
    v = jnp.var(x, axis=axis, keepdims=True)
    return (x - m) / jnp.sqrt(v + eps)

def _scatter_add(tgt, idx, src, axis=0):
    return tgt.at[idx].add(src)

def _segment_sum(src, seg, n):
    return jax.ops.segment_sum(src, seg, n)
kernel_name = 'mk_cond_seq_d4_seqx_r8_f69d2c'

def setup_inputs(seed: int=0):
    np.random.seed(seed)
    _w = jnp.asarray

    def _rec_inputs():
        import jax
        import jax.numpy as jnp
        _rk = jax.random.key(seed)
        x = -0.000125 + 0.9999 * jax.random.normal(jax.random.fold_in(_rk, 1), (64, 32, 128), jnp.float32)
        _lenS = 32 - jax.random.randint(jax.random.fold_in(_rk, 7), (64,), 0, max(1, 32 // 4) + 1, jnp.int32)
        _lenS2 = 32 - jax.random.randint(jax.random.fold_in(_rk, 8), (64,), 0, max(1, 32 // 4) + 1, jnp.int32)
        condB_safetyscore = -0.927215 + 0.920279 * jax.random.normal(jax.random.fold_in(_rk, 11), (64,), jnp.float32)
        itok_B_6_14 = jax.random.randint(jax.random.fold_in(_rk, 12), (64,), 6, 15, jnp.int32)
        itok_B_0_7 = jax.random.randint(jax.random.fold_in(_rk, 13), (64,), 0, 8, jnp.int32)
        condB_theta = jax.random.uniform(jax.random.fold_in(_rk, 14), (64,), jnp.float32, 0.0, 0.983423)
        condB_phi = jax.random.uniform(jax.random.fold_in(_rk, 15), (64,), jnp.float32, 0.0, 0.961312)
        return (x, condB_safetyscore, itok_B_6_14, itok_B_0_7, condB_theta, condB_phi)
    x, condB_safetyscore, itok_B_6_14, itok_B_0_7, condB_theta, condB_phi = _rec_inputs()

    def _L0_cond_setup():
        import jax, jax.numpy as jnp
        import numpy as np
        TEMPERATURE = 1.0
        ACT_THRESHOLD = 0.1
        MAX_ACT = 1.0
        SAFETY_KNOB = 1.0
        EPS = 1e-08

        def gram_schmidt(X):
            r = X.shape[1]
            Q = X
            for i in range(r):
                q = Q[:, i]
                q = q / (jnp.linalg.norm(q) + EPS)
                Q = Q.at[:, i].set(q)
                coeffs = q @ Q[:, i + 1:]
                Q = Q.at[:, i + 1:].add(-jnp.outer(q, coeffs))
            return Q
        key = jax.random.key(seed)
        ks = jax.random.split(key, 8)
        B, S, D, R = (8, 512, 128, 32)
        init_std = 0.02
        return {'hidden_states': jax.random.normal(ks[0], (B, S, D), jnp.float32), 'safety_score': jax.random.normal(ks[1], (B,), jnp.float32), 'U': jax.random.normal(ks[2], (D, R), jnp.float32) * init_std, 'V': jax.random.normal(ks[3], (D, R), jnp.float32) * init_std, 'safety_bias': jnp.zeros((D,), jnp.float32), 'gate_w1': jax.random.normal(ks[4], (D // 4, D), jnp.float32) * (1.0 / np.sqrt(D)), 'gate_b1': jnp.zeros((D // 4,), jnp.float32), 'gate_w2': jax.random.normal(ks[5], (1, D // 4), jnp.float32) * (1.0 / np.sqrt(D // 4)), 'gate_b2': jnp.zeros((1,), jnp.float32), 'resp_w': jax.random.normal(ks[6], (D, R), jnp.float32) * (1.0 / np.sqrt(R)), 'resp_b': jnp.zeros((D,), jnp.float32)}
    _L0_cond_all = _L0_cond_setup()
    _L0_cond_in = {k: v for k, v in _L0_cond_all.items() if k in ('U', 'V', 'safety_bias', 'gate_w1', 'gate_b1', 'gate_w2', 'gate_b2', 'resp_w', 'resp_b')}
    del _L0_cond_all

    def _L1_cond_setup():
        import jax, jax.numpy as jnp
        import numpy as np
        D = 128
        E = 8
        FF = 512
        TOPK = 2
        S = 32
        SE = 64
        SH = 128
        B, T = (2, 256)

        def _forward(x, subject_ids, ln_g, ln_b, subj_emb, hyp_w1, hyp_b1, hyp_w2, hyp_b2, sty_w1, sty_b1, sty_w2, sty_b2, router_w, exp_w1, exp_b1, exp_w2, exp_b2):
            mu = x.mean(-1, keepdims=True)
            var = x.var(-1, keepdims=True)
            h = (x - mu) * jax.lax.rsqrt(var + 1e-05) * ln_g + ln_b
            m_t = h.mean(1, keepdims=True)
            v_t = h.var(1, keepdims=True)
            h_norm = (h - m_t) * jax.lax.rsqrt(v_t + 1e-08)
            se = subj_emb[subject_ids]
            hyp = jax.nn.relu(se @ hyp_w1 + hyp_b1) @ hyp_w2 + hyp_b2
            sty = jax.nn.relu(hyp @ sty_w1 + sty_b1) @ sty_w2 + sty_b2
            gamma, beta = jnp.split(sty, 2, axis=-1)
            gamma = jax.nn.softplus(gamma) + 1e-08
            h = h_norm * gamma[:, None, :] + beta[:, None, :]
            h_flat = h.reshape(-1, D)
            probs = jax.nn.softmax(h_flat @ router_w, axis=-1)
            gates, idx = jax.lax.top_k(probs, TOPK)
            gates = gates / gates.sum(-1, keepdims=True)
            N = h_flat.shape[0]
            combine = jnp.zeros((N, E), h_flat.dtype).at[jnp.arange(N)[:, None], idx].add(gates)
            hid = jax.nn.relu(jnp.einsum('nd,edf->nef', h_flat, exp_w1) + exp_b1)
            eout = jnp.einsum('nef,efd->ned', hid, exp_w2) + exp_b2
            y = jnp.einsum('ned,ne->nd', eout, combine)
            return x + y.reshape(x.shape)
        key = jax.random.key(seed)
        ks = jax.random.split(key, 16)
        n = lambda k, sh, s=0.02: jax.random.normal(k, sh, dtype=jnp.float32) * s
        return {'x': jax.random.normal(ks[0], (B, T, D), dtype=jnp.float32), 'subject_ids': jax.random.randint(ks[1], (B,), 0, S), 'ln_g': jnp.ones((D,), jnp.float32), 'ln_b': jnp.zeros((D,), jnp.float32), 'subj_emb': n(ks[2], (S, SE)), 'hyp_w1': n(ks[3], (SE, SH), 1.0 / np.sqrt(SE)), 'hyp_b1': jnp.zeros((SH,), jnp.float32), 'hyp_w2': n(ks[4], (SH, SH), 1.0 / np.sqrt(SH)), 'hyp_b2': jnp.zeros((SH,), jnp.float32), 'sty_w1': n(ks[5], (SH, SH // 2), 1.0 / np.sqrt(SH)), 'sty_b1': jnp.zeros((SH // 2,), jnp.float32), 'sty_w2': n(ks[6], (SH // 2, 2 * D), 1.0 / np.sqrt(SH // 2)), 'sty_b2': jnp.zeros((2 * D,), jnp.float32), 'router_w': n(ks[7], (D, E), 1.0 / np.sqrt(D)), 'exp_w1': n(ks[8], (E, D, FF), 1.0 / np.sqrt(D)), 'exp_b1': jnp.zeros((E, FF), jnp.float32), 'exp_w2': n(ks[9], (E, FF, D), 1.0 / np.sqrt(FF)), 'exp_b2': jnp.zeros((E, D), jnp.float32)}
    _L1_cond_all = _L1_cond_setup()
    _L1_cond_in = {k: v for k, v in _L1_cond_all.items() if k in ('ln_g', 'ln_b', 'subj_emb', 'hyp_w1', 'hyp_b1', 'hyp_w2', 'hyp_b2', 'sty_w1', 'sty_b1', 'sty_w2', 'sty_b2', 'router_w', 'exp_w1', 'exp_b1', 'exp_w2', 'exp_b2')}
    del _L1_cond_all

    def _L2_cond_setup():
        import jax, jax.numpy as jnp
        import numpy as np
        E, H, I = (8, 128, 512)
        B, S = (4, 128)
        LN_EPS = 1e-12
        key = jax.random.key(seed)
        ks = jax.random.split(key, 8)
        x = jax.random.normal(ks[0], (B, S, H), dtype=jnp.float32)
        expert_idx = jax.random.randint(ks[1], (B,), 0, E, dtype=jnp.int64)
        Wi = jax.random.normal(ks[2], (E, H, I), dtype=jnp.float32) * 0.02
        bi = jnp.zeros((E, I), dtype=jnp.float32)
        Wo = jax.random.normal(ks[3], (E, I, H), dtype=jnp.float32) * 0.02
        bo = jnp.zeros((E, H), dtype=jnp.float32)
        gamma = jnp.ones((E, H), dtype=jnp.float32)
        beta = jnp.zeros((E, H), dtype=jnp.float32)
        return {'input_tensor': x, 'expert_idx': expert_idx, 'Wi': Wi, 'bi': bi, 'Wo': Wo, 'bo': bo, 'gamma': gamma, 'beta': beta}
    _L2_cond_all = _L2_cond_setup()
    _L2_cond_in = {k: v for k, v in _L2_cond_all.items() if k in ('Wi', 'bi', 'Wo', 'bo', 'gamma', 'beta')}
    del _L2_cond_all

    def _L3_cond_setup():
        import jax, jax.numpy as jnp
        import numpy as np
        key = jax.random.key(seed)
        k1, k2, k3 = jax.random.split(key, 3)
        B, N, D = (16, 512, 128)
        embeddings = jax.random.normal(k1, (B, N, D), dtype=jnp.float32)
        theta = jax.random.uniform(k2, (B,), dtype=jnp.float32)
        phi = jax.random.uniform(k3, (B,), dtype=jnp.float32)
        return {'embeddings': embeddings, 'theta': theta, 'phi': phi}
    _L3_cond_all = _L3_cond_setup()
    _L3_cond_in = {k: v for k, v in _L3_cond_all.items() if k in ()}
    del _L3_cond_all
    return {'x': x, 'condB_safetyscore': condB_safetyscore, 'itok_B_6_14': itok_B_6_14, 'itok_B_0_7': itok_B_0_7, 'condB_theta': condB_theta, 'condB_phi': condB_phi, 'L0_cond_U': _L0_cond_in['U'], 'L0_cond_V': _L0_cond_in['V'], 'L0_cond_safety_bias': _L0_cond_in['safety_bias'], 'L0_cond_gate_w1': _L0_cond_in['gate_w1'], 'L0_cond_gate_b1': _L0_cond_in['gate_b1'], 'L0_cond_gate_w2': _L0_cond_in['gate_w2'], 'L0_cond_gate_b2': _L0_cond_in['gate_b2'], 'L0_cond_resp_w': _L0_cond_in['resp_w'], 'L0_cond_resp_b': _L0_cond_in['resp_b'], 'L1_cond_ln_g': _L1_cond_in['ln_g'], 'L1_cond_ln_b': _L1_cond_in['ln_b'], 'L1_cond_subj_emb': _L1_cond_in['subj_emb'], 'L1_cond_hyp_w1': _L1_cond_in['hyp_w1'], 'L1_cond_hyp_b1': _L1_cond_in['hyp_b1'], 'L1_cond_hyp_w2': _L1_cond_in['hyp_w2'], 'L1_cond_hyp_b2': _L1_cond_in['hyp_b2'], 'L1_cond_sty_w1': _L1_cond_in['sty_w1'], 'L1_cond_sty_b1': _L1_cond_in['sty_b1'], 'L1_cond_sty_w2': _L1_cond_in['sty_w2'], 'L1_cond_sty_b2': _L1_cond_in['sty_b2'], 'L1_cond_router_w': _L1_cond_in['router_w'], 'L1_cond_exp_w1': _L1_cond_in['exp_w1'], 'L1_cond_exp_b1': _L1_cond_in['exp_b1'], 'L1_cond_exp_w2': _L1_cond_in['exp_w2'], 'L1_cond_exp_b2': _L1_cond_in['exp_b2'], 'L2_cond_Wi': _L2_cond_in['Wi'], 'L2_cond_bi': _L2_cond_in['bi'], 'L2_cond_Wo': _L2_cond_in['Wo'], 'L2_cond_bo': _L2_cond_in['bo'], 'L2_cond_gamma': _L2_cond_in['gamma'], 'L2_cond_beta': _L2_cond_in['beta']}

def reference(x, condB_safetyscore, itok_B_6_14, itok_B_0_7, condB_theta, condB_phi, L0_cond_U, L0_cond_V, L0_cond_safety_bias, L0_cond_gate_w1, L0_cond_gate_b1, L0_cond_gate_w2, L0_cond_gate_b2, L0_cond_resp_w, L0_cond_resp_b, L1_cond_ln_g, L1_cond_ln_b, L1_cond_subj_emb, L1_cond_hyp_w1, L1_cond_hyp_b1, L1_cond_hyp_w2, L1_cond_hyp_b2, L1_cond_sty_w1, L1_cond_sty_b1, L1_cond_sty_w2, L1_cond_sty_b2, L1_cond_router_w, L1_cond_exp_w1, L1_cond_exp_b1, L1_cond_exp_w2, L1_cond_exp_b2, L2_cond_Wi, L2_cond_bi, L2_cond_Wo, L2_cond_bo, L2_cond_gamma, L2_cond_beta):
    import jax
    import jax.numpy as jnp

    def _L0_cond_ref(hidden_states, safety_score, U, V, safety_bias, gate_w1, gate_b1, gate_w2, gate_b2, resp_w, resp_b):
        import jax, jax.numpy as jnp
        import numpy as np
        TEMPERATURE = 1.0
        ACT_THRESHOLD = 0.1
        MAX_ACT = 1.0
        SAFETY_KNOB = 1.0
        EPS = 1e-08

        def gram_schmidt(X):
            r = X.shape[1]
            Q = X
            for i in range(r):
                q = Q[:, i]
                q = q / (jnp.linalg.norm(q) + EPS)
                Q = Q.at[:, i].set(q)
                coeffs = q @ Q[:, i + 1:]
                Q = Q.at[:, i + 1:].add(-jnp.outer(q, coeffs))
            return Q
        R = resp_w.shape[1]
        U_o = gram_schmidt(U)
        V_o = gram_schmidt(V)
        basis = U_o @ V_o.T
        pooled = hidden_states.mean(axis=1)
        h1 = jax.nn.relu(pooled @ gate_w1.T + gate_b1)
        base_act = jax.nn.sigmoid(h1 @ gate_w2.T + gate_b2)
        mod = jax.nn.sigmoid(safety_score[:, None] / TEMPERATURE)
        knob = jnp.clip(jnp.asarray(SAFETY_KNOB, hidden_states.dtype), ACT_THRESHOLD, MAX_ACT)
        strength = (base_act * mod * knob)[:, None, :]
        proj = hidden_states @ basis
        feats = proj @ basis.T[:, :R]
        response = feats @ resp_w.T + resp_b + safety_bias
        return hidden_states + strength * response

    def _L1_cond_ref(x, subject_ids, ln_g, ln_b, subj_emb, hyp_w1, hyp_b1, hyp_w2, hyp_b2, sty_w1, sty_b1, sty_w2, sty_b2, router_w, exp_w1, exp_b1, exp_w2, exp_b2):
        import jax, jax.numpy as jnp
        import numpy as np
        D = 128
        E = 8
        FF = 512
        TOPK = 2
        S = 32
        SE = 64
        SH = 128
        B, T = (2, 256)

        def _forward(x, subject_ids, ln_g, ln_b, subj_emb, hyp_w1, hyp_b1, hyp_w2, hyp_b2, sty_w1, sty_b1, sty_w2, sty_b2, router_w, exp_w1, exp_b1, exp_w2, exp_b2):
            mu = x.mean(-1, keepdims=True)
            var = x.var(-1, keepdims=True)
            h = (x - mu) * jax.lax.rsqrt(var + 1e-05) * ln_g + ln_b
            m_t = h.mean(1, keepdims=True)
            v_t = h.var(1, keepdims=True)
            h_norm = (h - m_t) * jax.lax.rsqrt(v_t + 1e-08)
            se = subj_emb[subject_ids]
            hyp = jax.nn.relu(se @ hyp_w1 + hyp_b1) @ hyp_w2 + hyp_b2
            sty = jax.nn.relu(hyp @ sty_w1 + sty_b1) @ sty_w2 + sty_b2
            gamma, beta = jnp.split(sty, 2, axis=-1)
            gamma = jax.nn.softplus(gamma) + 1e-08
            h = h_norm * gamma[:, None, :] + beta[:, None, :]
            h_flat = h.reshape(-1, D)
            probs = jax.nn.softmax(h_flat @ router_w, axis=-1)
            gates, idx = jax.lax.top_k(probs, TOPK)
            gates = gates / gates.sum(-1, keepdims=True)
            N = h_flat.shape[0]
            combine = jnp.zeros((N, E), h_flat.dtype).at[jnp.arange(N)[:, None], idx].add(gates)
            hid = jax.nn.relu(jnp.einsum('nd,edf->nef', h_flat, exp_w1) + exp_b1)
            eout = jnp.einsum('nef,efd->ned', hid, exp_w2) + exp_b2
            y = jnp.einsum('ned,ne->nd', eout, combine)
            return x + y.reshape(x.shape)
        return _forward(x, subject_ids, ln_g, ln_b, subj_emb, hyp_w1, hyp_b1, hyp_w2, hyp_b2, sty_w1, sty_b1, sty_w2, sty_b2, router_w, exp_w1, exp_b1, exp_w2, exp_b2)

    def _L2_cond_ref(input_tensor, expert_idx, Wi, bi, Wo, bo, gamma, beta):
        import jax, jax.numpy as jnp
        import numpy as np
        E, H, I = (8, 128, 512)
        B, S = (4, 128)
        LN_EPS = 1e-12
        Wi_b = Wi[expert_idx]
        bi_b = bi[expert_idx]
        Wo_b = Wo[expert_idx]
        bo_b = bo[expert_idx]
        g_b = gamma[expert_idx]
        be_b = beta[expert_idx]
        h = jax.nn.gelu(jnp.einsum('bsh,bhi->bsi', input_tensor, Wi_b) + bi_b[:, None, :], approximate=False)
        o = jnp.einsum('bsi,bih->bsh', h, Wo_b) + bo_b[:, None, :]
        r = o + input_tensor
        mu = jnp.mean(r, axis=-1, keepdims=True)
        var = jnp.mean(jnp.square(r - mu), axis=-1, keepdims=True)
        y = (r - mu) * jax.lax.rsqrt(var + LN_EPS)
        return y * g_b[:, None, :] + be_b[:, None, :]

    def _L3_cond_ref(embeddings, theta, phi):
        import jax, jax.numpy as jnp
        import numpy as np
        B, N, D = embeddings.shape
        e = embeddings.reshape(B, N, D // 4, 4)
        ct = jnp.cos(theta)[:, None, None]
        st = jnp.sin(theta)[:, None, None]
        cp = jnp.cos(phi)[:, None, None]
        sp = jnp.sin(phi)[:, None, None]
        x0, x1, x2, x3 = (e[..., 0], e[..., 1], e[..., 2], e[..., 3])
        out = jnp.stack([x0 * ct + x1 * st, -x0 * st + x1 * ct, x2 * cp + x3 * sp, -x2 * sp + x3 * cp], axis=-1)
        return out.reshape(B, N, D)
    x = _L0_cond_ref(x, condB_safetyscore, L0_cond_U, L0_cond_V, L0_cond_safety_bias, L0_cond_gate_w1, L0_cond_gate_b1, L0_cond_gate_w2, L0_cond_gate_b2, L0_cond_resp_w, L0_cond_resp_b)
    x = _L1_cond_ref(x, itok_B_6_14, L1_cond_ln_g, L1_cond_ln_b, L1_cond_subj_emb, L1_cond_hyp_w1, L1_cond_hyp_b1, L1_cond_hyp_w2, L1_cond_hyp_b2, L1_cond_sty_w1, L1_cond_sty_b1, L1_cond_sty_w2, L1_cond_sty_b2, L1_cond_router_w, L1_cond_exp_w1, L1_cond_exp_b1, L1_cond_exp_w2, L1_cond_exp_b2)
    x = _L2_cond_ref(x, itok_B_0_7, L2_cond_Wi, L2_cond_bi, L2_cond_Wo, L2_cond_bo, L2_cond_gamma, L2_cond_beta)
    x = _L3_cond_ref(x, condB_theta, condB_phi)
    return x

_drawn_inputs = setup_inputs


def setup_inputs(seed=0):
    import zlib

    import numpy as np

    out = dict(_drawn_inputs(seed))
    spreads = {'L0_cond_safety_bias': (0.0, 0.462),
     'L0_cond_gate_b1': (0.0, 0.552),
     'L0_cond_resp_b': (0.0, 0.413),
     'L1_cond_ln_g': (1.0, 0.6),
     'L1_cond_ln_b': (0.0, 0.8),
     'L1_cond_hyp_b1': (0.0, 0.1),
     'L1_cond_hyp_b2': (0.0, 0.1),
     'L1_cond_sty_b1': (0.0, 0.1),
     'L1_cond_sty_b2': (0.0, 0.1),
     'L1_cond_exp_b1': (0.0, 0.1),
     'L1_cond_exp_b2': (0.0, 0.1),
     'L2_cond_bi': (0.0, 0.358),
     'L2_cond_bo': (0.0, 0.1),
     'L2_cond_gamma': (1.0, 0.2),
     'L2_cond_beta': (0.0, 0.1)}
    factors = {'L0_cond_V': 8.0, 'L0_cond_gate_w1': 2.977}
    for name, (base, spread) in spreads.items():
        noise = np.random.default_rng([zlib.crc32(name.encode()), seed]).standard_normal(out[name].shape)
        drawn = base * np.exp(spread * noise) if base else spread * noise
        out[name] = jnp.asarray(drawn.astype(out[name].dtype))
    for name, factor in factors.items():
        out[name] = (out[name] * factor).astype(out[name].dtype)
    return out
```

```python
import concourse.bass as bass
from concourse import mybir
from contextlib import ExitStack

F32, BF16, I32 = mybir.dt.float32, mybir.dt.bfloat16, mybir.dt.int32
ALU, ACT, AX = mybir.AluOpType, mybir.ActivationFunctionType, mybir.AxisListType

P = 128
D = 128
NS, T = 64, 32
NT = NS * T
TILES = NT // P
SPT = P // T
GT = 4
GROUPS = TILES // GT
GW = GT * P
SPG = GT * SPT
R = 32
E = 8
FF = 512
FC = FF // P
SUBJ, SE, SH = 32, 64, 128
NB1 = 2 * TILES + E - 1
NB2 = (NS + E * (SPT - 1)) // SPT
NY = 2
NE2 = 2
XW = D + 12
C_SLOT, C_GATE, C_COS, C_SIN = D, D + 2, D + 4, D + 8
EPS_GS, EPS_LN, EPS_T, EPS_SP, EPS_L2 = 1e-8, 1e-5, 1e-8, 1e-8, 1e-12
PI = 3.141592653589793
PI2_HI, PI2_LO = 6.28125, 2 * PI - 6.28125
ROUND = 12582912.0
SKIP = 1 << 20


def cond_seq_kernel(nc, x, score, ids1, ids2, theta, phi, U, V, safety_bias, gate_w1, gate_b1, gate_w2,
                    gate_b2, resp_w, resp_b, ln_g, ln_b, subj_emb, hyp_w1, hyp_b1, hyp_w2, hyp_b2,
                    sty_w1, sty_b1, sty_w2, sty_b2, router_w, exp_w1, exp_b1, exp_w2, exp_b2,
                    Wi, bi, Wo, bo, gamma2, beta2, out):
    ctx = ExitStack()
    with ctx:
        def sb(name, shape, dt=F32):
            return ctx.enter_context(nc.sbuf_tensor(name, shape, dt))

        def sem(name):
            return ctx.enter_context(nc.semaphore(name))

        w1 = sb("w1", [P, E, FF])
        w2 = sb("w2", [P, E, FC, D])
        wi = sb("wi", [P, E, FF])
        wo = sb("wo", [P, E, FC, D])
        b1c = sb("b1c", [P, E, FC])
        bic = sb("bic", [P, E, FC])
        brow = sb("brow", [E * FC, 2, P])
        b2r = sb("b2r", [P, E, D])
        bor = sb("bor", [P, E, D])
        g2r = sb("g2r", [P, E, D])
        be2r = sb("be2r", [P, E, D])
        Q = sb("Q", [P, 2, R])
        gw1 = sb("gw1", [R, D])
        rw = sb("rw", [P, R])
        col = sb("col", [P, 12])
        c_gb1, c_gw2, c_lng, c_lnb, c_hb1, c_hb2, c_sb1, c_sg, c_sbt = range(9)
        biasrow = sb("biasrow", [1, 2, D])
        gb2 = sb("gb2", [NS, 1])
        emb = sb("emb", [SUBJ, SE])
        hw1 = sb("hw1", [SE, SH])
        hw2 = sb("hw2", [SH, SH])
        sw1 = sb("sw1", [SH, SH // 2])
        sw2 = sb("sw2", [SH // 2, 2 * D])
        rout = sb("rout", [D, E])
        smp = sb("smp", [NS, 3])
        id1 = sb("id1", [SUBJ, NS], I32)
        id2 = sb("id2", [NS, 1], I32)
        ident = sb("ident", [P, P])
        tri = sb("tri", [P, P], BF16)
        ones = sb("ones", [P, P], BF16)
        onesrow = sb("onesrow", [1, P])
        mean4 = sb("mean4", [P, SPT])
        tmask = sb("tmask", [NS, TILES])
        smod = sb("smod", [NS, SPT, T])
        smodi = sb("smodi", [NS, 1], I32)
        smodf = sb("smodf", [NS, 1])
        qio = sb("qiota", [NS, SPT, T])
        io128 = sb("io128", [P, P], BF16)
        tileio = sb("tileio", [P, TILES, 2])
        down8 = sb("down8", [P, TILES, E])
        segm = sb("segm", [P, E, TILES])
        ones8 = sb("ones8", [P, E])
        pidx = sb("pidx", [P, 1])
        pmod = sb("pmod", [P, 1])
        pmodi = sb("pmodi", [P, 1], I32)
        pidxi = sb("pidxi", [P, 1], I32)
        mhalf = sb("mhalf", [P, 16])
        iob = sb("iob", [P, NB1])
        bstep = sb("bstep", [P, TILES])
        sstep = sb("sstep", [P, TILES])
        X = sb("X", [P, TILES, D])
        xT = sb("xT", [P, NT])
        x1r = sb("x1r", [P, TILES, XW])
        h0 = sb("h0", [P, TILES, D])
        hT = sb("hT", [P, NT])
        sq = xT
        hrow = X

        hdram = nc.dram_tensor("h_rows", [NT, D], F32).ap()
        xdram = nc.dram_tensor("x1_rows", [NT, XW], F32).ap()
        edram = nc.dram_tensor("expert_rows", [NB1 * P, D], F32).ap()

        sid = sb("sid", [SUBJ, NS])
        idf = sb("idf", [SUBJ, NS])
        gw1T = sb("gw1T", [D, R])
        rwT = sb("rwT", [R, D])
        pooledT = sb("pooledT", [D, NS])
        h1T = sb("h1T", [R, NS])
        seT = sb("seT", [SE, NS])
        hypT = sb("hypT", [SH, NS])
        hyp2T = sb("hyp2T", [SH, NS])
        styT = sb("styT", [SH // 2, NS])
        graw = sb("graw", [D, NS])
        gabs = sb("gabs", [D, NS])
        gexp = sb("gexp", [D, NS])
        gln = sb("gln", [D, NS])
        gpos = sb("gpos", [D, NS])
        gammaT = sb("gammaT", [D, NS])
        betaT = sb("betaT", [D, NS])
        gsn, gsd, gsr, gss = (sb(n, [P, 2]) for n in ("gsn", "gsd", "gsr", "gss"))
        crow = sb("crow", [1, D])
        crow4 = sb("crow4", [1, GT, D])
        fold = sb("fold", [R, 4, D])
        M = sb("M", [D, D])
        zs = sb("zs", [NS, 2])
        zexp = sb("zexp", [NS, 2])
        zden = sb("zden", [NS, 2])
        zsig = sb("zsig", [NS, 2])
        stren = sb("stren", [NS, 1])
        strtile = sb("strtile", [NS, TILES])
        strT = sb("strT", [P, TILES])
        bst = sb("bst", [P, TILES, 6])
        mv = sb("mv", [P, TILES, 2])
        ve, rs, nmr = (sb(n, [P, TILES]) for n in ("ve", "rs", "nmr"))
        tsum, tvar, tve, trs, tsc = (sb(n, [P, NS]) for n in ("tsum", "tvar", "tve", "trs", "tsc"))
        rt = lambda n, dt=F32: sb(n, [P, TILES, E], dt)
        rsh, rex, rp, req, rwt, o1, o2, rp2, slots, pick = (rt(n) for n in (
            "rsh", "rex", "rp", "req", "rwt", "o1", "o2", "rp2", "slots", "pick"))
        both = rt("both", BF16)
        rmx, rsum, rrec, m1, m2, mm1, mm2, gsum, grec = (sb(n, [P, TILES]) for n in (
            "rmx", "rsum", "rrec", "m1", "m2", "mm1", "mm2", "gsum", "grec"))
        tot, incl, texc, tbase = (sb(n, [P, E, TILES]) for n in ("tot", "incl", "texc", "tbase"))
        cmp8 = sb("cmp8", [P, E, TILES])
        nb, cb, cbe = (sb(n, [P, E]) for n in ("nb", "cb", "cbe"))
        cmpb = sb("cmpb", [P, NB1, E])
        bexf = sb("bexf", [P, NB1])
        bexi = sb("bexi", [P, NB1], I32)
        slotf = sb("slotf", [P, TILES, 2])
        sloti = sb("sloti", [P, TILES, 2], I32)
        slpi = sb("slpi", [P, TILES, 2], I32)
        slbi = sb("slbi", [P, TILES, 2], I32)
        slp = sb("slp", [P, TILES, 2])
        slb = sb("slb", [P, TILES, 2])
        ohp = sb("ohp", [P, 2 * TILES, P], BF16)
        eqb = h0[:].rearrange("p i d -> p (i d)")[:, 0:2 * TILES * NB1].rearrange("p (n b) -> p n b", b=NB1)
        tokb = sb("tokb", [P, 2 * TILES, 2, NB1], BF16)
        hilo = sb("hilo", [P, 2, NB1])
        mapf = sb("mapf", [P, NB1])
        map1 = sb("map1", [P, NB1], I32)
        id2f = sb("id2f", [NS, 1])
        a2 = sb("a2", [NS, E], BF16)
        a2f = sb("a2f", [NS, E])
        cnt2 = sb("cnt2", [P, E])
        cmp2 = sb("cmp2", [P, E, TILES])
        nb2, cb2, cbe2 = (sb(n, [P, E]) for n in ("nb2", "cb2", "cbe2"))
        slot2, slot2e = sb("slot2", [NS, 1]), sb("slot2e", [NS, E])
        io88 = sb("io88", [NS, SPT, NB2])
        oh88 = sb("oh88", [NS, SPT, NB2])
        tokv = sb("tokv", [NS, 2, T])
        cmpb2 = sb("cmpb2", [P, NB2, E])
        bex2f = sb("bex2f", [P, NB2])
        bex2i = sb("bex2i", [P, NB2], I32)
        map2f = sb("map2f", [P, 2, NB2])
        map2 = sb("map2", [P, 2, NB2], I32)
        ang = sb("ang", [NS, 4])
        angk, angr, angw, trig = (sb(n, [NS, 4]) for n in ("angk", "angr", "angw", "trig"))
        trig8 = sb("trig8", [NS, 8])
        trigt = sb("trigt", [NS, 8, TILES])
        hg = sb("hg", [P, 2, D])
        hgT = sb("hgT", [P, 2, P])
        ws = sb("ws", [P, 2, FF])
        hid = sb("hid", [P, 2, FC, P])
        es = sb("es", [P, 2, D])
        xg = sb("xg", [P, NB2, XW])
        eg = sb("eg", [P, NE2, 2, D])
        x2a = sb("x2a", [P, 2, D])
        x2 = sb("x2", [P, 2, D])
        x2b = sb("x2b", [P, 2, D])
        rr = sb("rr", [P, 2, D])
        st2 = sb("st2", [P, 6])
        mv2, ve2, rs2 = sb("mv2", [P, 2]), sb("ve2", [P, 1]), sb("rs2", [P, 2, 1])
        yn = sb("yn", [P, 2, D])
        yg = sb("yg", [P, 2, D])
        yb = sb("yb", [P, 2, D])
        yc = sb("yc", [P, 2, D])
        ysn = sb("ysn", [P, 2, D])
        yo = sb("yo", [P, NY, D])

        ps = [ctx.enter_context(nc.psum_tensor(f"bank{i}", [P, 512], F32)) for i in range(8)]

        def vec(v, n=P):
            return v.rearrange("(p o) -> p o", o=1)

        SMALL = [(gw1[:], gate_w1), (rw[:], resp_w), (gb2[:], gate_b2.partition_broadcast(NS)),
                 (emb[:], subj_emb), (hw1[:], hyp_w1), (hw2[:], hyp_w2), (sw1[:], sty_w1), (sw2[:], sty_w2),
                 (rout[:], router_w), (biasrow[:, 0, :], resp_b.rearrange("(o d) -> o d", o=1)),
                 (biasrow[:, 1, :], safety_bias.rearrange("(o d) -> o d", o=1)),
                 (smp[:, 0:1], vec(score)), (smp[:, 1:2], vec(theta)), (smp[:, 2:3], vec(phi)),
                 (id1[:], ids1.partition_broadcast(SUBJ)), (id2[:], vec(ids2)),
                 (col[0:R, c_gb1:c_gb1 + 1], vec(gate_b1)), (col[0:R, c_gw2:c_gw2 + 1], gate_w2.rearrange("o r -> r o")),
                 (col[:, c_lng:c_lng + 1], vec(ln_g)), (col[:, c_lnb:c_lnb + 1], vec(ln_b)),
                 (col[:, c_hb1:c_hb1 + 1], vec(hyp_b1)), (col[:, c_hb2:c_hb2 + 1], vec(hyp_b2)),
                 (col[0:SH // 2, c_sb1:c_sb1 + 1], vec(sty_b1)),
                 (col[:, c_sg:c_sg + 1], vec(sty_b2[0:D])), (col[:, c_sbt:c_sbt + 1], vec(sty_b2[D:2 * D]))]
        ROWS = [(brow[:, 0, :], exp_b1.rearrange("e (c p) -> (e c) p", p=P)),
                (brow[:, 1, :], bi.rearrange("e (c p) -> (e c) p", p=P)),
                (b2r[:], exp_b2.partition_broadcast(P)), (bor[:], bo.partition_broadcast(P)),
                (g2r[:], gamma2.partition_broadcast(P)), (be2r[:], beta2.partition_broadcast(P))]
        IOTAS = [(pidx[:], [[0, 1]], 0, 1), (pidxi[:], [[0, 1]], 0, 1), (io128[:], [[1, P]], 0, 0),
                 (tileio[:], [[1, TILES], [0, 2]], 0, 0), (down8[:], [[0, TILES], [-1, E]], E, 0),
                 (iob[:], [[1, NB1]], 0, 0), (bstep[:], [[P, TILES]], 0, 0), (sstep[:], [[SPT, TILES]], 0, 0),
                 (qio[:], [[1, SPT], [0, T]], 0, 0), (io88[:], [[1, SPT], [SPT, NB2]], 0, 0),
                 (tokv[:, 0, :], [[0, T]], 0, T), (tokv[:, 1, :], [[0, T]], -SKIP, T)]
        N_SMALL, N_ROWS, N_CONST, N_SIDE = len(SMALL), len(ROWS), 16 + len(IOTAS), TILES + 6

        (ld_uv, ld_x, ld_small, ld_w1, ld_w2, ld_wi, ld_wo, ld_rows, consts, dconsts, pool_own, act_own, dve_own,
         gs_dots, gs_norm, gs_step, xt_ps, xt_sb, pooled_ps, sid_ready, side_ps, side_sb, crow_ready,
         fold_ps, fold_sb, style_abs, style_exp, style_ready, z_sb, z_exp, str_in, str_ps, str_sb,
         resp_ps, x1_ready, var_ready, rs_ready, nmr_ready, h0_ready, h0T_ps, hT_raw, hT_centred, sq_ready,
         tvar_ready, trs_ready, h_scaled, h_ready, logit_ps, hrow_ps, hrow_sb, h_stored,
         logit_shift, logit_exp, onehots, rank_ps, places, map_in, map_ps, map_ready,
         a2_ready, rank2_ps, oh88_ready, map2_ps, map2_ready, ang_ready, trig_ready, trigt_ready, trig_ps,
         x_row_ready, bias_ps, bias_ready, x_stored, row_T_ps, row_T_sb, ws_ready, up_ps, hid_sb, down_ps, es_ready,
         x2_ready, xT2_ps, xT2_sb, wi_ready, up2_ps, hid2_sb, down2_ps, ve2_ready, rs2_ready,
         yo_ready) = map(sem, """
         ld_uv ld_x ld_small ld_w1 ld_w2 ld_wi ld_wo ld_rows consts dconsts pool_own act_own dve_own
         gs_dots gs_norm gs_step xt_ps xt_sb pooled_ps sid_ready side_ps side_sb crow_ready
         fold_ps fold_sb style_abs style_exp style_ready z_sb z_exp str_in str_ps str_sb
         resp_ps x1_ready var_ready rs_ready nmr_ready h0_ready h0T_ps hT_raw hT_centred sq_ready
         tvar_ready trs_ready h_scaled h_ready logit_ps hrow_ps hrow_sb h_stored
         logit_shift logit_exp onehots rank_ps places map_in map_ps map_ready
         a2_ready rank2_ps oh88_ready map2_ps map2_ready ang_ready trig_ready trigt_ready trig_ps
         x_row_ready bias_ps bias_ready x_stored row_T_ps row_T_sb ws_ready up_ps hid_sb down_ps es_ready
         x2_ready xT2_ps xT2_sb wi_ready up2_ps hid2_sb down2_ps ve2_ready rs2_ready
         yo_ready""".split())
        hg_ready = [sem(f"hg_ready{i}") for i in range(2)]
        es_stored = [sem(f"es_stored{i}") for i in range(2)]
        xg_ready = [sem(f"xg_ready{i}") for i in range(2)]
        eg_ready = [sem(f"eg_ready{i}") for i in range(NE2)]
        yo_stored = [sem(f"yo_stored{i}") for i in range(NY)]

        block = ctx.enter_context(nc.Block())

        def g128(t, g):
            return t[:, g * GT:(g + 1) * GT]

        @block.sync
        def _(sp):
            sp.dma_start(Q[:, 0, :], U).then_inc(ld_uv, 16)
            sp.dma_start(Q[:, 1, :], V).then_inc(ld_uv, 16)
            sp.dma_start(X[:], x.rearrange("(i s) t d -> (s t) i d", s=SPT)).then_inc(ld_x, 16)
            for dst, src in SMALL:
                sp.dma_start(dst, src).then_inc(ld_small, 16)
            sp.dma_start(w1[:], exp_w1.rearrange("e d f -> d e f")).then_inc(ld_w1, 16)
            sp.dma_start(w2[:], exp_w2.rearrange("e (c p) d -> p e c d", p=P)).then_inc(ld_w2, 16)
            for dst, src in ROWS:
                sp.dma_start(dst, src).then_inc(ld_rows, 16)
            sp.dma_start(wi[:], Wi.rearrange("e d f -> d e f")).then_inc(ld_wi, 16)
            sp.dma_start(wo[:], Wo.rearrange("e (c p) d -> p e c d", p=P)).then_inc(ld_wo, 16)
            for g in range(GROUPS):
                sp.wait_ge(hrow_sb, g + 1)
                sp.dma_start(hdram[g * GW:(g + 1) * GW, :].rearrange("(i p) d -> p i d", p=P),
                             g128(hrow, g)).then_inc(h_stored, 16)
            sp.wait_ge(x_row_ready, 1)
            sp.dma_start(xdram.rearrange("(i p) d -> p i d", p=P), x1r[:]).then_inc(x_stored, 16)

            def store(i, u):
                b = 2 * i + u
                sp.wait_ge(es_ready, b + 1)
                sp.dma_start(edram[bass.ds(b * P, P), :], es[:, u, :]).then_inc(es_stored[u], 16)
            with sp.Fori(0, NB1 // 2) as i:
                for u in range(2):
                    store(i, u)
            store(NB1 // 2, 0)

        @block.gpsimd
        def _(pool):
            count = [0]

            def const(ins):
                count[0] += 1
                ins.then_inc(consts, 1)
                pool.wait_ge(consts, count[0])

            const(pool.memset(ident[:], 0.0))
            const(pool.affine_select(out=ident[:], in_=ident[:], compare_op=ALU.not_equal, fill=1.0, base=0,
                                     pattern=[[-1, P]], channel_multiplier=1))
            const(pool.memset(mean4[:], 1.0 / T))
            const(pool.affine_select(out=mean4[:], in_=mean4[:], compare_op=ALU.is_ge, fill=0.0, base=0,
                                     pattern=[[-T, SPT]], channel_multiplier=1))
            const(pool.affine_select(out=mean4[:], in_=mean4[:], compare_op=ALU.is_ge, fill=0.0, base=T - 1,
                                     pattern=[[T, SPT]], channel_multiplier=-1))
            const(pool.memset(tri[:], 1.0))
            const(pool.affine_select(out=tri[:], in_=tri[:], compare_op=ALU.is_gt, fill=0.0, base=0,
                                     pattern=[[1, P]], channel_multiplier=-1))
            const(pool.memset(ones[:], 1.0))
            const(pool.memset(onesrow[:], 1.0))
            const(pool.memset(tmask[:], 1.0))
            const(pool.affine_select(out=tmask[:], in_=tmask[:], compare_op=ALU.is_ge, fill=0.0, base=0,
                                     pattern=[[-SPT, TILES]], channel_multiplier=1))
            const(pool.affine_select(out=tmask[:], in_=tmask[:], compare_op=ALU.is_ge, fill=0.0, base=SPT - 1,
                                     pattern=[[SPT, TILES]], channel_multiplier=-1))
            const(pool.memset(mhalf[:], -0.5))
            const(pool.memset(ones8[:], 1.0))
            const(pool.memset(segm[:], 1.0))
            const(pool.memset(segm[:, :, 0:1], 0.0))
            for dst, pattern, base, mult in IOTAS:
                const(pool.iota(dst, pattern=pattern, base=base, channel_multiplier=mult,
                                allow_small_or_imprecise_dtypes=True))
            assert count[0] == N_CONST

            for g in range(GROUPS):
                pool.wait_ge(var_ready, g + 1)
                pool.tensor_tensor(g128(rs, g), g128(ve, g), mhalf[:, 0:GT], ALU.pow).then_inc(rs_ready, 1)
            for g in range(GROUPS):
                pool.wait_ge(tvar_ready, g + 1)
                pool.tensor_tensor(trs[:, g * SPG:(g + 1) * SPG], tve[:, g * SPG:(g + 1) * SPG],
                                   mhalf[:, 0:SPG], ALU.pow).then_inc(trs_ready, 1)
            for g in range(GROUPS):
                pool.wait_ge(h_scaled, g + 1)
                h = hT[:, g * GW:(g + 1) * GW].rearrange("p (s t) -> p s t", t=T)
                pool.tensor_tensor(h, h, betaT[:, g * SPG:(g + 1) * SPG].unsqueeze(2).to_broadcast([P, SPG, T]),
                                   ALU.add).then_inc(h_ready, 1)

            pool.wait_ge(h_stored, 16 * GROUPS)
            pool.wait_ge(map_ready, 1)

            def gather_x(j):
                if j == 0:
                    pool.wait_ge(x_stored, 16)
                    pool.wait_ge(map2_ready, 1)
                if j >= 2:
                    pool.wait_ge(xg_ready[j % 2], 16 * (j // 2))
                pool.indirect_dma_start(
                    out=xg[:, j, :], out_offset=None, in_=xdram,
                    in_offset=bass.IndirectOffsetOnAxis(ap=map2[:, 0, j:j + 1], axis=0)).then_inc(xg_ready[j % 2], 16)

            for b in range(NB1):
                if b >= 2:
                    pool.wait_ge(row_T_ps, b - 1)
                pool.indirect_dma_start(
                    out=hg[:, b % 2, :], out_offset=None, in_=hdram,
                    in_offset=bass.IndirectOffsetOnAxis(ap=map1[:, b:b + 1], axis=0)).then_inc(hg_ready[b % 2], 16)
                if b >= 8 and b % 2 == 0 and (b - 8) // 2 < NB2:
                    gather_x((b - 8) // 2)
            for j in range((NB1 - 8 + 1) // 2, NB2):
                gather_x(j)
            pool.wait_ge(es_stored[0], 16 * ((NB1 + 1) // 2))
            pool.wait_ge(es_stored[1], 16 * (NB1 // 2))
            pool.wait_ge(xg_ready[0], 16 * ((NB2 + 1) // 2))
            pool.wait_ge(xg_ready[1], 16 * (NB2 // 2))

            def gather_e(j):
                if j >= NE2:
                    pool.wait_ge(x2_ready, j - NE2 + 1)
                for k in range(2):
                    pool.indirect_dma_start(
                        out=eg[:, j % NE2, k, :], out_offset=None, in_=edram,
                        in_offset=bass.IndirectOffsetOnAxis(
                            ap=xg[:, j, C_SLOT + k:C_SLOT + k + 1].bitcast(I32), axis=0)).then_inc(eg_ready[j % NE2], 16)

            gather_e(0)
            gather_e(1)
            for j in range(NB2):
                if j + 2 < NB2:
                    gather_e(j + 2)
                pool.wait_ge(ve2_ready, j + 1)
                pool.tensor_tensor(rs2[:, j % 2, :], ve2[:], mhalf[:, 0:1], ALU.pow).then_inc(rs2_ready, 1)
                pool.wait_ge(yo_ready, j + 1)
                pool.indirect_dma_start(
                    out=out.rearrange("s t d -> (s t) d"),
                    out_offset=bass.IndirectOffsetOnAxis(ap=map2[:, 1, j:j + 1], axis=0),
                    in_=yo[:, j % NY, :], in_offset=None, bounds_check=NT - 1, oob_is_err=False).then_inc(yo_stored[j % NY], 16)
            for u in range(NY):
                pool.wait_ge(yo_stored[u], 16 * len(range(u, NB2, NY)))

        @block.scalar
        def _(act):
            def side(n):
                if n < TILES:
                    act.wait_ge(xt_ps, n + 1)
                    act.activation(xT[:, n * P:(n + 1) * P], ps[1 + n % 2][:, 0:P], ACT.Copy).then_inc(xt_sb, 1)
                    return
                n -= TILES
                act.wait_ge(side_ps, n + 1)
                if n == 0:
                    act.wait_ge(pooled_ps, 1)
                    act.activation(gw1T[:], ps[4][:, 0:R], ACT.Copy)
                    act.activation(rwT[:], ps[4][0:R, P:2 * P], ACT.Copy)
                    last = act.activation(pooledT[:], ps[3][:, 0:NS], ACT.Copy)
                elif n == 1:
                    act.activation(h1T[:], ps[5][0:R, 0:NS], ACT.Relu, bias=col[0:R, c_gb1:c_gb1 + 1])
                    last = act.activation(seT[:], ps[5][0:SE, NS:2 * NS], ACT.Copy)
                elif n == 2:
                    act.activation(zs[:, 0:1], ps[6][0:NS, 0:1], ACT.Identity, bias=gb2[:])
                    act.activation(zs[:, 1:2], smp[:, 0:1], ACT.Copy)
                    last = act.activation(hypT[:], ps[6][:, NS:2 * NS], ACT.Relu, bias=col[:, c_hb1:c_hb1 + 1])
                elif n == 3:
                    last = act.activation(hyp2T[:], ps[5][:, 0:NS], ACT.Identity, bias=col[:, c_hb2:c_hb2 + 1])
                elif n == 4:
                    last = act.activation(styT[:], ps[6][0:SH // 2, 0:NS], ACT.Relu, bias=col[0:SH // 2, c_sb1:c_sb1 + 1])
                else:
                    act.activation(graw[:], ps[5][:, 0:NS], ACT.Identity, bias=col[:, c_sg:c_sg + 1])
                    act.activation(gabs[:], ps[5][:, 0:NS], ACT.Abs, bias=col[:, c_sg:c_sg + 1])
                    last = act.activation(betaT[:], ps[5][:, NS:2 * NS], ACT.Identity, bias=col[:, c_sbt:c_sbt + 1])
                last.then_inc(side_sb, 1)

            for i in range(R):
                act.wait_ge(gs_dots, i + 1)
                act.activation(gsn[:], ps[0][:, 0:2 * R:R], ACT.Sqrt).then_inc(gs_norm, 1)
                if 1 <= i <= N_SIDE:
                    if i == TILES + 1:
                        act.wait_ge(ld_small, 16 * N_SMALL)
                    side(i - 1)
            act.wait_ge(side_sb, N_SIDE - TILES)
            act.activation(zexp[:], zs[:], ACT.Exp, scale=-1.0).then_inc(z_exp, 1)
            act.activation(gexp[:], gabs[:], ACT.Exp, scale=-1.0).then_inc(act_own, 1)
            act.wait_ge(act_own, 1)
            act.activation(gln[:], gexp[:], ACT.Ln, bias=1.0).then_inc(style_exp, 1)
            for g in range(GROUPS):
                act.wait_ge(nmr_ready, g + 1)
                for t in range(g * GT, (g + 1) * GT):
                    last = act.activation(h0[:, t, :], x1r[:, t, 0:D], ACT.Identity, bias=nmr[:, t:t + 1],
                                          scale=rs[:, t:t + 1])
                last.then_inc(h0_ready, 1)
                act.wait_ge(h0T_ps, g + 1)
                act.activation(hT[:, g * GW:(g + 1) * GW], ps[4 + g % 2][:], ACT.Identity,
                               bias=col[:, c_lnb:c_lnb + 1], scale=col[:, c_lng:c_lng + 1]).then_inc(hT_raw, 1)
            for g in range(GROUPS):
                act.wait_ge(hT_centred, g + 1)
                cols = slice(g * GW, (g + 1) * GW)
                act.activation(sq[:, cols], hT[:, cols], ACT.Square).then_inc(sq_ready, 1)
            for g in range(GROUPS):
                act.wait_ge(hrow_ps, g + 1)
                act.activation(g128(hrow, g), ps[4 + g % 2][:].rearrange("p (i d) -> p i d", d=D),
                               ACT.Copy).then_inc(hrow_sb, 1)
            act.wait_ge(logit_shift, 1)
            act.activation(rex[:], rsh[:], ACT.Exp).then_inc(logit_exp, 1)
            act.wait_ge(ang_ready, 1)
            act.activation(trig[:], angw[:], ACT.Sin).then_inc(trig_ready, 1)

            def hidden(i, u):
                b = 2 * i + u
                e = act.value_load(bexi[0:1, bass.ds(b, 1)], min_val=0, max_val=E - 1)
                act.wait_ge(up_ps, b + 1)
                if not isinstance(i, int) or i > 0:
                    act.wait_ge(down_ps, b - 1)
                for c in range(FC):
                    last = act.activation(hid[:, u, c, :], ps[2 + u][:, c * P:(c + 1) * P], ACT.Relu,
                                          bias=b1c[:, bass.ds(e, 1), c])
                last.then_inc(hid_sb, 1)
            act.wait_ge(bias_ready, 1)
            act.wait_ge(places, 1)
            for u in range(2):
                hidden(0, u)
            with act.Fori(1, NB1 // 2) as i:
                for u in range(2):
                    hidden(i, u)
            hidden(NB1 // 2, 0)

            def hidden2(i, u):
                j = 2 * i + u
                e = act.value_load(bex2i[0:1, bass.ds(j, 1)], min_val=0, max_val=E - 1)
                act.wait_ge(up2_ps, j + 1)
                if not isinstance(i, int) or i > 0:
                    act.wait_ge(down2_ps, j - 1)
                for c in range(FC):
                    last = act.activation(hid[:, u, c, :], ps[2 + u][:, c * P:(c + 1) * P], ACT.Gelu,
                                          bias=bic[:, bass.ds(e, 1), c])
                last.then_inc(hid2_sb, 1)
            act.wait_ge(down_ps, NB1)
            for u in range(2):
                hidden2(0, u)
            with act.Fori(1, NB2 // 2) as i:
                for u in range(2):
                    hidden2(i, u)

        @block.tensor
        def _(pe):
            mm = pe.matmul

            def side(n):
                if n < TILES:
                    if n >= 2:
                        pe.wait_ge(xt_sb, n - 1)
                    pe.transpose(ps[1 + n % 2][:, 0:P], X[:, n, :], ident[:]).then_inc(xt_ps, 1)
                    m = mm(ps[3][:, n * SPT:(n + 1) * SPT], X[:, n, :], mean4[:], start=True, stop=True)
                    if n == TILES - 1:
                        m.then_inc(pooled_ps, 1)
                    return
                n -= TILES
                if n:
                    pe.wait_ge(side_sb, n)
                if n == 0:
                    pe.wait_ge(ld_small, 16 * N_SMALL)
                    pe.transpose(ps[4][:, 0:R], gw1[:], ident[0:R, 0:R])
                    last = pe.transpose(ps[4][0:R, P:2 * P], rw[:], ident[:])
                elif n == 1:
                    pe.wait_ge(sid_ready, 1)
                    mm(ps[5][0:R, 0:NS], gw1T[:], pooledT[:], start=True, stop=True)
                    last = mm(ps[5][0:SE, NS:2 * NS], emb[:], sid[:], start=True, stop=True)
                elif n == 2:
                    mm(ps[6][0:NS, 0:1], h1T[:], col[0:R, c_gw2:c_gw2 + 1], start=True, stop=True)
                    last = mm(ps[6][:, NS:2 * NS], hw1[:], seT[:], start=True, stop=True)
                elif n == 3:
                    last = mm(ps[5][:, 0:NS], hw2[:], hypT[:], start=True, stop=True)
                elif n == 4:
                    last = mm(ps[6][0:SH // 2, 0:NS], sw1[:], hyp2T[:], start=True, stop=True)
                else:
                    mm(ps[5][:, 0:NS], sw2[:, 0:D], styT[:], start=True, stop=True)
                    last = mm(ps[5][:, NS:2 * NS], sw2[:, D:2 * D], styT[:], start=True, stop=True)
                last.then_inc(side_ps, 1)

            pe.wait_ge(ld_uv, 32)
            for i in range(R):
                if i:
                    pe.wait_ge(gs_step, i)
                mm(ps[0][:, 0:R - i], Q[:, 0, i:i + 1].to_broadcast([P, P]), Q[:, 0, i:R], start=True, stop=True)
                mm(ps[0][:, R:2 * R - i], Q[:, 1, i:i + 1].to_broadcast([P, P]), Q[:, 1, i:R],
                   start=True, stop=True).then_inc(gs_dots, 1)
                if 1 <= i <= N_SIDE:
                    if i == 1:
                        pe.wait_ge(consts, N_CONST)
                        pe.wait_ge(ld_x, 16)
                    side(i - 1)
            pe.wait_ge(gs_step, R)
            mm(ps[0][0:R, 0:R], Q[:, 1, :], Q[:, 1, :], start=True, stop=True)
            mm(ps[0][0:R, P:2 * P], Q[0:R, 0, :], rwT[:], start=True, stop=True)
            pe.transpose(ps[0][0:R, 2 * P:3 * P], Q[:, 0, :], ident[:]).then_inc(fold_ps, 1)
            pe.wait_ge(fold_sb, 1)
            mm(ps[4][0:R, 0:D], fold[:, 0, 0:R], fold[:, 1, :], start=True, stop=True).then_inc(fold_ps, 1)
            pe.wait_ge(fold_sb, 2)
            mm(ps[5][:, 0:D], fold[:, 2, :], fold[:, 3, :], start=True, stop=True).then_inc(fold_ps, 1)
            pe.wait_ge(str_in, 1)
            mm(ps[3][:, 0:TILES], smod[:].rearrange("s q t -> s (q t)"), strtile[:], start=True, stop=True).then_inc(str_ps, 1)
            pe.wait_ge(fold_sb, 3)
            pe.wait_ge(crow_ready, 1)
            pe.wait_ge(xt_sb, TILES)
            for g in range(GROUPS):
                if g >= 2:
                    pe.wait_ge(x1_ready, g - 1)
                bank = ps[1 + g % 2]
                mm(bank[:], onesrow[:], crow4[:].rearrange("o i d -> o (i d)"), start=True, stop=False)
                for j in range(GT):
                    t = g * GT + j
                    last = mm(bank[:, j * D:(j + 1) * D], xT[:, t * P:(t + 1) * P], M[:], start=False, stop=(j == GT - 1))
                last.then_inc(resp_ps, 1)
            for g in range(GROUPS):
                pe.wait_ge(h0_ready, g + 1)
                if g >= 2:
                    pe.wait_ge(hT_raw, g - 1)
                for j in range(GT):
                    last = pe.transpose(ps[4 + g % 2][:, j * P:(j + 1) * P], h0[:, g * GT + j, :], ident[:])
                last.then_inc(h0T_ps, 1)
            for g in range(GROUPS):
                pe.wait_ge(h_ready, g + 1)
                for t in range(g * GT, (g + 1) * GT):
                    last = mm(ps[6][:, t * E:(t + 1) * E], hT[:, t * P:(t + 1) * P], rout[:], start=True, stop=True)
                last.then_inc(logit_ps, 1)
                pe.wait_ge(hT_raw, GROUPS)
                if g >= 2:
                    pe.wait_ge(hrow_sb, g - 1)
                for j in range(GT):
                    t = g * GT + j
                    last = pe.transpose(ps[4 + g % 2][:, j * D:(j + 1) * D], hT[:, t * P:(t + 1) * P], ident[:])
                last.then_inc(hrow_ps, 1)
            pe.wait_ge(onehots, 1)
            mm(ps[3][:, 0:P], tri[:], both[:].rearrange("p i e -> p (i e)"), start=True, stop=True)
            mm(ps[3][:, P:2 * P], ones[:], both[:].rearrange("p i e -> p (i e)"), start=True, stop=True).then_inc(rank_ps, 1)
            pe.wait_ge(map_in, 1)
            for n in range(2 * TILES):
                last = mm(ps[7][:, 0:2 * NB1], ohp[:, n, :], tokb[:, n, :, :].rearrange("p k b -> p (k b)"),
                          start=(n == 0), stop=(n == 2 * TILES - 1))
            last.then_inc(map_ps, 1)
            pe.wait_ge(a2_ready, 1)
            mm(ps[6][0:NS, 0:E], tri[0:NS, 0:NS], a2[:], start=True, stop=True)
            mm(ps[6][:, E:2 * E], ones[0:NS, :], a2[:], start=True, stop=True).then_inc(rank2_ps, 1)
            pe.wait_ge(oh88_ready, 1)
            for k in range(2):
                for q in range(SPT):
                    last = mm(ps[6][q * T:(q + 1) * T, (1 + k) * NB2:(2 + k) * NB2], tokv[:, k, :], oh88[:, q, :],
                              start=True, stop=True)
            last.then_inc(map2_ps, 1)
            pe.wait_ge(trigt_ready, 1)
            mm(ps[6][:, P:2 * P], smod[:].rearrange("s q t -> s (q t)"), trigt[:].rearrange("s k i -> s (k i)"),
               start=True, stop=True).then_inc(trig_ps, 1)

            pe.wait_ge(ld_rows, 16 * N_ROWS)
            for k in range(2):
                last = pe.transpose(ps[7][:, k * E * FC:(k + 1) * E * FC], brow[:, k, :], ident[0:E * FC, 0:E * FC])
            last.then_inc(bias_ps, 1)

            def rows_T(i, u):
                pe.wait_ge(hg_ready[u], 16 * (i + 1))
                if not isinstance(i, int) or i > 0:
                    pe.wait_ge(row_T_sb, 2 * i + u - 1)
                pe.transpose(ps[u][:, 0:P], hg[:, u, :], ident[:]).then_inc(row_T_ps, 1)

            def up(i, u):
                b = 2 * i + u
                pe.wait_ge(row_T_sb, b + 1)
                pe.wait_ge(ws_ready, b + 1)
                if not isinstance(i, int) or i > 0:
                    pe.wait_ge(hid_sb, b - 1)
                for c in range(FC):
                    last = mm(ps[2 + u][:, c * P:(c + 1) * P], ws[:, u, c * P:(c + 1) * P], hgT[:, u, :], start=True, stop=True)
                last.then_inc(up_ps, 1)

            def down(i, u):
                b = 2 * i + u
                e = pe.value_load(bexi[0:1, bass.ds(b, 1)], min_val=0, max_val=E - 1)
                pe.wait_ge(hid_sb, b + 1)
                if not isinstance(i, int) or i > 0:
                    pe.wait_ge(es_ready, b - 1)
                for c in range(FC):
                    last = mm(ps[4 + u][:, 0:D], hid[:, u, c, :], w2[:, bass.ds(e, 1), c, :], start=(c == 0), stop=(c == FC - 1))
                last.then_inc(down_ps, 1)

            pe.wait_ge(ld_w2, 16)
            rows_T(0, 0)
            rows_T(0, 1)
            up(0, 0)
            rows_T(1, 0)
            up(0, 1)
            down(0, 0)
            rows_T(1, 1)
            up(1, 0)
            down(0, 1)
            with pe.Fori(1, NB1 // 2 - 1) as i:
                rows_T(i + 1, 0)
                up(i, 1)
                down(i, 0)
                rows_T(i + 1, 1)
                up(i + 1, 0)
                down(i, 1)
            i = NB1 // 2 - 1
            rows_T(i + 1, 0)
            up(i, 1)
            down(i, 0)
            up(i + 1, 0)
            down(i, 1)
            down(i + 1, 0)

            def rows_T2(i, u):
                j = 2 * i + u
                pe.wait_ge(x2_ready, j + 1)
                pe.transpose(ps[u][:, 0:P], x2[:, u, :], ident[:]).then_inc(xT2_ps, 1)

            def up2(i, u):
                j = 2 * i + u
                pe.wait_ge(xT2_sb, j + 1)
                pe.wait_ge(wi_ready, j + 1)
                if not isinstance(i, int) or i > 0:
                    pe.wait_ge(hid2_sb, j - 1)
                for c in range(FC):
                    last = mm(ps[2 + u][:, c * P:(c + 1) * P], ws[:, u, c * P:(c + 1) * P], hgT[:, u, :], start=True, stop=True)
                last.then_inc(up2_ps, 1)

            def down2(i, u):
                j = 2 * i + u
                e = pe.value_load(bex2i[0:1, bass.ds(j, 1)], min_val=0, max_val=E - 1)
                pe.wait_ge(hid2_sb, j + 1)
                if not isinstance(i, int) or i > 0:
                    pe.wait_ge(ve2_ready, j - 1)
                for c in range(FC):
                    last = mm(ps[4 + u][:, 0:D], hid[:, u, c, :], wo[:, bass.ds(e, 1), c, :], start=(c == 0), stop=(c == FC - 1))
                last.then_inc(down2_ps, 1)

            pe.wait_ge(ld_wo, 16)
            pe.wait_ge(es_ready, NB1)
            rows_T2(0, 0)
            up2(0, 0)
            rows_T2(0, 1)
            up2(0, 1)
            down2(0, 0)
            rows_T2(1, 0)
            up2(1, 0)
            down2(0, 1)
            with pe.Fori(1, NB2 // 2 - 1) as i:
                rows_T2(i, 1)
                up2(i, 1)
                down2(i, 0)
                rows_T2(i + 1, 0)
                up2(i + 1, 0)
                down2(i, 1)
            i = NB2 // 2 - 1
            rows_T2(i, 1)
            up2(i, 1)
            down2(i, 0)
            down2(i, 1)

        @block.vector
        def _(dve):
            count = [0]

            def link(ins):
                count[0] += 1
                ins.then_inc(dve_own, 1)
                dve.wait_ge(dve_own, count[0])

            def masks():
                dve.wait_ge(consts, N_CONST)
                dve.wait_ge(ld_small, 16 * N_SMALL)
                link(dve.tensor_scalar(smodi[:], pidxi[0:NS, :], SPT - 1, None, ALU.bitwise_and))
                link(dve.tensor_scalar(pmodi[:], pidxi[:], T - 1, None, ALU.bitwise_and))
                link(dve.tensor_copy(smodf[:], smodi[:]))
                link(dve.tensor_copy(pmod[:], pmodi[:]))
                link(dve.tensor_scalar(smod[:], qio[:], smodf[:], None, ALU.is_equal))
                link(dve.tensor_copy(idf[:], id1[:]))
                dve.tensor_scalar(sid[:], idf[:], pidx[0:SUBJ, :], None, ALU.is_equal).then_inc(sid_ready, 1)
                link(dve.tensor_add(crow[:], biasrow[:, 0, :], biasrow[:, 1, :]))
                dve.tensor_copy(crow4[:], crow[:].unsqueeze(1).to_broadcast([1, GT, D])).then_inc(crow_ready, 1)

            dve.wait_ge(ld_uv, 32)
            for i in range(R):
                dve.wait_ge(gs_norm, i + 1)
                link(dve.tensor_scalar_add(gsd[:], gsn[:], EPS_GS))
                link(dve.reciprocal(gsr[:], gsd[:]))
                q = dve.tensor_tensor(Q[:, :, i], Q[:, :, i], gsr[:], ALU.mult)
                if i == R - 1:
                    q.then_inc(gs_step, 1)
                    break
                link(q)
                link(dve.tensor_tensor(gss[:], Q[:, :, i], gsr[:], ALU.mult))
                for k in range(2):
                    last = dve.scalar_tensor_tensor(Q[:, k, i + 1:R], ps[0][:, k * R + 1:(k + 1) * R - i], gss[:, k:k + 1],
                                                    Q[:, k, i + 1:R], ALU.mult, ALU.subtract, reverse1=True)
                last.then_inc(gs_step, 1)
                if i == TILES - 2:
                    masks()

            dve.wait_ge(fold_ps, 1)
            dve.tensor_copy(fold[:, 0, 0:R], ps[0][0:R, 0:R])
            dve.tensor_copy(fold[:, 1:3, :], ps[0][0:R, P:3 * P].rearrange("p (k d) -> p k d", d=D)).then_inc(fold_sb, 1)
            dve.wait_ge(z_exp, 1)
            link(dve.tensor_scalar_add(zden[:], zexp[:], 1.0))
            link(dve.reciprocal(zsig[:], zden[:]))
            link(dve.tensor_tensor(stren[:], zsig[:, 0:1], zsig[:, 1:2], ALU.mult))
            dve.tensor_scalar(strtile[:], tmask[:], stren[:], None, ALU.mult).then_inc(str_in, 1)
            dve.wait_ge(fold_ps, 2)
            dve.tensor_copy(fold[:, 3, :], ps[4][0:R, 0:D]).then_inc(fold_sb, 1)
            dve.wait_ge(fold_ps, 3)
            dve.tensor_copy(M[:], ps[5][:, 0:D]).then_inc(fold_sb, 1)
            dve.wait_ge(str_ps, 1)
            link(dve.tensor_copy(strT[:], ps[3][:, 0:TILES]))
            dve.wait_ge(style_exp, 1)
            link(dve.tensor_scalar_max(gpos[:], graw[:], 0.0))
            link(dve.scalar_tensor_tensor(gammaT[:], gpos[:], EPS_SP, gln[:], ALU.add, ALU.add))

            def x1_of(g):
                dve.wait_ge(resp_ps, g + 1)
                for j in range(GT):
                    t = g * GT + j
                    last = dve.scalar_tensor_tensor(x1r[:, t, 0:D], ps[1 + g % 2][:, j * D:(j + 1) * D], strT[:, t:t + 1],
                                                    X[:, t, :], ALU.mult, ALU.add)
                last.then_inc(x1_ready, 1)
                dve.wait_ge(x1_ready, g + 1)
                for t in range(g * GT, (g + 1) * GT):
                    last = dve.bn_stats(bst[:, t, :], x1r[:, t, 0:D])
                link(last)
                for t in range(g * GT, (g + 1) * GT):
                    last = dve.bn_aggr(mv[:, t, :], bst[:, t, :])
                link(last)
                dve.tensor_scalar_add(g128(ve, g), g128(mv, g)[:, :, 1], EPS_LN).then_inc(var_ready, 1)

            def shift_of(g):
                dve.wait_ge(rs_ready, g + 1)
                dve.scalar_tensor_tensor(g128(nmr, g), g128(mv, g)[:, :, 0], -1.0, g128(rs, g), ALU.mult,
                                         ALU.mult).then_inc(nmr_ready, 1)

            for g in range(GROUPS):
                x1_of(g)
                if g:
                    shift_of(g - 1)
            shift_of(GROUPS - 1)

            def over_tokens(g):
                return hT[:, g * GW:(g + 1) * GW].rearrange("p (s t) -> p s t", t=T), slice(g * SPG, (g + 1) * SPG)

            def spread(t, ss):
                return t[:, ss].unsqueeze(2).to_broadcast([P, SPG, T])

            for g in range(GROUPS):
                h, ss = over_tokens(g)
                dve.wait_ge(hT_raw, g + 1)
                link(dve.tensor_reduce(tsum[:, ss], h, AX.X, ALU.add))
                dve.scalar_tensor_tensor(h, spread(tsum, ss), -1.0 / T, h, ALU.mult, ALU.add).then_inc(hT_centred, 1)
            for g in range(GROUPS):
                h, ss = over_tokens(g)
                dve.wait_ge(sq_ready, g + 1)
                link(dve.tensor_reduce(tvar[:, ss], sq[:, g * GW:(g + 1) * GW].rearrange("p (s t) -> p s t", t=T),
                                       AX.X, ALU.add))
                dve.tensor_scalar(tve[:, ss], tvar[:, ss], 1.0 / T, EPS_T, ALU.mult, ALU.add).then_inc(tvar_ready, 1)
            for g in range(GROUPS):
                h, ss = over_tokens(g)
                dve.wait_ge(trs_ready, g + 1)
                link(dve.tensor_tensor(tsc[:, ss], trs[:, ss], gammaT[:, ss], ALU.mult))
                dve.tensor_tensor(h, h, spread(tsc, ss), ALU.mult).then_inc(h_scaled, 1)

            def wide(t):
                return t[:].unsqueeze(2).to_broadcast([P, TILES, E])

            dve.wait_ge(logit_ps, GROUPS)
            logits = ps[6][:, 0:P].rearrange("p (i e) -> p i e", e=E)
            link(dve.tensor_reduce(rmx[:], logits, AX.X, ALU.max))
            dve.tensor_tensor(rsh[:], logits, wide(rmx), ALU.subtract).then_inc(logit_shift, 1)
            dve.wait_ge(logit_exp, 1)
            link(dve.tensor_reduce(rsum[:], rex[:], AX.X, ALU.add))
            link(dve.reciprocal(rrec[:], rsum[:]))
            link(dve.tensor_tensor(rp[:], rex[:], wide(rrec), ALU.mult))
            for probs, m, mm, o in ((rp, m1, mm1, o1), (rp2, m2, mm2, o2)):
                link(dve.tensor_reduce(m[:], probs[:], AX.X, ALU.max))
                link(dve.tensor_tensor(req[:], probs[:], wide(m), ALU.is_equal))
                link(dve.tensor_tensor(rwt[:], req[:], down8[:], ALU.mult))
                link(dve.tensor_reduce(mm[:], rwt[:], AX.X, ALU.max))
                link(dve.tensor_tensor(o[:], rwt[:], wide(mm), ALU.is_equal))
                if o is o1:
                    link(dve.scalar_tensor_tensor(rp2[:], o1[:], -2.0, rp[:], ALU.mult, ALU.add))
            dve.tensor_tensor(both[:], o1[:], o2[:], ALU.add).then_inc(onehots, 1)
            link(dve.tensor_tensor(gsum[:], m1[:], m2[:], ALU.add))
            link(dve.reciprocal(grec[:], gsum[:]))
            dve.tensor_tensor(x1r[:, :, C_GATE], m1[:], grec[:], ALU.mult)
            dve.tensor_tensor(x1r[:, :, C_GATE + 1], m2[:], grec[:], ALU.mult)

            dve.wait_ge(rank_ps, 1)
            link(dve.tensor_copy(tot[:], ps[3][:, P:2 * P].rearrange("p (i e) -> p e i", e=E)))
            flat = lambda t: t[:].rearrange("p e i -> p (e i)")
            link(dve.tensor_tensor_scan(flat(incl), flat(segm), flat(tot), 0.0, ALU.mult, ALU.add))

            def blocks_of(counts, steps, cmp, n, upto, before):
                link(dve.tensor_tensor(cmp[:], counts.unsqueeze(2).to_broadcast([P, E, TILES]),
                                       steps[:].unsqueeze(1).to_broadcast([P, E, TILES]), ALU.is_gt))
                link(dve.tensor_reduce(n[:], cmp[:], AX.X, ALU.add))
                link(dve.tensor_tensor_scan(upto[:], ones8[:], n[:], 0.0, ALU.mult, ALU.add))
                link(dve.tensor_tensor(before[:], upto[:], n[:], ALU.subtract))

            def expert_of_block(cmp, upto, asfloat, asint, n):
                link(dve.tensor_tensor(cmp[:], iob[:, 0:n].unsqueeze(2).to_broadcast([P, n, E]),
                                       upto[:].unsqueeze(1).to_broadcast([P, n, E]), ALU.is_ge))
                link(dve.tensor_reduce(asfloat[:], cmp[:], AX.X, ALU.add))
                return dve.tensor_scalar_min(asint[:], asfloat[:], float(E - 1))

            blocks_of(incl[:, :, TILES - 1], bstep, cmp8, nb, cb, cbe)
            expert_of_block(cmpb, cb, bexf, bexi, NB1).then_inc(places, 1)
            link(dve.tensor_tensor(texc[:], incl[:], tot[:], ALU.subtract))
            link(dve.scalar_tensor_tensor(tbase[:], cbe[:].unsqueeze(2).to_broadcast([P, E, TILES]), float(P), texc[:],
                                          ALU.mult, ALU.add))
            link(dve.tensor_tensor(slots[:], ps[3][:, 0:P].rearrange("p (i e) -> p i e", e=E),
                                   tbase[:].rearrange("p e i -> p i e"), ALU.add))
            for k, o in enumerate((o1, o2)):
                link(dve.tensor_tensor(pick[:], o[:], slots[:], ALU.mult))
                link(dve.tensor_reduce(slotf[:, :, k], pick[:], AX.X, ALU.add))
            link(dve.tensor_copy(sloti[:], slotf[:]))
            dve.tensor_copy(x1r[:, :, C_SLOT:C_SLOT + 2].bitcast(I32), sloti[:])
            dve.tensor_scalar(slpi[:], sloti[:], P - 1, None, ALU.bitwise_and)
            link(dve.tensor_scalar(slbi[:], sloti[:], 7, None, ALU.logical_shift_right))
            dve.tensor_copy(slp[:], slpi[:])
            link(dve.tensor_copy(slb[:], slbi[:]))
            link(dve.tensor_tensor(eqb, iob[:].unsqueeze(1).to_broadcast([P, 2 * TILES, NB1]),
                                   slb[:].rearrange("p i k -> p (i k)").unsqueeze(2).to_broadcast([P, 2 * TILES, NB1]),
                                   ALU.is_equal))
            dve.tensor_tensor(tokb[:, :, 0, :], eqb,
                              tileio[:].rearrange("p i k -> p (i k)").unsqueeze(2).to_broadcast([P, 2 * TILES, NB1]), ALU.mult)
            dve.tensor_scalar(tokb[:, :, 1, :], eqb, pidx[:], None, ALU.mult)
            for n in range(2 * TILES):
                last = dve.tensor_scalar(ohp[:, n, :], io128[:], slp[:, n // 2, n % 2:n % 2 + 1], None, ALU.is_equal)
            last.then_inc(map_in, 1)
            dve.wait_ge(ld_w1, 16)
            dve.wait_ge(map_ps, 1)
            link(dve.tensor_copy(hilo[:], ps[7][:, 0:2 * NB1].rearrange("p (k b) -> p k b", k=2)))
            dve.scalar_tensor_tensor(map1[:], hilo[:, 0, :], float(P), hilo[:, 1, :], ALU.mult, ALU.add).then_inc(map_ready, 1)

            link(dve.tensor_copy(id2f[:], id2[:]))
            link(dve.tensor_scalar(a2f[:], iob[0:NS, 0:E], id2f[:], None, ALU.is_equal))
            dve.tensor_copy(a2[:], a2f[:]).then_inc(a2_ready, 1)
            dve.wait_ge(rank2_ps, 1)
            link(dve.tensor_copy(cnt2[:], ps[6][:, E:2 * E]))
            blocks_of(cnt2[:], sstep, cmp2, nb2, cb2, cbe2)
            link(expert_of_block(cmpb2, cb2, bex2f, bex2i, NB2))
            link(dve.scalar_tensor_tensor(slot2e[:], cbe2[0:NS, :], float(SPT), ps[6][0:NS, 0:E], ALU.mult, ALU.add))
            link(dve.tensor_tensor(a2f[:], a2f[:], slot2e[:], ALU.mult))
            link(dve.tensor_reduce(slot2[:], a2f[:], AX.X, ALU.add))
            dve.tensor_scalar(oh88[:], io88[:], slot2[:], None, ALU.is_equal).then_inc(oh88_ready, 1)
            dve.wait_ge(map2_ps, 1)
            dve.tensor_scalar(map2[:, 0, :], ps[6][:, NB2:2 * NB2], pmod[:], None, ALU.add)
            dve.tensor_scalar(map2[:, 1, :], ps[6][:, 2 * NB2:3 * NB2], pmod[:], float(SKIP), ALU.add,
                              ALU.add).then_inc(map2_ready, 1)
            two = slice(0, 2)
            link(dve.tensor_scalar(angk[:, two], smp[:, 1:3], 1.0 / (2 * PI), ROUND, ALU.mult, ALU.add))
            link(dve.tensor_scalar_add(angk[:, two], angk[:, two], -ROUND))
            link(dve.scalar_tensor_tensor(ang[:, two], angk[:, two], -PI2_HI, smp[:, 1:3], ALU.mult, ALU.add))
            link(dve.scalar_tensor_tensor(angr[:, two], angk[:, two], -PI2_LO, ang[:, two], ALU.mult, ALU.add))
            link(dve.tensor_scalar_add(angr[:, 2:4], angr[:, two], PI / 2))
            link(dve.tensor_scalar(angk[:], angr[:], PI, -2 * PI, ALU.is_gt, ALU.mult))
            link(dve.tensor_tensor(ang[:], angr[:], angk[:], ALU.add))
            dve.tensor_scalar(angw[:], ang[:], 3.1415925, -3.1415925, ALU.min, ALU.max).then_inc(ang_ready, 1)
            dve.wait_ge(trig_ready, 1)
            for k in range(4):
                dve.tensor_copy(trig8[:, k:k + 1], trig[:, 2 + k // 2:3 + k // 2])
                last = dve.tensor_scalar_mul(trig8[:, 4 + k:5 + k], trig[:, k // 2:k // 2 + 1], -1.0 if k % 2 else 1.0)
            link(last)
            dve.tensor_tensor(trigt[:], trig8[:].unsqueeze(2).to_broadcast([NS, 8, TILES]),
                              tmask[:].unsqueeze(1).to_broadcast([NS, 8, TILES]), ALU.mult).then_inc(trigt_ready, 1)
            dve.wait_ge(trig_ps, 1)
            dve.tensor_copy(x1r[:, :, C_COS:C_COS + 8],
                            ps[6][:, P:2 * P].rearrange("p (k i) -> p i k", i=TILES)).then_inc(x_row_ready, 1)
            dve.wait_ge(bias_ps, 1)
            for k, t in enumerate((b1c, bic)):
                last = dve.tensor_copy(t[:].rearrange("p e c -> p (e c)"), ps[7][:, k * E * FC:(k + 1) * E * FC])
            last.then_inc(bias_ready, 1)

            def expert(table, b):
                return dve.value_load(table[0:1, bass.ds(b, 1)], min_val=0, max_val=E - 1)

            def weights(i, u):
                b = 2 * i + u
                e = expert(bexi, b)
                if not isinstance(i, int) or i > 0:
                    dve.wait_ge(up_ps, b - 1)
                dve.tensor_copy(ws[:, u, :], w1[:, bass.ds(e, 1), :]).then_inc(ws_ready, 1)

            def columns(i, u):
                b = 2 * i + u
                dve.wait_ge(row_T_ps, b + 1)
                dve.tensor_copy(hgT[:, u, :], ps[u][:, 0:P]).then_inc(row_T_sb, 1)

            def rows_out(i, u):
                b = 2 * i + u
                e = expert(bexi, b)
                dve.wait_ge(down_ps, b + 1)
                if not isinstance(i, int) or i > 0:
                    dve.wait_ge(es_stored[u], 16 * i)
                dve.tensor_tensor(es[:, u, :], ps[4 + u][:, 0:D], b2r[:, bass.ds(e, 1), :].rearrange("p o d -> p (o d)"),
                                  ALU.add).then_inc(es_ready, 1)

            dve.wait_ge(places, 1)
            dve.wait_ge(ld_rows, 16 * N_ROWS)
            for u in range(2):
                weights(0, u)
                columns(0, u)
            for u in range(2):
                weights(1, u)
                columns(1, u)
                rows_out(0, u)
            with dve.Fori(1, NB1 // 2 - 1) as i:
                for u in range(2):
                    weights(i + 1, u)
                    columns(i + 1, u)
                    rows_out(i, u)
            i = NB1 // 2 - 1
            weights(i + 1, 0)
            columns(i + 1, 0)
            rows_out(i, 0)
            rows_out(i, 1)
            rows_out(i + 1, 0)

            def one(t, j, a, b):
                return t[:, bass.ds(j, 1), a:b].rearrange("p o c -> p (o c)")

            def row_of(t, e):
                return t[:, bass.ds(e, 1), :].rearrange("p o d -> p (o d)")

            def combine(i, u):
                j = 2 * i + u
                e = expert(bex2i, j)
                dve.wait_ge(eg_ready[u], 32 * (i + 1))
                if not isinstance(i, int) or i > 0:
                    dve.wait_ge(xT2_ps, j - 1)
                link2(dve.scalar_tensor_tensor(x2a[:, u, :], eg[:, u, 0, :],
                                               one(xg, j, C_GATE, C_GATE + 1), one(xg, j, 0, D), ALU.mult, ALU.add), j, 0)
                dve.scalar_tensor_tensor(x2[:, u, :], eg[:, u, 1, :],
                                         one(xg, j, C_GATE + 1, C_GATE + 2), x2a[:, u, :], ALU.mult, ALU.add).then_inc(x2_ready, 1)
                if not isinstance(i, int) or i > 0:
                    dve.wait_ge(up2_ps, j - 1)
                dve.tensor_copy(ws[:, u, :], wi[:, bass.ds(e, 1), :]).then_inc(wi_ready, 1)
                dve.wait_ge(x2_ready, j + 1)
                link2(dve.tensor_tensor(x2b[:, u, :], x2[:, u, :], row_of(bor, e), ALU.add), j, 1)
                dve.wait_ge(xT2_ps, j + 1)
                dve.tensor_copy(hgT[:, u, :], ps[u][:, 0:P]).then_inc(xT2_sb, 1)

            L2 = [sem(f"dve2_{n}") for n in range(12)]

            def link2(ins, j, n):
                ins.then_inc(L2[n], 1)
                dve.wait_ge(L2[n], j + 1)

            def norm_rotate(i, u):
                j = 2 * i + u
                e = expert(bex2i, j)
                dve.wait_ge(down2_ps, j + 1)
                link2(dve.tensor_tensor(rr[:, u, :], ps[4 + u][:, 0:D], x2b[:, u, :], ALU.add), j, 2)
                link2(dve.tensor_reduce(mv2[:, 0:1], rr[:, u, :], AX.X, ALU.add), j, 3)
                link2(dve.tensor_scalar_mul(mv2[:, 1:2], mv2[:, 0:1], -1.0 / D), j, 4)
                link2(dve.tensor_scalar(x2a[:, u, :], rr[:, u, :], mv2[:, 1:2], None, ALU.add), j, 9)
                link2(dve.tensor_tensor(x2b[:, u, :], x2a[:, u, :], x2a[:, u, :], ALU.mult), j, 10)
                link2(dve.tensor_reduce(st2[:, 0:1], x2b[:, u, :], AX.X, ALU.add), j, 11)
                dve.tensor_scalar(ve2[:], st2[:, 0:1], 1.0 / D, EPS_L2, ALU.mult, ALU.add).then_inc(ve2_ready, 1)
                dve.wait_ge(rs2_ready, j + 1)
                link2(dve.tensor_scalar(yn[:, u, :], x2a[:, u, :], rs2[:, u, :], None, ALU.mult), j, 5)
                link2(dve.tensor_tensor(yg[:, u, :], yn[:, u, :], row_of(g2r, e), ALU.mult), j, 6)
                link2(dve.tensor_tensor(yb[:, u, :], yg[:, u, :], row_of(be2r, e), ALU.add), j, 7)
                y4 = yb[:, u, :].rearrange("p (a c) -> p a c", c=4)
                y22 = yb[:, u, :].rearrange("p (a c) -> p a c", c=2)
                cos = xg[:, bass.ds(j, 1), C_COS:C_COS + 4].to_broadcast([P, D // 4, 4])
                sin = xg[:, bass.ds(j, 1), C_SIN:C_SIN + 4].to_broadcast([P, D // 4, 4])
                dve.tensor_tensor(yc[:, u, :].rearrange("p (a c) -> p a c", c=4), y4, cos, ALU.mult)
                s4 = ysn[:, u, :].rearrange("p (a c) -> p a c", c=4)
                for h in range(2):
                    last = dve.tensor_tensor(s4[:, :, h::2], y4[:, :, 1 - h::2], sin[:, :, h::2], ALU.mult)
                link2(last, j, 8)
                if not isinstance(i, int) or i > 0:
                    dve.wait_ge(yo_stored[u], 16 * i)
                dve.tensor_tensor(yo[:, u, :], yc[:, u, :], ysn[:, u, :], ALU.add).then_inc(yo_ready, 1)

            dve.wait_ge(up_ps, NB1)
            combine(0, 0)
            combine(0, 1)
            norm_rotate(0, 0)
            with dve.Fori(1, NB2 // 2) as i:
                combine(i, 0)
                norm_rotate(i - 1, 1)
                combine(i, 1)
                norm_rotate(i, 0)
            norm_rotate(NB2 // 2 - 1, 1)


_INS = ["x", "condB_safetyscore", "itok_B_6_14", "itok_B_0_7", "condB_theta", "condB_phi"] + [
    f"L0_cond_{n}" for n in ("U", "V", "safety_bias", "gate_w1", "gate_b1", "gate_w2", "gate_b2", "resp_w", "resp_b")] + [
    f"L1_cond_{n}" for n in ("ln_g", "ln_b", "subj_emb", "hyp_w1", "hyp_b1", "hyp_w2", "hyp_b2", "sty_w1", "sty_b1",
                             "sty_w2", "sty_b2", "router_w", "exp_w1", "exp_b1", "exp_w2", "exp_b2")] + [
    f"L2_cond_{n}" for n in ("Wi", "bi", "Wo", "bo", "gamma", "beta")]
_OUTS = [((NS, T, D), "float32")]


def kernel(**inputs):
    import numpy as _np
    import concourse.bacc as _bacc
    from concourse import mybir as _mybir
    from concourse.bass_utils import run_bass_kernel_spmd as _run

    nc = _bacc.Bacc("TRN2", target_bir_lowering=False, num_devices=1)
    arrays, args = {}, []
    for name in _INS:
        a = _np.ascontiguousarray(inputs[name])
        arrays[f"in_{name}_dram"] = a
        args.append(nc.dram_tensor(f"in_{name}_dram", a.shape, _mybir.dt.from_np(a.dtype), kind="ExternalInput").ap())
    for i, (shape, dtype) in enumerate(_OUTS):
        dt = _mybir.dt.from_np(_np.dtype(dtype))
        args.append(nc.dram_tensor(f"out_{i}_dram", shape, dt, kind="ExternalOutput").ap())
    cond_seq_kernel(nc, *args)
    r = _run(nc, [arrays], core_ids=[0])
    got = tuple(r.results[0][f"out_{i}_dram"] for i in range(len(_OUTS)))
    return got[0]
```

```python
import concourse.bass as bass
from concourse import mybir
from contextlib import ExitStack

F32, BF16, I32 = mybir.dt.float32, mybir.dt.bfloat16, mybir.dt.int32
ALU, ACT, AX = mybir.AluOpType, mybir.ActivationFunctionType, mybir.AxisListType

P = 128
D = 128
NS, T = 64, 32
NT = NS * T
TILES = NT // P
SPT = P // T
GT = 4
GROUPS = TILES // GT
GW = GT * P
SPG = GT * SPT
R = 32
E = 8
FF = 512
FC = FF // P
SUBJ, SE, SH = 32, 64, 128
NB1 = 2 * TILES + E - 1
NB2 = (NS + E * (SPT - 1)) // SPT
LAG = 3
RING = 4
XW = D + 12
C_SLOT, C_GATE, C_COS, C_SIN = D, D + 2, D + 4, D + 8
EPS_GS, EPS_LN, EPS_T, EPS_SP, EPS_L2 = 1e-8, 1e-5, 1e-8, 1e-8, 1e-12
PI = 3.141592653589793
PI2_HI, PI2_LO = 6.28125, 2 * PI - 6.28125
ROUND = 12582912.0


def cond_seq_kernel(nc, x, score, ids1, ids2, theta, phi, U, V, safety_bias, gate_w1, gate_b1, gate_w2,
                    gate_b2, resp_w, resp_b, ln_g, ln_b, subj_emb, hyp_w1, hyp_b1, hyp_w2, hyp_b2,
                    sty_w1, sty_b1, sty_w2, sty_b2, router_w, exp_w1, exp_b1, exp_w2, exp_b2,
                    Wi, bi, Wo, bo, gamma2, beta2, out):
    ctx = ExitStack()
    with ctx:
        def sb(name, shape, dt=F32):
            return ctx.enter_context(nc.sbuf_tensor(name, shape, dt))

        def sem(name):
            return ctx.enter_context(nc.semaphore(name))

        w2 = sb("w2", [P, E, FC, D])
        wo = sb("wo", [P, E, FC, D])
        brow = sb("brow", [E, 2, FF])
        bexp1 = sb("bexp1", [E, NB1])
        bexp2 = sb("bexp2", [E, NB2])
        bh1 = sb("bh1", [P, FC, NB1])
        bh2 = sb("bh2", [P, FC, NB2])
        b2blk = sb("b2blk", [P, RING, D])
        bor = sb("bor", [1, E, D])
        g2r = sb("g2r", [P, E, D])
        be2r = sb("be2r", [P, E, D])
        Q = sb("Q", [P, 2, R])
        gw1 = sb("gw1", [R, D])
        rw = sb("rw", [P, R])
        col = sb("col", [P, 12])
        c_gb1, c_gw2, c_lng, c_lnb, c_hb1, c_hb2, c_sb1, c_sg, c_sbt = range(9)
        biasrow = sb("biasrow", [1, 2, D])
        gb2 = sb("gb2", [NS, 1])
        emb = sb("emb", [SUBJ, SE])
        hw1 = sb("hw1", [SE, SH])
        hw2 = sb("hw2", [SH, SH])
        sw1 = sb("sw1", [SH, SH // 2])
        sw2 = sb("sw2", [SH // 2, 2 * D])
        rout = sb("rout", [D, E])
        smp = sb("smp", [NS, 3])
        id1 = sb("id1", [SUBJ, NS], I32)
        id2 = sb("id2", [NS, 1], I32)
        ident = sb("ident", [P, P])
        tri = sb("tri", [P, P], BF16)
        ones = sb("ones", [P, P], BF16)
        onesrow = sb("onesrow", [1, P])
        mean4 = sb("mean4", [P, SPT])
        tmask = sb("tmask", [NS, TILES])
        smod = sb("smod", [NS, SPT, T])
        smodi = sb("smodi", [NS, 1], I32)
        smodf = sb("smodf", [NS, 1])
        qio = sb("qiota", [NS, SPT, T])
        io128 = sb("io128", [P, P], BF16)
        tileio = sb("tileio", [P, TILES, 2])
        down8 = sb("down8", [P, TILES, E])
        segm = sb("segm", [P, E, TILES])
        ones8 = sb("ones8", [P, E])
        pidx = sb("pidx", [P, 1])
        pmod = sb("pmod", [P, 1])
        pmodi = sb("pmodi", [P, 1], I32)
        pidxi = sb("pidxi", [P, 1], I32)
        mhalf = sb("mhalf", [P, 16])
        iob = sb("iob", [P, NB1])
        bstep = sb("bstep", [P, TILES])
        sstep = sb("sstep", [P, TILES])
        big = sb("big", [P, 4 * NT])
        tiles_of = lambda a: a.rearrange("p (i d) -> p i d", d=D)
        X = tiles_of(big[:, 0:NT])
        xT = big[:, NT:2 * NT]
        x1r = sb("x1r", [P, TILES, XW])
        h0 = tiles_of(big[:, 2 * NT:3 * NT])
        hT = big[:, 3 * NT:4 * NT]
        sq = xT
        hrow = X

        hdram = nc.dram_tensor("h_rows", [NT, D], F32).ap()
        xdram = nc.dram_tensor("x1_rows", [NT, XW], F32).ap()
        edram = nc.dram_tensor("expert_rows", [NB1 * P, D], F32).ap()

        sid = sb("sid", [SUBJ, NS])
        idf = sb("idf", [SUBJ, NS])
        gw1T = sb("gw1T", [D, R])
        rwT = sb("rwT", [R, D])
        pooledT = sb("pooledT", [D, NS])
        h1T = sb("h1T", [R, NS])
        seT = sb("seT", [SE, NS])
        hypT = sb("hypT", [SH, NS])
        hyp2T = sb("hyp2T", [SH, NS])
        styT = sb("styT", [SH // 2, NS])
        graw = sb("graw", [D, NS])
        gabs = sb("gabs", [D, NS])
        gexp = sb("gexp", [D, NS])
        gln = sb("gln", [D, NS])
        gpos = sb("gpos", [D, NS])
        gammaT = sb("gammaT", [D, NS])
        betaT = sb("betaT", [D, NS])
        gsn, gsd, gsr, gss = (sb(n, [P, 2]) for n in ("gsn", "gsd", "gsr", "gss"))
        crow = sb("crow", [1, D])
        crow4 = sb("crow4", [1, GT, D])
        fold = sb("fold", [R, 4, D])
        M = sb("M", [D, D])
        zs = sb("zs", [NS, 2])
        zexp = sb("zexp", [NS, 2])
        zden = sb("zden", [NS, 2])
        zsig = sb("zsig", [NS, 2])
        stren = sb("stren", [NS, 1])
        strtile = sb("strtile", [NS, TILES])
        strT = sb("strT", [P, TILES])
        bst = sb("bst", [P, TILES, 6])
        mv = sb("mv", [P, TILES, 2])
        ve, rs, rstd, nmr = (sb(n, [P, TILES]) for n in ("ve", "rs", "rstd", "nmr"))
        tsum, tvar, tve, trs, trr, tsc = (sb(n, [P, NS]) for n in ("tsum", "tvar", "tve", "trs", "trr", "tsc"))
        rt = lambda n, dt=F32: sb(n, [P, TILES, E], dt)
        rsh, rex, rp, req, rwt, o1, o2, rp2, slots, pick = (rt(n) for n in (
            "rsh", "rex", "rp", "req", "rwt", "o1", "o2", "rp2", "slots", "pick"))
        both = rt("both", BF16)
        rmx, rsum, rrec, m1, m2, mm1, mm2, gsum, grec = (sb(n, [P, TILES]) for n in (
            "rmx", "rsum", "rrec", "m1", "m2", "mm1", "mm2", "gsum", "grec"))
        tot, incl, texc, tbase = (sb(n, [P, E, TILES]) for n in ("tot", "incl", "texc", "tbase"))
        cmp8 = sb("cmp8", [P, E, TILES])
        nb, cb, cbe = (sb(n, [P, E]) for n in ("nb", "cb", "cbe"))
        cmpb = sb("cmpb", [P, NB1, E])
        bexf = sb("bexf", [P, NB1])
        bexi = sb("bexi", [P, NB1], I32)
        slotf = sb("slotf", [P, TILES, 2])
        sloti = sb("sloti", [P, TILES, 2], I32)
        slpi = sb("slpi", [P, TILES, 2], I32)
        slbi = sb("slbi", [P, TILES, 2], I32)
        slp = sb("slp", [P, TILES, 2])
        slb = sb("slb", [P, TILES, 2])
        ohp = sb("ohp", [P, 2 * TILES, P], BF16)
        eqb = big[:, 2 * NT:2 * NT + 2 * TILES * NB1].rearrange("p (n b) -> p n b", b=NB1)
        tokb = sb("tokb", [P, 2 * TILES, 2, NB1], BF16)
        hilo = sb("hilo", [P, 2, NB1])
        mapf = sb("mapf", [P, NB1])
        map1 = sb("map1", [P, NB1], I32)
        id2f = sb("id2f", [NS, 1])
        a2 = sb("a2", [NS, E], BF16)
        a2f = sb("a2f", [NS, E])
        cnt2 = sb("cnt2", [P, E])
        cmp2 = sb("cmp2", [P, E, TILES])
        nb2, cb2, cbe2 = (sb(n, [P, E]) for n in ("nb2", "cb2", "cbe2"))
        slot2, slot2e = sb("slot2", [NS, 1]), sb("slot2e", [NS, E])
        io88 = sb("io88", [NS, SPT, NB2])
        oh88 = sb("oh88", [NS, SPT, NB2])
        tokv = sb("tokv", [NS, T])
        sback = sb("sback", [NS, 1])
        cmpb2 = sb("cmpb2", [P, NB2, E])
        bex2f = sb("bex2f", [P, NB2])
        bex2i = sb("bex2i", [P, NB2], I32)
        map2 = sb("map2", [P, NB2], I32)
        samp = sb("samp", [1, NB2 * SPT], I32)
        ang = sb("ang", [NS, 4])
        angk, angr, angw, trig = (sb(n, [NS, 4]) for n in ("angk", "angr", "angw", "trig"))
        trig8 = sb("trig8", [NS, 8])
        trigt = sb("trigt", [NS, 8, TILES])
        hg = sb("hg", [P, 2, D])
        hgT = sb("hgT", [P, 2, P])
        ws = sb("ws", [P, RING, FF])
        hid = sb("hid", [P, 2, FC, P])
        es = sb("es", [P, 2, D])
        xg = sb("xg", [P, NB2, XW])
        eg = big[:, 0:NB2 * 2 * D].rearrange("p (j k d) -> p j k d", k=2, d=D)
        x2a = sb("x2a", [P, D])
        x2, rr = (sb(n, [P, RING, D]) for n in ("x2", "rr"))
        st2, mv2 = sb("st2", [P, 6]), sb("mv2", [P, RING, 2])
        ve2, rs2 = sb("ve2", [P, RING]), sb("rs2", [P, RING])
        yn = sb("yn", [P, D])
        yg = sb("yg", [P, D])
        yb = sb("yb", [P, D])
        yc = sb("yc", [P, D])
        ysn = sb("ysn", [P, D])
        yo = sb("yo", [P, 2, D])

        ps = [ctx.enter_context(nc.psum_tensor(f"bank{i}", [P, 512], F32)) for i in range(8)]

        def vec(v, n=P):
            return v.rearrange("(p o) -> p o", o=1)

        SMALL = [(gw1[:], gate_w1), (rw[:], resp_w), (gb2[:], gate_b2.partition_broadcast(NS)),
                 (emb[:], subj_emb), (hw1[:], hyp_w1), (hw2[:], hyp_w2), (sw1[:], sty_w1), (sw2[:], sty_w2),
                 (rout[:], router_w), (biasrow[:, 0, :], resp_b.rearrange("(o d) -> o d", o=1)),
                 (biasrow[:, 1, :], safety_bias.rearrange("(o d) -> o d", o=1)),
                 (smp[:, 0:1], vec(score)), (smp[:, 1:2], vec(theta)), (smp[:, 2:3], vec(phi)),
                 (id1[:], ids1.partition_broadcast(SUBJ)), (id2[:], vec(ids2)),
                 (col[0:R, c_gb1:c_gb1 + 1], vec(gate_b1)), (col[0:R, c_gw2:c_gw2 + 1], gate_w2.rearrange("o r -> r o")),
                 (col[:, c_lng:c_lng + 1], vec(ln_g)), (col[:, c_lnb:c_lnb + 1], vec(ln_b)),
                 (col[:, c_hb1:c_hb1 + 1], vec(hyp_b1)), (col[:, c_hb2:c_hb2 + 1], vec(hyp_b2)),
                 (col[0:SH // 2, c_sb1:c_sb1 + 1], vec(sty_b1)),
                 (col[:, c_sg:c_sg + 1], vec(sty_b2[0:D])), (col[:, c_sbt:c_sbt + 1], vec(sty_b2[D:2 * D]))]
        ROWS = [(brow[:, 0, :], exp_b1), (brow[:, 1, :], bi), (bor[:], bo.rearrange("(o e) d -> o e d", o=1)),
                (g2r[:], gamma2.partition_broadcast(P)), (be2r[:], beta2.partition_broadcast(P))]
        IOTAS = [(pidx[:], [[0, 1]], 0, 1), (pidxi[:], [[0, 1]], 0, 1), (io128[:], [[1, P]], 0, 0),
                 (tileio[:], [[1, TILES], [0, 2]], 0, 0), (down8[:], [[0, TILES], [-1, E]], E, 0),
                 (iob[:], [[1, NB1]], 0, 0), (bstep[:], [[P, TILES]], 0, 0), (sstep[:], [[SPT, TILES]], 0, 0),
                 (qio[:], [[1, SPT], [0, T]], 0, 0), (io88[:], [[1, SPT], [SPT, NB2]], 0, 0),
                 (tokv[:], [[0, T]], 0, T), (sback[:], [[0, 1]], -NS, 1)]
        GS_MASKS, GS_A2, GS_ANGLES, GS_RANK2, GS_MAP2 = 12, 14, 15, 23, 28
        GS_BUSY = 6
        N_SMALL, N_ROWS, N_CONST, N_SIDE = len(SMALL), len(ROWS), 16 + len(IOTAS), TILES + 6

        (ld_uv, ld_x, ld_small, ld_w2, ld_wo, ld_rows, consts, act_own, dve_own, gs_dots, gs_norm,
         q_ready, xt_ps, xt_sb, pooled_ps, sid_ready, side_ps, side_sb, crow_ready, fold_ps, fold_sb,
         style_exp, z_exp, str_in, str_ps, resp_ps, x1_ready, var_ready, std_ready, nmr_ready, h0_ready,
         h0T_ps, hT_raw, hT_centred, sq_ready, tvar_ready, tstd_ready, h_ready, logit_ps, hrow_ps,
         hrow_sb, h_stored, logit_shift, logit_exp, onehots, rank_ps, places, eqb_ready, tok_lo, map_in,
         map_ps, map_ready, a2_ready, rank2_ps, oh88_ready, map2_ps, map2_ready, ang_ready, trig_ready,
         trigt_ready, trig_ps, x_row_ready, bexp_ready, bias_ps, bias_ready, x_stored, row_T_ps, row_T_sb,
         up_ps, hidA_sb, hidB_sb, down_ps, es_ready, x2_ready, xT2_ps, xT2_sb, up2_ps, hid2_sb, down2_ps,
         ve2_ready, rs2_ready, yo_ready, c_x2a, b_rr, b_stats, b_aggr, n_yn, n_yg, n_yb, n_rot) = map(sem, """
         ld_uv ld_x ld_small ld_w2 ld_wo ld_rows consts act_own dve_own gs_dots gs_norm q_ready
         xt_ps xt_sb pooled_ps sid_ready side_ps side_sb crow_ready fold_ps fold_sb style_exp z_exp
         str_in str_ps resp_ps x1_ready var_ready std_ready nmr_ready h0_ready h0T_ps hT_raw hT_centred
         sq_ready tvar_ready tstd_ready h_ready logit_ps hrow_ps hrow_sb h_stored logit_shift logit_exp
         onehots rank_ps places eqb_ready tok_lo map_in map_ps map_ready a2_ready rank2_ps oh88_ready
         map2_ps map2_ready ang_ready trig_ready trigt_ready trig_ps x_row_ready bexp_ready bias_ps bias_ready
         x_stored row_T_ps row_T_sb up_ps hidA_sb hidB_sb down_ps es_ready x2_ready xT2_ps
         xT2_sb up2_ps hid2_sb down2_ps ve2_ready rs2_ready yo_ready c_x2a b_rr b_stats b_aggr n_yn
         n_yg n_yb n_rot""".split())
        gs_step = [sem(f"gs_step_{m}") for m in "UV"]
        hg_ready = [sem(f"hg_ready{i}") for i in range(2)]
        es_stored = [sem(f"es_stored{i}") for i in range(2)]
        xg_ready = [sem(f"xg_ready{i}") for i in range(2)]
        eg_ready = [sem(f"eg_ready{i}") for i in range(2)]
        w1_ready = [sem(f"w1_ready{i}") for i in range(RING)]
        b2_ready = [sem(f"b2_ready{i}") for i in range(RING)]
        wi_ready = [sem(f"wi_ready{i}") for i in range(RING)]
        yo_stored = [sem(f"yo_stored{i}") for i in range(2)]

        block = ctx.enter_context(nc.Block())

        def early(j, n):
            return isinstance(j, int) and j < n

        def blocks(eng, n, head, tail, step):
            assert head % RING == 0 and (n - tail - head) % RING == 0
            for j in range(head):
                step(j, j % RING)
            with eng.Fori(head // RING, (n - tail) // RING) as i:
                for r in range(RING):
                    step(RING * i + r, r)
            for j in range(n - tail, n):
                step(j, j % RING)

        def g128(t, g):
            return t[:, g * GT:(g + 1) * GT]

        @block.sync
        def _(sp):
            sp.dma_start(Q[:, 0, :], U).then_inc(ld_uv, 16)
            sp.dma_start(Q[:, 1, :], V).then_inc(ld_uv, 16)
            sp.dma_start(X, x.rearrange("(i s) t d -> (s t) i d", s=SPT)).then_inc(ld_x, 16)
            for dst, src in SMALL:
                sp.dma_start(dst, src).then_inc(ld_small, 16)
            sp.dma_start(w2[:], exp_w2.rearrange("e (c p) d -> p e c d", p=P)).then_inc(ld_w2, 16)
            for dst, src in ROWS:
                sp.dma_start(dst, src).then_inc(ld_rows, 16)
            sp.dma_start(wo[:], Wo.rearrange("e (c p) d -> p e c d", p=P)).then_inc(ld_wo, 16)
            for g in range(GROUPS):
                sp.wait_ge(hrow_sb, g + 1)
                sp.dma_start(hdram[g * GW:(g + 1) * GW, :].rearrange("(i p) d -> p i d", p=P),
                             g128(hrow, g)).then_inc(h_stored, 16)
            def weights1(b, r):
                e = sp.value_load(bexi[0:1, bass.ds(b, 1)], min_val=0, max_val=E - 1)
                if not early(b, RING):
                    sp.wait_ge(up_ps, b - RING + 1)
                sp.dma_start(ws[:, r, :], exp_w1[bass.ds(e, 1), :, :].rearrange("e d f -> (e d) f")).then_inc(w1_ready[r], 16)
                if not early(b, RING):
                    sp.wait_ge(es_ready, b - RING + 1)
                sp.dma_start(b2blk[:, r, :],
                             exp_b2[bass.ds(e, 1), :].rearrange("e d -> (e d)").partition_broadcast(P)).then_inc(b2_ready[r], 16)

            def store(b, r):
                sp.wait_ge(es_ready, b + 1)
                sp.dma_start(edram[bass.ds(b * P, P), :], es[:, r % 2, :]).then_inc(es_stored[r % 2], 16)

            def step1(b, r):
                store(b, r)
                if not (isinstance(b, int) and b + RING >= NB1):
                    weights1(b + RING, r)
            sp.wait_ge(places, 1)
            for b in range(RING):
                weights1(b, b)
            sp.wait_ge(x_row_ready, 1)
            sp.dma_start(xdram.rearrange("(i p) d -> p i d", p=P), x1r[:]).then_inc(x_stored, 16)
            blocks(sp, NB1, 0, RING + NB1 % RING, step1)

            def weights2(j, r):
                e = sp.value_load(bex2i[0:1, bass.ds(j, 1)], min_val=0, max_val=E - 1)
                if not early(j, RING):
                    sp.wait_ge(up2_ps, j - RING + 1)
                sp.dma_start(ws[:, r, :], Wi[bass.ds(e, 1), :, :].rearrange("e d f -> (e d) f")).then_inc(wi_ready[r], 16)

            def samples_out(j, r):
                _, places_ = nc.values_load_multi_w_load_instructions(
                    samp[0:1, bass.ds(SPT * j, SPT)], engines=[mybir.EngineType.SP])
                sp.wait_ge(yo_ready, j + 1)
                for q in range(SPT):
                    sp.dma_start(out[bass.ds(places_[q], 1), :, :].rearrange("s t d -> (s t) d"),
                                 yo[q * T:(q + 1) * T, r % 2, :], bounds_check="skip_entire_dma").then_inc(yo_stored[r % 2], 16)
            for j in range(RING):
                sp.wait_ge(up_ps, max(range(j, NB1, RING)) + 1)
                weights2(j, j)

            def step2(j, r):
                if not early(j, LAG):
                    samples_out(j - LAG, (r - LAG) % RING)
                if not (isinstance(j, int) and j + RING >= NB2):
                    weights2(j + RING, r)
            blocks(sp, NB2 + LAG, RING, RING + LAG + NB2 % RING, step2)
            for u in range(2):
                sp.wait_ge(yo_stored[u], 16 * SPT * len(range(u, NB2, 2)))

        @block.gpsimd
        def _(pool):
            count = [0]

            def const(ins):
                count[0] += 1
                ins.then_inc(consts, 1)
                pool.wait_ge(consts, count[0])

            const(pool.memset(ident[:], 0.0))
            const(pool.affine_select(out=ident[:], in_=ident[:], compare_op=ALU.not_equal, fill=1.0, base=0,
                                     pattern=[[-1, P]], channel_multiplier=1))
            const(pool.memset(mean4[:], 1.0 / T))
            const(pool.affine_select(out=mean4[:], in_=mean4[:], compare_op=ALU.is_ge, fill=0.0, base=0,
                                     pattern=[[-T, SPT]], channel_multiplier=1))
            const(pool.affine_select(out=mean4[:], in_=mean4[:], compare_op=ALU.is_ge, fill=0.0, base=T - 1,
                                     pattern=[[T, SPT]], channel_multiplier=-1))
            const(pool.memset(tri[:], 1.0))
            const(pool.affine_select(out=tri[:], in_=tri[:], compare_op=ALU.is_gt, fill=0.0, base=0,
                                     pattern=[[1, P]], channel_multiplier=-1))
            const(pool.memset(ones[:], 1.0))
            const(pool.memset(onesrow[:], 1.0))
            const(pool.memset(tmask[:], 1.0))
            const(pool.affine_select(out=tmask[:], in_=tmask[:], compare_op=ALU.is_ge, fill=0.0, base=0,
                                     pattern=[[-SPT, TILES]], channel_multiplier=1))
            const(pool.affine_select(out=tmask[:], in_=tmask[:], compare_op=ALU.is_ge, fill=0.0, base=SPT - 1,
                                     pattern=[[SPT, TILES]], channel_multiplier=-1))
            const(pool.memset(mhalf[:], -0.5))
            const(pool.memset(ones8[:], 1.0))
            const(pool.memset(segm[:], 1.0))
            const(pool.memset(segm[:, :, 0:1], 0.0))
            for dst, pattern, base, mult in IOTAS:
                const(pool.iota(dst, pattern=pattern, base=base, channel_multiplier=mult,
                                allow_small_or_imprecise_dtypes=True))
            assert count[0] == N_CONST

            pool.wait_ge(eqb_ready, 1)
            pool.tensor_scalar(tokb[:, :, 1, :], eqb, pidx[:], 0.0, ALU.mult, ALU.add).then_inc(tok_lo, 1)

            pool.wait_ge(h_stored, 16 * GROUPS)
            pool.wait_ge(map_ready, 1)

            def power(i):
                two = slice(2 * i % RING, 2 * i % RING + 2)
                pool.wait_ge(ve2_ready, 2 * i + 2)
                pool.tensor_tensor(rs2[:, two], ve2[:, two], mhalf[:, 0:2], ALU.pow).then_inc(rs2_ready, 2)

            def gather_x(j):
                if j == 0:
                    pool.wait_ge(x_stored, 16)
                    pool.wait_ge(map2_ready, 1)
                if j >= 2:
                    pool.wait_ge(xg_ready[j % 2], 16 * (j // 2))
                pool.indirect_dma_start(
                    out=xg[:, j, :], out_offset=None, in_=xdram,
                    in_offset=bass.IndirectOffsetOnAxis(ap=map2[:, j:j + 1], axis=0)).then_inc(xg_ready[j % 2], 16)

            for b in range(NB1):
                if b >= 2:
                    pool.wait_ge(row_T_ps, b - 1)
                pool.indirect_dma_start(
                    out=hg[:, b % 2, :], out_offset=None, in_=hdram,
                    in_offset=bass.IndirectOffsetOnAxis(ap=map1[:, b:b + 1], axis=0)).then_inc(hg_ready[b % 2], 16)
                if b >= 8 and b % 2 == 0 and (b - 8) // 2 < NB2:
                    gather_x((b - 8) // 2)
            for j in range((NB1 - 8 + 1) // 2, NB2):
                gather_x(j)
            pool.wait_ge(es_stored[0], 16 * ((NB1 + 1) // 2))
            pool.wait_ge(es_stored[1], 16 * (NB1 // 2))
            pool.wait_ge(xg_ready[0], 16 * ((NB2 + 1) // 2))
            pool.wait_ge(xg_ready[1], 16 * (NB2 // 2))

            def gather_e(j):
                if j >= 2:
                    pool.wait_ge(eg_ready[j % 2], 32 * (j // 2))
                for k in range(2):
                    pool.indirect_dma_start(
                        out=eg[:, j, k, :], out_offset=None, in_=edram,
                        in_offset=bass.IndirectOffsetOnAxis(
                            ap=xg[:, j, C_SLOT + k:C_SLOT + k + 1].bitcast(I32), axis=0)).then_inc(eg_ready[j % 2], 16)

            for j in range(NB2):
                gather_e(j)
                if j >= 6 and j % 2 == 0:
                    power(j // 2 - 3)
            for i in range(NB2 // 2 - 3, NB2 // 2):
                power(i)

        @block.scalar
        def _(act):
            def token_std(g):
                ss = slice(g * SPG, (g + 1) * SPG)
                act.wait_ge(tvar_ready, g + 1)
                act.activation(trs[:, ss], tve[:, ss], ACT.Sqrt).then_inc(tstd_ready, 1)

            def layer_norm(g):
                act.wait_ge(nmr_ready, g + 1)
                for t in range(g * GT, (g + 1) * GT):
                    last = act.activation(h0[:, t, :], x1r[:, t, 0:D], ACT.Identity, bias=nmr[:, t:t + 1],
                                          scale=rstd[:, t:t + 1])
                last.then_inc(h0_ready, 1)
                act.wait_ge(h0T_ps, g + 1)
                act.activation(hT[:, g * GW:(g + 1) * GW], ps[4 + g % 2][:], ACT.Identity,
                               bias=col[:, c_lnb:c_lnb + 1], scale=col[:, c_lng:c_lng + 1]).then_inc(hT_raw, 1)

            def side(n):
                if n < TILES:
                    act.wait_ge(xt_ps, n + 1)
                    act.activation(xT[:, n * P:(n + 1) * P], ps[1 + n % 2][:, 0:P], ACT.Copy).then_inc(xt_sb, 1)
                    return
                n -= TILES
                act.wait_ge(side_ps, n + 1)
                if n == 0:
                    act.wait_ge(pooled_ps, 1)
                    act.activation(gw1T[:], ps[6][:, 0:R], ACT.Copy)
                    act.activation(rwT[:], ps[6][0:R, P:2 * P], ACT.Copy)
                    last = act.activation(pooledT[:], ps[3][:, 0:NS], ACT.Copy)
                elif n == 1:
                    act.activation(h1T[:], ps[5][0:R, 0:NS], ACT.Relu, bias=col[0:R, c_gb1:c_gb1 + 1])
                    last = act.activation(seT[:], ps[5][0:SE, NS:2 * NS], ACT.Copy)
                elif n == 2:
                    act.activation(zs[:, 0:1], ps[6][0:NS, 0:1], ACT.Identity, bias=gb2[:])
                    act.activation(zs[:, 1:2], smp[:, 0:1], ACT.Copy)
                    last = act.activation(hypT[:], ps[6][:, NS:2 * NS], ACT.Relu, bias=col[:, c_hb1:c_hb1 + 1])
                elif n == 3:
                    last = act.activation(hyp2T[:], ps[5][:, 0:NS], ACT.Identity, bias=col[:, c_hb2:c_hb2 + 1])
                elif n == 4:
                    last = act.activation(styT[:], ps[6][0:SH // 2, 0:NS], ACT.Relu, bias=col[0:SH // 2, c_sb1:c_sb1 + 1])
                else:
                    act.activation(graw[:], ps[5][:, 0:NS], ACT.Identity, bias=col[:, c_sg:c_sg + 1])
                    act.activation(gabs[:], ps[5][:, 0:NS], ACT.Abs, bias=col[:, c_sg:c_sg + 1])
                    last = act.activation(betaT[:], ps[5][:, NS:2 * NS], ACT.Identity, bias=col[:, c_sbt:c_sbt + 1])
                last.then_inc(side_sb, 1)

            for i in range(R):
                for k in range(2):
                    act.wait_ge(gs_dots, 2 * i + k + 1)
                    act.activation(gsn[:, k:k + 1], ps[4 * k][:, 0:1], ACT.Sqrt).then_inc(gs_norm, 1)
                if 1 <= i <= N_SIDE:
                    if i == TILES + 1:
                        act.wait_ge(ld_small, 16 * N_SMALL)
                    side(i - 1)
            act.wait_ge(side_sb, N_SIDE - TILES)
            act.activation(zexp[:], zs[:], ACT.Exp, scale=-1.0).then_inc(z_exp, 1)
            act.activation(gexp[:], gabs[:], ACT.Exp, scale=-1.0).then_inc(act_own, 1)
            act.wait_ge(act_own, 1)
            act.activation(gln[:], gexp[:], ACT.Ln, bias=1.0).then_inc(style_exp, 1)
            act.wait_ge(ang_ready, 1)
            act.activation(trig[:], angw[:], ACT.Sin).then_inc(trig_ready, 1)
            for g in range(GROUPS):
                act.wait_ge(var_ready, g + 1)
                act.activation(g128(rs, g), g128(ve, g), ACT.Sqrt).then_inc(std_ready, 1)
                if g:
                    layer_norm(g - 1)
            layer_norm(GROUPS - 1)
            for g in range(GROUPS):
                act.wait_ge(hT_centred, g + 1)
                cols = slice(g * GW, (g + 1) * GW)
                act.activation(sq[:, cols], hT[:, cols], ACT.Square).then_inc(sq_ready, 1)
                if g:
                    token_std(g - 1)
            token_std(GROUPS - 1)
            for g in range(GROUPS):
                act.wait_ge(hrow_ps, g + 1)
                act.activation(g128(hrow, g), ps[4 + g % 2][:].rearrange("p (i d) -> p i d", d=D),
                               ACT.Copy).then_inc(hrow_sb, 1)
            act.wait_ge(logit_shift, 1)
            act.activation(rex[:], rsh[:], ACT.Exp).then_inc(logit_exp, 1)

            def hidden(b, r):
                u = r % 2
                act.wait_ge(up_ps, b + 1)
                if not early(b, 2):
                    act.wait_ge(down_ps, b - 1)
                for c in range(FC // 2):
                    last = act.activation(hid[:, u, c, :], ps[2 + u][:, c * P:(c + 1) * P], ACT.Relu,
                                          bias=bh1[:, c, bass.ds(b, 1)])
                last.then_inc(hidA_sb, 1)
            act.wait_ge(bias_ps, 1)
            act.activation(bh1[:].rearrange("p c b -> p (c b)"), ps[6][:, 0:FC * NB1], ACT.Copy)
            act.activation(bh2[:].rearrange("p c b -> p (c b)"), ps[6][:, FC * NB1:FC * (NB1 + NB2)], ACT.Copy).then_inc(bias_ready, 1)
            act.wait_ge(bias_ready, 1)
            blocks(act, NB1, RING, NB1 % RING, hidden)

            def columns2(j, r):
                act.wait_ge(xT2_ps, j + 1)
                act.activation(hgT[:, r % 2, :], ps[r % 2][:, 0:P], ACT.Copy).then_inc(xT2_sb, 1)

            def hidden2(j, r):
                u = r % 2
                act.wait_ge(up2_ps, j + 1)
                if not early(j, 2):
                    act.wait_ge(down2_ps, j - 1)
                for c in range(FC):
                    last = act.activation(hid[:, u, c, :], ps[2 + 2 * (c // 2) + u][:, c % 2 * P:(c % 2 + 1) * P], ACT.Gelu,
                                          bias=bh2[:, c, bass.ds(j, 1)])
                last.then_inc(hid2_sb, 1)

            def step2(j, r):
                hidden2(j, r)
                if not (isinstance(j, int) and j + 2 >= NB2):
                    columns2(j + 2, r + 2)
            act.wait_ge(down_ps, NB1)
            columns2(0, 0)
            columns2(1, 1)
            blocks(act, NB2, RING, NB2 % RING, step2)

        @block.tensor
        def _(pe):
            mm = pe.matmul

            def side(n):
                if n < TILES:
                    if n >= 2:
                        pe.wait_ge(xt_sb, n - 1)
                    pe.transpose(ps[1 + n % 2][:, 0:P], X[:, n, :], ident[:]).then_inc(xt_ps, 1)
                    m = mm(ps[3][:, n * SPT:(n + 1) * SPT], X[:, n, :], mean4[:], start=True, stop=True)
                    if n == TILES - 1:
                        m.then_inc(pooled_ps, 1)
                    return
                n -= TILES
                if n:
                    pe.wait_ge(side_sb, n)
                if n == 0:
                    pe.wait_ge(ld_small, 16 * N_SMALL)
                    pe.transpose(ps[6][:, 0:R], gw1[:], ident[0:R, 0:R])
                    last = pe.transpose(ps[6][0:R, P:2 * P], rw[:], ident[:])
                elif n == 1:
                    pe.wait_ge(sid_ready, 1)
                    mm(ps[5][0:R, 0:NS], gw1T[:], pooledT[:], start=True, stop=True)
                    last = mm(ps[5][0:SE, NS:2 * NS], emb[:], sid[:], start=True, stop=True)
                elif n == 2:
                    mm(ps[6][0:NS, 0:1], h1T[:], col[0:R, c_gw2:c_gw2 + 1], start=True, stop=True)
                    last = mm(ps[6][:, NS:2 * NS], hw1[:], seT[:], start=True, stop=True)
                elif n == 3:
                    last = mm(ps[5][:, 0:NS], hw2[:], hypT[:], start=True, stop=True)
                elif n == 4:
                    last = mm(ps[6][0:SH // 2, 0:NS], sw1[:], hyp2T[:], start=True, stop=True)
                else:
                    mm(ps[5][:, 0:NS], sw2[:, 0:D], styT[:], start=True, stop=True)
                    last = mm(ps[5][:, NS:2 * NS], sw2[:, D:2 * D], styT[:], start=True, stop=True)
                last.then_inc(side_ps, 1)

            pe.wait_ge(ld_uv, 32)
            for i in range(R):
                for k in range(2):
                    if i:
                        pe.wait_ge(gs_step[k], i)
                    mm(ps[4 * k][:, 0:R - i], Q[:, k, i:i + 1].to_broadcast([P, P]), Q[:, k, i:R],
                       start=True, stop=True).then_inc(gs_dots, 1)
                if 1 <= i <= N_SIDE:
                    if i == 1:
                        pe.wait_ge(consts, N_CONST)
                        pe.wait_ge(ld_x, 16)
                    side(i - 1)
                if i:
                    for _ in range(GS_BUSY):
                        mm(ps[7][:], ones[:], ones[:].unsqueeze(1).to_broadcast([P, 4, P]), start=True, stop=True)
                if i == GS_RANK2:
                    pe.wait_ge(a2_ready, 1)
                    mm(ps[3][0:NS, 0:E], tri[0:NS, 0:NS], a2[:], start=True, stop=True)
                    mm(ps[3][:, E:2 * E], ones[0:NS, :], a2[:], start=True, stop=True).then_inc(rank2_ps, 1)
                if i == GS_MAP2:
                    pe.wait_ge(oh88_ready, 1)
                    for q in range(SPT):
                        mm(ps[3][q * T:(q + 1) * T, NB2:2 * NB2], tokv[:], oh88[:, q, :], start=True, stop=True)
                    mm(ps[3][0:1, P:P + NB2 * SPT], sback[:], oh88[:].rearrange("s q b -> s b q"),
                       start=True, stop=True).then_inc(map2_ps, 1)
            pe.wait_ge(q_ready, 1)
            mm(ps[0][0:R, 0:R], Q[:, 1, :], Q[:, 1, :], start=True, stop=True)
            mm(ps[0][0:R, P:2 * P], Q[0:R, 0, :], rwT[:], start=True, stop=True)
            pe.transpose(ps[0][0:R, 2 * P:3 * P], Q[:, 0, :], ident[:]).then_inc(fold_ps, 1)
            pe.wait_ge(fold_sb, 1)
            mm(ps[4][0:R, 0:D], fold[:, 0, 0:R], fold[:, 1, :], start=True, stop=True).then_inc(fold_ps, 1)
            pe.wait_ge(fold_sb, 2)
            mm(ps[5][:, 0:D], fold[:, 2, :], fold[:, 3, :], start=True, stop=True).then_inc(fold_ps, 1)
            pe.wait_ge(str_in, 1)
            mm(ps[3][:, 0:TILES], smod[:].rearrange("s q t -> s (q t)"), strtile[:], start=True, stop=True).then_inc(str_ps, 1)
            pe.wait_ge(fold_sb, 3)
            pe.wait_ge(crow_ready, 1)
            pe.wait_ge(xt_sb, TILES)
            for g in range(GROUPS):
                if g >= 2:
                    pe.wait_ge(x1_ready, g - 1)
                bank = ps[1 + g % 2]
                mm(bank[:], onesrow[:], crow4[:].rearrange("o i d -> o (i d)"), start=True, stop=False)
                for j in range(GT):
                    t = g * GT + j
                    last = mm(bank[:, j * D:(j + 1) * D], xT[:, t * P:(t + 1) * P], M[:], start=False, stop=(j == GT - 1))
                last.then_inc(resp_ps, 1)
            for g in range(GROUPS):
                pe.wait_ge(h0_ready, g + 1)
                if g >= 2:
                    pe.wait_ge(hT_raw, g - 1)
                for j in range(GT):
                    last = pe.transpose(ps[4 + g % 2][:, j * P:(j + 1) * P], h0[:, g * GT + j, :], ident[:])
                last.then_inc(h0T_ps, 1)
            pe.wait_ge(trigt_ready, 1)
            mm(ps[6][:, P:2 * P], smod[:].rearrange("s q t -> s (q t)"), trigt[:].rearrange("s k i -> s (k i)"),
               start=True, stop=True).then_inc(trig_ps, 1)
            for g in range(GROUPS):
                pe.wait_ge(h_ready, g + 1)
                for t in range(g * GT, (g + 1) * GT):
                    last = mm(ps[7][:, t * E:(t + 1) * E], hT[:, t * P:(t + 1) * P], rout[:], start=True, stop=True)
                last.then_inc(logit_ps, 1)
            for g in range(GROUPS):
                if g >= 2:
                    pe.wait_ge(hrow_sb, g - 1)
                for j in range(GT):
                    t = g * GT + j
                    last = pe.transpose(ps[4 + g % 2][:, j * D:(j + 1) * D], hT[:, t * P:(t + 1) * P], ident[:])
                last.then_inc(hrow_ps, 1)
            pe.wait_ge(onehots, 1)
            mm(ps[3][:, 0:P], tri[:], both[:].rearrange("p i e -> p (i e)"), start=True, stop=True)
            mm(ps[3][:, P:2 * P], ones[:], both[:].rearrange("p i e -> p (i e)"), start=True, stop=True).then_inc(rank_ps, 1)
            pe.wait_ge(ld_rows, 16 * N_ROWS)
            pe.wait_ge(bexp_ready, 1)
            for k, (oh, n) in enumerate(((bexp1, NB1), (bexp2, NB2))):
                for c in range(FC):
                    at = k * FC * NB1 + c * n
                    last = mm(ps[6][:, at:at + n], brow[:, k, c * P:(c + 1) * P], oh[:], start=True, stop=True)
            last.then_inc(bias_ps, 1)
            pe.wait_ge(map_in, 1)
            pe.wait_ge(tok_lo, 1)
            for n in range(2 * TILES):
                last = mm(ps[1][:, 0:2 * NB1], ohp[:, n, :], tokb[:, n, :, :].rearrange("p k b -> p (k b)"),
                          start=(n == 0), stop=(n == 2 * TILES - 1))
            last.then_inc(map_ps, 1)

            def rows_T(b, r):
                pe.wait_ge(hg_ready[r % 2], 16 * (b // 2 + 1) if isinstance(b, int) else 8 * (b - r % 2) + 16)
                if not early(b, 2):
                    pe.wait_ge(row_T_sb, b - 1)
                pe.transpose(ps[r % 2][:, 0:P], hg[:, r % 2, :], ident[:]).then_inc(row_T_ps, 1)

            def up_product(u, w):
                for c in range(FC):
                    last = mm(ps[2 + 2 * (c // 2) + u][:, c % 2 * P:(c % 2 + 1) * P], ws[:, w, c * P:(c + 1) * P],
                              hgT[:, u, :], start=True, stop=True)
                return last

            def up(b, r):
                pe.wait_ge(row_T_sb, b + 1)
                pe.wait_ge(w1_ready[r % RING], 16 * (b // RING + 1) if isinstance(b, int) else 4 * (b - r % RING) + 16)
                if not early(b, 2):
                    pe.wait_ge(hidA_sb, b - 1)
                    pe.wait_ge(hidB_sb, b - 1)
                up_product(r % 2, r % RING).then_inc(up_ps, 1)

            def down(b, r):
                u = r % 2
                e = pe.value_load(bexi[0:1, bass.ds(b, 1)], min_val=0, max_val=E - 1)
                pe.wait_ge(hidA_sb, b + 1)
                pe.wait_ge(hidB_sb, b + 1)
                if not early(b, 2):
                    pe.wait_ge(es_ready, b - 1)
                for c in range(FC):
                    last = mm(ps[6 + u][:, 0:D], hid[:, u, c, :], w2[:, bass.ds(e, 1), c, :], start=(c == 0), stop=(c == FC - 1))
                last.then_inc(down_ps, 1)

            def step1(b, r):
                if not (isinstance(b, int) and b + 2 >= NB1):
                    rows_T(b + 2, r + 2)
                if not (isinstance(b, int) and b + 1 >= NB1):
                    up(b + 1, r + 1)
                down(b, r)

            pe.wait_ge(ld_w2, 16)
            rows_T(0, 0)
            rows_T(1, 1)
            up(0, 0)
            blocks(pe, NB1, RING, NB1 % RING, step1)

            def rows_T2(j, r):
                pe.wait_ge(x2_ready, j + 1)
                if not early(j, 2):
                    pe.wait_ge(xT2_sb, j - 1)
                pe.transpose(ps[r % 2][:, 0:P], x2[:, r % RING, :], ident[:]).then_inc(xT2_ps, 1)

            def up2(j, r):
                pe.wait_ge(xT2_sb, j + 1)
                pe.wait_ge(wi_ready[r % RING], 16 * (j // RING + 1) if isinstance(j, int) else 4 * (j - r % RING) + 16)
                if not early(j, 2):
                    pe.wait_ge(hid2_sb, j - 1)
                up_product(r % 2, r % RING).then_inc(up2_ps, 1)

            def down2(j, r):
                u = r % 2
                e = pe.value_load(bex2i[0:1, bass.ds(j, 1)], min_val=0, max_val=E - 1)
                if not early(j, 2):
                    pe.wait_ge(b_rr, j - 1)
                mm(ps[6 + u][:, 0:D], onesrow[:], bor[:, bass.ds(e, 1), :], start=True, stop=False)
                pe.wait_ge(hid2_sb, j + 1)
                for c in range(FC):
                    last = mm(ps[6 + u][:, 0:D], hid[:, u, c, :], wo[:, bass.ds(e, 1), c, :], start=False, stop=(c == FC - 1))
                last.then_inc(down2_ps, 1)

            def step2(j, r):
                if not (isinstance(j, int) and j + 2 >= NB2):
                    rows_T2(j + 2, r + 2)
                if not (isinstance(j, int) and j + 1 >= NB2):
                    up2(j + 1, r + 1)
                down2(j, r)

            pe.wait_ge(ld_wo, 16)
            pe.wait_ge(es_ready, NB1)
            rows_T2(0, 0)
            rows_T2(1, 1)
            up2(0, 0)
            blocks(pe, NB2, RING, NB2 % RING, step2)

        @block.vector
        def _(dve):
            count = [0]

            def link(ins):
                count[0] += 1
                ins.then_inc(dve_own, 1)
                dve.wait_ge(dve_own, count[0])

            def masks():
                dve.wait_ge(consts, N_CONST)
                dve.wait_ge(ld_small, 16 * N_SMALL)
                link(dve.tensor_scalar(smodi[:], pidxi[0:NS, :], SPT - 1, None, ALU.bitwise_and))
                link(dve.tensor_scalar(pmodi[:], pidxi[:], T - 1, None, ALU.bitwise_and))
                link(dve.tensor_copy(smodf[:], smodi[:]))
                link(dve.tensor_copy(pmod[:], pmodi[:]))
                link(dve.tensor_scalar(smod[:], qio[:], smodf[:], None, ALU.is_equal))
                link(dve.tensor_copy(idf[:], id1[:]))
                dve.tensor_scalar(sid[:], idf[:], pidx[0:SUBJ, :], None, ALU.is_equal).then_inc(sid_ready, 1)
                link(dve.tensor_add(crow[:], biasrow[:, 0, :], biasrow[:, 1, :]))
                dve.tensor_copy(crow4[:], crow[:].unsqueeze(1).to_broadcast([1, GT, D])).then_inc(crow_ready, 1)

            def blocks_of(counts, steps, cmp, n, upto, before):
                link(dve.tensor_tensor(cmp[:], counts.unsqueeze(2).to_broadcast([P, E, TILES]),
                                       steps[:].unsqueeze(1).to_broadcast([P, E, TILES]), ALU.is_gt))
                link(dve.tensor_reduce(n[:], cmp[:], AX.X, ALU.add))
                link(dve.tensor_tensor_scan(upto[:], ones8[:], n[:], 0.0, ALU.mult, ALU.add))
                link(dve.tensor_tensor(before[:], upto[:], n[:], ALU.subtract))

            def expert_of_block(cmp, upto, asfloat, asint, n):
                link(dve.tensor_tensor(cmp[:], iob[:, 0:n].unsqueeze(2).to_broadcast([P, n, E]),
                                       upto[:].unsqueeze(1).to_broadcast([P, n, E]), ALU.is_ge))
                link(dve.tensor_reduce(asfloat[:], cmp[:], AX.X, ALU.add))
                return dve.tensor_scalar_min(asint[:], asfloat[:], float(E - 1))

            two = slice(0, 2)

            def turns():
                link(dve.tensor_scalar(angk[:, two], smp[:, 1:3], 1.0 / (2 * PI), ROUND, ALU.mult, ALU.add))
                link(dve.tensor_scalar_add(angk[:, two], angk[:, two], -ROUND))
                link(dve.scalar_tensor_tensor(ang[:, two], angk[:, two], -PI2_HI, smp[:, 1:3], ALU.mult, ALU.add))

            def reduced():
                link(dve.scalar_tensor_tensor(angr[:, two], angk[:, two], -PI2_LO, ang[:, two], ALU.mult, ALU.add))
                link(dve.tensor_scalar_add(angr[:, 2:4], angr[:, two], PI / 2))
                link(dve.tensor_scalar(angk[:], angr[:], PI, -2 * PI, ALU.is_gt, ALU.mult))

            def clamped():
                link(dve.tensor_tensor(ang[:], angr[:], angk[:], ALU.add))
                dve.tensor_scalar(angw[:], ang[:], 3.1415925, -3.1415925, ALU.min, ALU.max).then_inc(ang_ready, 1)

            ANGLES = [turns, reduced, clamped]

            dve.wait_ge(ld_uv, 32)
            for i in range(R):
                dve.wait_ge(gs_norm, 2 * i + 2)
                link(dve.tensor_scalar_add(gsd[:], gsn[:], EPS_GS))
                link(dve.reciprocal(gsr[:], gsd[:]))
                q = dve.tensor_tensor(Q[:, :, i], Q[:, :, i], gsr[:], ALU.mult)
                if i == R - 1:
                    q.then_inc(q_ready, 1)
                    break
                link(q)
                link(dve.tensor_tensor(gss[:], Q[:, :, i], gsr[:], ALU.mult))
                for k in range(2):
                    dve.scalar_tensor_tensor(Q[:, k, i + 1:R], ps[4 * k][:, 1:R - i], gss[:, k:k + 1],
                                             Q[:, k, i + 1:R], ALU.mult, ALU.subtract, reverse1=True).then_inc(gs_step[k], 1)
                if i == GS_MASKS:
                    masks()
                elif i == GS_A2:
                    link(dve.tensor_copy(id2f[:], id2[:]))
                    link(dve.tensor_scalar(a2f[:], iob[0:NS, 0:E], id2f[:], None, ALU.is_equal))
                    dve.tensor_copy(a2[:], a2f[:]).then_inc(a2_ready, 1)
                elif GS_ANGLES <= i < GS_ANGLES + len(ANGLES):
                    ANGLES[i - GS_ANGLES]()
                elif i == GS_RANK2:
                    dve.wait_ge(rank2_ps, 1)
                    link(dve.tensor_copy(cnt2[:], ps[3][:, E:2 * E]))
                    blocks_of(cnt2[:], sstep, cmp2, nb2, cb2, cbe2)
                elif i == GS_RANK2 + 1:
                    link(expert_of_block(cmpb2, cb2, bex2f, bex2i, NB2))
                    link(dve.scalar_tensor_tensor(slot2e[:], cbe2[0:NS, :], float(SPT), ps[3][0:NS, 0:E], ALU.mult, ALU.add))
                elif i == GS_RANK2 + 2:
                    link(dve.tensor_tensor(a2f[:], a2f[:], slot2e[:], ALU.mult))
                    link(dve.tensor_reduce(slot2[:], a2f[:], AX.X, ALU.add))
                    dve.tensor_scalar(oh88[:], io88[:], slot2[:], None, ALU.is_equal).then_inc(oh88_ready, 1)
                elif i == GS_MAP2:
                    dve.wait_ge(map2_ps, 1)
                    dve.tensor_scalar(samp[:], ps[3][0:1, P:P + NB2 * SPT], float(NS), None, ALU.add)
                    dve.tensor_scalar(map2[:], ps[3][:, NB2:2 * NB2], pmod[:], None, ALU.add).then_inc(map2_ready, 1)

            dve.wait_ge(fold_ps, 1)
            dve.tensor_copy(fold[:, 0, 0:R], ps[0][0:R, 0:R])
            dve.tensor_copy(fold[:, 1:3, :], ps[0][0:R, P:3 * P].rearrange("p (k d) -> p k d", d=D)).then_inc(fold_sb, 1)
            dve.wait_ge(z_exp, 1)
            link(dve.tensor_scalar_add(zden[:], zexp[:], 1.0))
            link(dve.reciprocal(zsig[:], zden[:]))
            link(dve.tensor_tensor(stren[:], zsig[:, 0:1], zsig[:, 1:2], ALU.mult))
            dve.tensor_scalar(strtile[:], tmask[:], stren[:], None, ALU.mult).then_inc(str_in, 1)
            dve.wait_ge(fold_ps, 2)
            dve.tensor_copy(fold[:, 3, :], ps[4][0:R, 0:D]).then_inc(fold_sb, 1)
            dve.wait_ge(fold_ps, 3)
            dve.tensor_copy(M[:], ps[5][:, 0:D]).then_inc(fold_sb, 1)
            dve.wait_ge(str_ps, 1)
            link(dve.tensor_copy(strT[:], ps[3][:, 0:TILES]))
            dve.wait_ge(style_exp, 1)
            link(dve.tensor_scalar_max(gpos[:], graw[:], 0.0))
            link(dve.scalar_tensor_tensor(gammaT[:], gpos[:], EPS_SP, gln[:], ALU.add, ALU.add))

            def x1_of(g):
                dve.wait_ge(resp_ps, g + 1)
                for j in range(GT):
                    t = g * GT + j
                    last = dve.scalar_tensor_tensor(x1r[:, t, 0:D], ps[1 + g % 2][:, j * D:(j + 1) * D], strT[:, t:t + 1],
                                                    X[:, t, :], ALU.mult, ALU.add)
                last.then_inc(x1_ready, 1)
                dve.wait_ge(x1_ready, g + 1)
                for t in range(g * GT, (g + 1) * GT):
                    last = dve.bn_stats(bst[:, t, :], x1r[:, t, 0:D])
                link(last)
                for t in range(g * GT, (g + 1) * GT):
                    last = dve.bn_aggr(mv[:, t, :], bst[:, t, :])
                link(last)
                dve.tensor_scalar_add(g128(ve, g), g128(mv, g)[:, :, 1], EPS_LN).then_inc(var_ready, 1)

            def shift_of(g):
                dve.wait_ge(std_ready, g + 1)
                link(dve.reciprocal(g128(rstd, g), g128(rs, g)))
                dve.scalar_tensor_tensor(g128(nmr, g), g128(mv, g)[:, :, 0], -1.0, g128(rstd, g), ALU.mult,
                                         ALU.mult).then_inc(nmr_ready, 1)

            for g in range(GROUPS):
                x1_of(g)
                if g:
                    shift_of(g - 1)
            shift_of(GROUPS - 1)

            dve.wait_ge(trig_ready, 1)
            for k in range(4):
                dve.tensor_copy(trig8[:, k:k + 1], trig[:, 2 + k // 2:3 + k // 2])
                last = dve.tensor_scalar_mul(trig8[:, 4 + k:5 + k], trig[:, k // 2:k // 2 + 1], -1.0 if k % 2 else 1.0)
            link(last)
            dve.tensor_tensor(trigt[:], trig8[:].unsqueeze(2).to_broadcast([NS, 8, TILES]),
                              tmask[:].unsqueeze(1).to_broadcast([NS, 8, TILES]), ALU.mult).then_inc(trigt_ready, 1)

            def over_tokens(g):
                return hT[:, g * GW:(g + 1) * GW].rearrange("p (s t) -> p s t", t=T), slice(g * SPG, (g + 1) * SPG)

            def spread(t, ss):
                return t[:, ss].unsqueeze(2).to_broadcast([P, SPG, T])

            for g in range(GROUPS):
                h, ss = over_tokens(g)
                dve.wait_ge(hT_raw, g + 1)
                link(dve.tensor_reduce(tsum[:, ss], h, AX.X, ALU.add))
                dve.scalar_tensor_tensor(h, spread(tsum, ss), -1.0 / T, h, ALU.mult, ALU.add).then_inc(hT_centred, 1)
            for g in range(GROUPS):
                h, ss = over_tokens(g)
                dve.wait_ge(sq_ready, g + 1)
                link(dve.tensor_reduce(tvar[:, ss], sq[:, g * GW:(g + 1) * GW].rearrange("p (s t) -> p s t", t=T),
                                       AX.X, ALU.add))
                dve.tensor_scalar(tve[:, ss], tvar[:, ss], 1.0 / T, EPS_T, ALU.mult, ALU.add).then_inc(tvar_ready, 1)
            for g in range(GROUPS):
                h, ss = over_tokens(g)
                dve.wait_ge(tstd_ready, g + 1)
                link(dve.reciprocal(trr[:, ss], trs[:, ss]))
                link(dve.tensor_tensor(tsc[:, ss], trr[:, ss], gammaT[:, ss], ALU.mult))
                link(dve.tensor_tensor(h, h, spread(tsc, ss), ALU.mult))
                dve.tensor_tensor(h, h, spread(betaT, ss), ALU.add).then_inc(h_ready, 1)

            dve.wait_ge(trig_ps, 1)
            dve.tensor_copy(x1r[:, :, C_COS:C_COS + 8],
                            ps[6][:, P:2 * P].rearrange("p (k i) -> p i k", i=TILES))

            def wide(t):
                return t[:].unsqueeze(2).to_broadcast([P, TILES, E])

            dve.wait_ge(logit_ps, GROUPS)
            logits = ps[7][:, 0:P].rearrange("p (i e) -> p i e", e=E)
            link(dve.tensor_reduce(rmx[:], logits, AX.X, ALU.max))
            dve.tensor_tensor(rsh[:], logits, wide(rmx), ALU.subtract).then_inc(logit_shift, 1)
            dve.wait_ge(logit_exp, 1)
            link(dve.tensor_reduce(rsum[:], rex[:], AX.X, ALU.add))
            link(dve.reciprocal(rrec[:], rsum[:]))
            link(dve.tensor_tensor(rp[:], rex[:], wide(rrec), ALU.mult))
            for probs, m, mm, o in ((rp, m1, mm1, o1), (rp2, m2, mm2, o2)):
                link(dve.tensor_reduce(m[:], probs[:], AX.X, ALU.max))
                link(dve.tensor_tensor(req[:], probs[:], wide(m), ALU.is_equal))
                link(dve.tensor_tensor(rwt[:], req[:], down8[:], ALU.mult))
                link(dve.tensor_reduce(mm[:], rwt[:], AX.X, ALU.max))
                link(dve.tensor_tensor(o[:], rwt[:], wide(mm), ALU.is_equal))
                if o is o1:
                    link(dve.scalar_tensor_tensor(rp2[:], o1[:], -2.0, rp[:], ALU.mult, ALU.add))
            dve.tensor_tensor(both[:], o1[:], o2[:], ALU.add).then_inc(onehots, 1)
            link(dve.tensor_tensor(gsum[:], m1[:], m2[:], ALU.add))
            link(dve.reciprocal(grec[:], gsum[:]))
            dve.tensor_tensor(x1r[:, :, C_GATE], m1[:], grec[:], ALU.mult)
            dve.tensor_tensor(x1r[:, :, C_GATE + 1], m2[:], grec[:], ALU.mult)

            dve.wait_ge(rank_ps, 1)
            link(dve.tensor_copy(tot[:], ps[3][:, P:2 * P].rearrange("p (i e) -> p e i", e=E)))
            flat = lambda t: t[:].rearrange("p e i -> p (e i)")
            link(dve.tensor_tensor_scan(flat(incl), flat(segm), flat(tot), 0.0, ALU.mult, ALU.add))

            blocks_of(incl[:, :, TILES - 1], bstep, cmp8, nb, cb, cbe)
            expert_of_block(cmpb, cb, bexf, bexi, NB1).then_inc(places, 1)
            for oh, of in ((bexp1, bexf), (bexp2, bex2f)):
                last = dve.tensor_scalar(oh[:], of[0:E, :], pidx[0:E, :], None, ALU.is_equal)
            last.then_inc(bexp_ready, 1)
            link(dve.tensor_tensor(texc[:], incl[:], tot[:], ALU.subtract))
            link(dve.scalar_tensor_tensor(tbase[:], cbe[:].unsqueeze(2).to_broadcast([P, E, TILES]), float(P), texc[:],
                                          ALU.mult, ALU.add))
            link(dve.tensor_tensor(slots[:], ps[3][:, 0:P].rearrange("p (i e) -> p i e", e=E),
                                   tbase[:].rearrange("p e i -> p i e"), ALU.add))
            for k, o in enumerate((o1, o2)):
                link(dve.tensor_tensor(pick[:], o[:], slots[:], ALU.mult))
                link(dve.tensor_reduce(slotf[:, :, k], pick[:], AX.X, ALU.add))
            link(dve.tensor_copy(sloti[:], slotf[:]))
            dve.tensor_copy(x1r[:, :, C_SLOT:C_SLOT + 2].bitcast(I32), sloti[:]).then_inc(x_row_ready, 1)
            dve.tensor_scalar(slpi[:], sloti[:], P - 1, None, ALU.bitwise_and)
            link(dve.tensor_scalar(slbi[:], sloti[:], 7, None, ALU.logical_shift_right))
            dve.tensor_copy(slp[:], slpi[:])
            link(dve.tensor_copy(slb[:], slbi[:]))
            dve.tensor_tensor(eqb, iob[:].unsqueeze(1).to_broadcast([P, 2 * TILES, NB1]),
                              slb[:].rearrange("p i k -> p (i k)").unsqueeze(2).to_broadcast([P, 2 * TILES, NB1]),
                              ALU.is_equal).then_inc(eqb_ready, 1)
            dve.wait_ge(eqb_ready, 1)
            dve.tensor_tensor(tokb[:, :, 0, :], eqb,
                              tileio[:].rearrange("p i k -> p (i k)").unsqueeze(2).to_broadcast([P, 2 * TILES, NB1]), ALU.mult)
            for n in range(2 * TILES):
                last = dve.tensor_scalar(ohp[:, n, :], io128[:], slp[:, n // 2, n % 2:n % 2 + 1], None, ALU.is_equal)
            last.then_inc(map_in, 1)
            dve.wait_ge(map_ps, 1)
            link(dve.tensor_copy(hilo[:], ps[1][:, 0:2 * NB1].rearrange("p (k b) -> p k b", k=2)))
            dve.scalar_tensor_tensor(map1[:], hilo[:, 0, :], float(P), hilo[:, 1, :], ALU.mult, ALU.add).then_inc(map_ready, 1)

            def expert(table, b):
                return dve.value_load(table[0:1, bass.ds(b, 1)], min_val=0, max_val=E - 1)

            def columns(b, r):
                dve.wait_ge(row_T_ps, b + 1)
                if not early(b, 2):
                    dve.wait_ge(up_ps, b - 1)
                dve.tensor_copy(hgT[:, r % 2, :], ps[r % 2][:, 0:P]).then_inc(row_T_sb, 1)

            def hidden(b, r):
                u = r % 2
                dve.wait_ge(up_ps, b + 1)
                if not early(b, 2):
                    dve.wait_ge(down_ps, b - 1)
                for c in range(FC // 2, FC):
                    last = dve.tensor_scalar(hid[:, u, c, :], ps[4 + u][:, (c - FC // 2) * P:(c - FC // 2 + 1) * P],
                                             bh1[:, c, bass.ds(b, 1)], 0.0, ALU.add, ALU.max)
                last.then_inc(hidB_sb, 1)

            def rows_out(b, r):
                u = r % 2
                dve.wait_ge(down_ps, b + 1)
                dve.wait_ge(b2_ready[r % RING], 16 * (b // RING + 1) if isinstance(b, int) else 4 * (b - r % RING) + 16)
                if not early(b, 2):
                    dve.wait_ge(es_stored[u], 16 * (b // 2) if isinstance(b, int) else 8 * (b - u))
                dve.tensor_tensor(es[:, u, :], ps[6 + u][:, 0:D], b2blk[:, r % RING, :], ALU.add).then_inc(es_ready, 1)

            def row_of(t, e):
                return t[:, bass.ds(e, 1), :].rearrange("p o d -> p (o d)")

            def step1(b, r):
                if not (isinstance(b, int) and b + 2 >= NB1):
                    columns(b + 2, r + 2)
                if not (isinstance(b, int) and b + 1 >= NB1):
                    hidden(b + 1, r + 1)
                rows_out(b, r)

            dve.wait_ge(bias_ready, 1)
            columns(0, 0)
            columns(1, 1)
            hidden(0, 0)
            blocks(dve, NB1, RING, NB1 % RING, step1)

            dve.wait_ge(ld_rows, 16 * N_ROWS)
            def of_block(j, a, b):
                return xg[:, bass.ds(j, 1), a:b].rearrange("p o c -> p (o c)")

            def wait2(s_, j):
                dve.wait_ge(s_, j + 1)

            def step2(j, r):
                comb = not (isinstance(j, int) and j + 3 >= NB2)
                meas = not (isinstance(j, int) and not 0 <= j < NB2)
                norm = not (isinstance(j, int) and j < 3)
                c, rc, rn = j + 3, (r + 3) % RING, (r - 3) % RING
                n = j - 3
                if norm:
                    en = expert(bex2i, n)
                    wait2(rs2_ready, n)
                    dve.tensor_scalar(yn[:], rr[:, rn, :], mv2[:, rn, 0:1], rs2[:, rn:rn + 1], ALU.subtract,
                                      ALU.mult).then_inc(n_yn, 1)
                if comb:
                    if not early(c, 1):
                        dve.wait_ge(x2_ready, c)
                    dve.wait_ge(eg_ready[rc % 2], 32 * (c // 2 + 1) if isinstance(c, int) else 16 * (c - rc % 2) + 32)
                    dve.scalar_tensor_tensor(x2a[:], one(eg, c, 0), of_block(c, C_GATE, C_GATE + 1), of_block(c, 0, D),
                                             ALU.mult, ALU.add).then_inc(c_x2a, 1)
                if norm:
                    wait2(n_yn, n)
                    dve.tensor_tensor(yg[:], yn[:], row_of(g2r, en), ALU.mult).then_inc(n_yg, 1)
                if comb:
                    wait2(c_x2a, c)
                    dve.scalar_tensor_tensor(x2[:, rc, :], one(eg, c, 1), of_block(c, C_GATE + 1, C_GATE + 2), x2a[:],
                                             ALU.mult, ALU.add).then_inc(x2_ready, 1)
                if norm:
                    wait2(n_yg, n)
                    dve.tensor_tensor(yb[:], yg[:], row_of(be2r, en), ALU.add).then_inc(n_yb, 1)
                if meas:
                    wait2(down2_ps, j)
                    wait2(x2_ready, j)
                    dve.tensor_tensor(rr[:, r, :], ps[6 + r % 2][:, 0:D], x2[:, r, :], ALU.add).then_inc(b_rr, 1)
                if norm:
                    wait2(n_yb, n)
                    y4 = yb[:].rearrange("p (a c) -> p a c", c=4)
                    s4 = ysn[:].rearrange("p (a c) -> p a c", c=4)
                    cos = xg[:, bass.ds(n, 1), C_COS:C_COS + 4].to_broadcast([P, D // 4, 4])
                    sin = xg[:, bass.ds(n, 1), C_SIN:C_SIN + 4].to_broadcast([P, D // 4, 4])
                    dve.tensor_tensor(yc[:].rearrange("p (a c) -> p a c", c=4), y4, cos, ALU.mult)
                if meas:
                    wait2(b_rr, j)
                    dve.bn_stats(st2[:], rr[:, r, :]).then_inc(b_stats, 1)
                if norm:
                    for k in range(2):
                        last = dve.tensor_tensor(s4[:, :, k::2], y4[:, :, 1 - k::2], sin[:, :, k::2], ALU.mult)
                        if meas and k == 0:
                            wait2(b_stats, j)
                    last.then_inc(n_rot, 1)
                elif meas:
                    wait2(b_stats, j)
                if meas:
                    dve.bn_aggr(mv2[:, r, :], st2[:]).then_inc(b_aggr, 1)
                if norm:
                    wait2(n_rot, n)
                    if not early(n, 2):
                        dve.wait_ge(yo_stored[rn % 2], 64 * (n // 2) if isinstance(n, int) else 32 * (n - rn % 2))
                    dve.tensor_tensor(yo[:, rn % 2, :], yc[:], ysn[:], ALU.add).then_inc(yo_ready, 1)
                if meas:
                    wait2(b_aggr, j)
                    dve.tensor_scalar_add(ve2[:, r:r + 1], mv2[:, r, 1:2], EPS_L2).then_inc(ve2_ready, 1)

            def one(t, j, k):
                return t[:, bass.ds(j, 1), k, :].rearrange("p o d -> p (o d)")

            for j in range(-3, 0):
                step2(j, j % RING)
            blocks(dve, NB2 + LAG, RING, RING + LAG + NB2 % RING, step2)


_INS = ["x", "condB_safetyscore", "itok_B_6_14", "itok_B_0_7", "condB_theta", "condB_phi"] + [
    f"L0_cond_{n}" for n in ("U", "V", "safety_bias", "gate_w1", "gate_b1", "gate_w2", "gate_b2", "resp_w", "resp_b")] + [
    f"L1_cond_{n}" for n in ("ln_g", "ln_b", "subj_emb", "hyp_w1", "hyp_b1", "hyp_w2", "hyp_b2", "sty_w1", "sty_b1",
                             "sty_w2", "sty_b2", "router_w", "exp_w1", "exp_b1", "exp_w2", "exp_b2")] + [
    f"L2_cond_{n}" for n in ("Wi", "bi", "Wo", "bo", "gamma", "beta")]
_OUTS = [((NS, T, D), "float32")]


def kernel(**inputs):
    import numpy as _np
    import concourse.bacc as _bacc
    from concourse import mybir as _mybir
    from concourse.bass_utils import run_bass_kernel_spmd as _run

    nc = _bacc.Bacc("TRN2", target_bir_lowering=False, num_devices=1)
    arrays, args = {}, []
    for name in _INS:
        a = _np.ascontiguousarray(inputs[name])
        arrays[f"in_{name}_dram"] = a
        args.append(nc.dram_tensor(f"in_{name}_dram", a.shape, _mybir.dt.from_np(a.dtype), kind="ExternalInput").ap())
    for i, (shape, dtype) in enumerate(_OUTS):
        dt = _mybir.dt.from_np(_np.dtype(dtype))
        args.append(nc.dram_tensor(f"out_{i}_dram", shape, dt, kind="ExternalOutput").ap())
    cond_seq_kernel(nc, *args)
    r = _run(nc, [arrays], core_ids=[0])
    got = tuple(r.results[0][f"out_{i}_dram"] for i in range(len(_OUTS)))
    return got[0]
```

```python
import concourse.bass as bass
from concourse import mybir
from contextlib import ExitStack

F32, BF16, I32 = mybir.dt.float32, mybir.dt.bfloat16, mybir.dt.int32
ALU, ACT, AX = mybir.AluOpType, mybir.ActivationFunctionType, mybir.AxisListType

P = 128
D = 128
NS, T = 64, 32
NT = NS * T
TILES = NT // P
SPT = P // T
GT = 4
GROUPS = TILES // GT
GW = GT * P
SPG = GT * SPT
R = 32
E = 8
FF = 512
FC = FF // P
SUBJ, SE, SH = 32, 64, 128
NB1 = 2 * TILES + E - 1
NB2 = (NS + E * (SPT - 1)) // SPT
NLAG = 4
LAG = 3
RING = 4
XW = D + 12
C_SLOT, C_GATE, C_COS, C_SIN = D, D + 2, D + 4, D + 8
EPS_GS, EPS_LN, EPS_T, EPS_SP, EPS_L2 = 1e-8, 1e-5, 1e-8, 1e-8, 1e-12
PI = 3.141592653589793
PI2_HI, PI2_LO = 6.28125, 2 * PI - 6.28125
ROUND = 12582912.0


def cond_seq_kernel(nc, x, score, ids1, ids2, theta, phi, U, V, safety_bias, gate_w1, gate_b1, gate_w2,
                    gate_b2, resp_w, resp_b, ln_g, ln_b, subj_emb, hyp_w1, hyp_b1, hyp_w2, hyp_b2,
                    sty_w1, sty_b1, sty_w2, sty_b2, router_w, exp_w1, exp_b1, exp_w2, exp_b2,
                    Wi, bi, Wo, bo, gamma2, beta2, out):
    ctx = ExitStack()
    with ctx:
        def sb(name, shape, dt=F32):
            return ctx.enter_context(nc.sbuf_tensor(name, shape, dt))

        def sem(name):
            return ctx.enter_context(nc.semaphore(name))

        w2 = sb("w2", [P, E, FC, D])
        wo = sb("wo", [P, E, FC, D])
        brow = sb("brow", [E, 2, FF])
        bexp1 = sb("bexp1", [E, NB1])
        bexp2 = sb("bexp2", [E, NB2])
        bh1 = sb("bh1", [P, FC, NB1])
        bh2 = sb("bh2", [P, FC, NB2])
        b2blk = sb("b2blk", [P, RING, D])
        bor = sb("bor", [1, E, D])
        g2r = sb("g2r", [P, E, D])
        be2r = sb("be2r", [P, E, D])
        Q = sb("Q", [P, 2, R])
        gw1 = sb("gw1", [R, D])
        rw = sb("rw", [P, R])
        col = sb("col", [P, 12])
        c_gb1, c_gw2, c_lng, c_lnb, c_hb1, c_hb2, c_sb1, c_sg, c_sbt = range(9)
        biasrow = sb("biasrow", [1, 2, D])
        gb2 = sb("gb2", [NS, 1])
        emb = sb("emb", [SUBJ, SE])
        hw1 = sb("hw1", [SE, SH])
        hw2 = sb("hw2", [SH, SH])
        sw1 = sb("sw1", [SH, SH // 2])
        sw2 = sb("sw2", [SH // 2, 2 * D])
        rout = sb("rout", [D, E])
        smp = sb("smp", [NS, 3])
        id1 = sb("id1", [SUBJ, NS], I32)
        id2 = sb("id2", [NS, 1], I32)
        ident = sb("ident", [P, P])
        tri = sb("tri", [P, P], BF16)
        ones = sb("ones", [P, P], BF16)
        onesrow = sb("onesrow", [1, P])
        mean4 = sb("mean4", [P, SPT])
        tmask = sb("tmask", [NS, TILES])
        smod = sb("smod", [NS, SPT, T])
        smodi = sb("smodi", [NS, 1], I32)
        smodf = sb("smodf", [NS, 1])
        qio = sb("qiota", [NS, SPT, T])
        io128 = sb("io128", [P, P], BF16)
        iob16 = sb("iob16", [P, NB1], BF16)
        down8 = sb("down8", [P, TILES, E])
        segm = sb("segm", [P, E, TILES])
        ones8 = sb("ones8", [P, E])
        pidx = sb("pidx", [P, 1])
        pmod = sb("pmod", [P, 1])
        pmodi = sb("pmodi", [P, 1], I32)
        pidxi = sb("pidxi", [P, 1], I32)
        mhalf = sb("mhalf", [P, 2])
        iob = sb("iob", [P, NB1])
        bstep = sb("bstep", [P, TILES])
        sstep = sb("sstep", [P, TILES])
        big = sb("big", [P, 4 * NT])
        tiles_of = lambda a: a.rearrange("p (i d) -> p i d", d=D)
        X = tiles_of(big[:, 0:NT])
        xT = big[:, NT:2 * NT]
        x1r = sb("x1r", [P, TILES, XW])
        h0 = tiles_of(big[:, 2 * NT:3 * NT])
        hT = big[:, 3 * NT:4 * NT]
        sq = xT
        hrow = X

        hdram = nc.dram_tensor("h_rows", [NT, D], F32).ap()
        xdram = nc.dram_tensor("x1_rows", [NT, XW], F32).ap()
        edram = nc.dram_tensor("expert_rows", [NB1 * P, D], F32).ap()

        sid = sb("sid", [SUBJ, NS])
        idf = sb("idf", [SUBJ, NS])
        gw1T = sb("gw1T", [D, R])
        rwT = sb("rwT", [R, D])
        pooledT = sb("pooledT", [D, NS])
        h1T = sb("h1T", [R, NS])
        seT = sb("seT", [SE, NS])
        hypT = sb("hypT", [SH, NS])
        hyp2T = sb("hyp2T", [SH, NS])
        styT = sb("styT", [SH // 2, NS])
        graw = sb("graw", [D, NS])
        gabs = sb("gabs", [D, NS])
        gexp = sb("gexp", [D, NS])
        gln = sb("gln", [D, NS])
        gpos = sb("gpos", [D, NS])
        gammaT = sb("gammaT", [D, NS])
        betaT = sb("betaT", [D, NS])
        gsn = sb("gsn", [P, 2, 2])
        gsd, gsd2, gsr, gss = (sb(n, [P, 2]) for n in ("gsd", "gsd2", "gsr", "gss"))
        gseps = sb("gseps", [P, 1])
        crow = sb("crow", [1, D])
        crow4 = sb("crow4", [1, GT, D])
        fold = sb("fold", [R, 4, D])
        M = sb("M", [D, D])
        zs = sb("zs", [NS, 2])
        zexp = sb("zexp", [NS, 2])
        zden = sb("zden", [NS, 2])
        zsig = sb("zsig", [NS, 2])
        stren = sb("stren", [NS, 1])
        strtile = sb("strtile", [NS, TILES])
        strT = sb("strT", [P, TILES])
        bst = sb("bst", [P, TILES, 6])
        mv = sb("mv", [P, TILES, 2])
        ve, rs, rstd, nmr = (sb(n, [P, TILES]) for n in ("ve", "rs", "rstd", "nmr"))
        tsum, tmean, tvar, tve, trs, trr, tsc = (sb(n, [P, NS]) for n in ("tsum", "tmean", "tvar", "tve", "trs", "trr", "tsc"))
        rt = lambda n, dt=F32: sb(n, [P, TILES, E], dt)
        rsh, rex, rp, req, rwt, o1, o2, rp2, slots, pick = (rt(n) for n in (
            "rsh", "rex", "rp", "req", "rwt", "o1", "o2", "rp2", "slots", "pick"))
        both = rt("both", BF16)
        rmx, rsum, rrec, m1, m2, mm1, mm2, gsum, grec = (sb(n, [P, TILES]) for n in (
            "rmx", "rsum", "rrec", "m1", "m2", "mm1", "mm2", "gsum", "grec"))
        tot, incl, texc, tbase = (sb(n, [P, E, TILES]) for n in ("tot", "incl", "texc", "tbase"))
        cmp8 = sb("cmp8", [P, E, TILES])
        nb, cb, cbe = (sb(n, [P, E]) for n in ("nb", "cb", "cbe"))
        cmpb = sb("cmpb", [P, NB1, E])
        bexf = sb("bexf", [P, NB1])
        bexi = sb("bexi", [P, NB1], I32)
        slotf = sb("slotf", [P, TILES, 2])
        sloti = sb("sloti", [P, TILES, 2], I32)
        slpi = sb("slpi", [P, TILES, 2], I32)
        slbi = sb("slbi", [P, TILES, 2], I32)
        slp = sb("slp", [P, TILES, 2])
        slb = sb("slb", [P, TILES, 2], BF16)
        ohp = sb("ohp", [P, 2 * TILES, P], BF16)
        eqb = sb("eqb", [P, 2 * TILES, NB1], BF16)
        tokb = sb("tokb", [P, 2 * TILES, 2, NB1], BF16)
        hilo = sb("hilo", [P, 2, NB1])
        mapf = sb("mapf", [P, NB1])
        map1 = sb("map1", [P, NB1], I32)
        id2f = sb("id2f", [NS, 1])
        a2 = sb("a2", [NS, E], BF16)
        a2f = sb("a2f", [NS, E])
        cnt2 = sb("cnt2", [P, E])
        cmp2 = sb("cmp2", [P, E, TILES])
        nb2, cb2, cbe2 = (sb(n, [P, E]) for n in ("nb2", "cb2", "cbe2"))
        slot2, slot2e = sb("slot2", [NS, 1]), sb("slot2e", [NS, E])
        io88 = sb("io88", [NS, SPT, NB2])
        oh88 = sb("oh88", [NS, SPT, NB2])
        tokv = sb("tokv", [NS, T])
        sback = sb("sback", [NS, 1])
        cmpb2 = sb("cmpb2", [P, NB2, E])
        bex2f = sb("bex2f", [P, NB2])
        bex2i = sb("bex2i", [P, NB2], I32)
        map2 = sb("map2", [P, NB2], I32)
        samp = sb("samp", [1, NB2 * SPT], I32)
        ang = sb("ang", [NS, 4])
        angk, angr, angw, trig = (sb(n, [NS, 4]) for n in ("angk", "angr", "angw", "trig"))
        trig8 = sb("trig8", [NS, 8])
        trigt = sb("trigt", [NS, 8, TILES])
        hg = sb("hg", [P, RING, D])
        hgT = sb("hgT", [P, 2, P])
        ws = sb("ws", [P, RING, FF])
        hid = sb("hid", [P, 2, FC, P])
        es = sb("es", [P, 2, D])
        xg = sb("xg", [P, NB2, XW])
        eg = big[:, 0:NB2 * 2 * D].rearrange("p (j k d) -> p j k d", k=2, d=D)
        x2a = sb("x2a", [P, D])
        x2, rr = (sb(n, [P, RING, D]) for n in ("x2", "rr"))
        st2, mv2 = sb("st2", [P, 6]), sb("mv2", [P, RING, 2])
        ve2, rs2 = (sb(n, [P, RING]) for n in ("ve2", "rs2"))
        yn = sb("yn", [P, 2, D])
        yb = sb("yb", [P, D])
        yc = sb("yc", [P, D])
        ysn = sb("ysn", [P, D])
        yo = sb("yo", [P, RING, D])

        ps = [ctx.enter_context(nc.psum_tensor(f"bank{i}", [P, 512], F32)) for i in range(8)]

        def vec(v, n=P):
            return v.rearrange("(p o) -> p o", o=1)

        SMALL = [(gw1[:], gate_w1), (rw[:], resp_w), (gb2[:], gate_b2.partition_broadcast(NS)),
                 (emb[:], subj_emb), (hw1[:], hyp_w1), (hw2[:], hyp_w2), (sw1[:], sty_w1), (sw2[:], sty_w2),
                 (rout[:], router_w), (biasrow[:, 0, :], resp_b.rearrange("(o d) -> o d", o=1)),
                 (biasrow[:, 1, :], safety_bias.rearrange("(o d) -> o d", o=1)),
                 (smp[:, 0:1], vec(score)), (smp[:, 1:2], vec(theta)), (smp[:, 2:3], vec(phi)),
                 (id1[:], ids1.partition_broadcast(SUBJ)), (id2[:], vec(ids2)),
                 (col[0:R, c_gb1:c_gb1 + 1], vec(gate_b1)), (col[0:R, c_gw2:c_gw2 + 1], gate_w2.rearrange("o r -> r o")),
                 (col[:, c_lng:c_lng + 1], vec(ln_g)), (col[:, c_lnb:c_lnb + 1], vec(ln_b)),
                 (col[:, c_hb1:c_hb1 + 1], vec(hyp_b1)), (col[:, c_hb2:c_hb2 + 1], vec(hyp_b2)),
                 (col[0:SH // 2, c_sb1:c_sb1 + 1], vec(sty_b1)),
                 (col[:, c_sg:c_sg + 1], vec(sty_b2[0:D])), (col[:, c_sbt:c_sbt + 1], vec(sty_b2[D:2 * D]))]
        ROWS = [(brow[:, 0, :], exp_b1), (brow[:, 1, :], bi), (bor[:], bo.rearrange("(o e) d -> o e d", o=1)),
                (g2r[:], gamma2.partition_broadcast(P)), (be2r[:], beta2.partition_broadcast(P))]
        IOTAS = [(pidx[:], [[0, 1]], 0, 1), (pidxi[:], [[0, 1]], 0, 1), (io128[:], [[1, P]], 0, 0),
                 (down8[:], [[0, TILES], [-1, E]], E, 0),
                 (iob[:], [[1, NB1]], 0, 0), (iob16[:], [[1, NB1]], 0, 0), (bstep[:], [[P, TILES]], 0, 0), (sstep[:], [[SPT, TILES]], 0, 0),
                 (qio[:], [[1, SPT], [0, T]], 0, 0), (io88[:], [[1, SPT], [SPT, NB2]], 0, 0),
                 (tokv[:], [[0, T]], 0, T), (sback[:], [[0, 1]], -NS, 1)]
        GS_MASKS, GS_A2, GS_ANGLES, GS_RANK2, GS_MAP2 = 12, 14, 15, 23, 28
        GS_BUSY, LOGIT_BUSY, STYLE_BUSY, GATHER_BUSY = 5, 11, 1, 12
        GS_SIDE = 3
        GS_RESP, GS_LONG = (26, 28, 29, 30), (GS_MASKS, GS_RANK2, GS_RANK2 + 1, GS_RANK2 + 2, GS_MAP2)
        SHARED = 4
        FIRST2 = NB1 - NB2 - 2
        RESP_BANK = (1, 2, 5, 6)
        POOL_OH = 6
        N_SMALL, N_ROWS, N_CONST, N_SIDE = len(SMALL), len(ROWS), 17 + len(IOTAS), TILES + 6

        (ld_uv, ld_x, ld_small, ld_w2, ld_wo, ld_rows, consts, act_own, dve_own, gs_dots, gs_root, gs_norm,
         q_ready, xt_ps, xt_sb, pooled_ps, sid_ready, side_ps, side_sb, crow_ready, fold_ps, fold_sb,
         style_exp, z_exp, str_in, str_ps, resp_ps, x1_ready, var_ready, std_ready, nmr_ready, h0A_ready, h0B_ready,
         h0T_ps, hT_raw, tmean_ready, centred_even, centred_odd, sq_ready, tvar_ready, tstd_ready, h_scaled, h_ready, last_ready, logit_ps, hrow_ps,
         hrow_sb, h_stored, logit_shift, logit_exp, onehots, rank_ps, places, eqb_ready, tok_ready, tile_ready, ohp_pool, slp_ready, map_in,
         map_ps, map_ready, a2_ready, rank2_ps, oh88_ready, map2_ps, map2_ready, ang_ready, trig_ready,
         trigt_ready, trig_ps, x_row_ready, bexp_ready, bias_ps, bias_ready, x_stored, row_T_ps, row_T_sb,
         up_ps, hidA_sb, hidB_sb, down_ps, es_ready, x2_ready, xT2_ps, xT2_sb, up2_ps, hid2_sb, down2_ps,
         ve2_ready, rs2_ready, yn_ready, yo_ready, c_x2a, b_rr, b_stats, b_aggr, n_yg, n_yb, n_rot) = map(sem, """
         ld_uv ld_x ld_small ld_w2 ld_wo ld_rows consts act_own dve_own gs_dots gs_root gs_norm q_ready
         xt_ps xt_sb pooled_ps sid_ready side_ps side_sb crow_ready fold_ps fold_sb style_exp z_exp
         str_in str_ps resp_ps x1_ready var_ready std_ready nmr_ready h0A_ready h0B_ready h0T_ps hT_raw tmean_ready centred_even centred_odd
         sq_ready tvar_ready tstd_ready h_scaled h_ready last_ready logit_ps hrow_ps hrow_sb h_stored logit_shift logit_exp
         onehots rank_ps places eqb_ready tok_ready tile_ready ohp_pool slp_ready map_in map_ps map_ready a2_ready rank2_ps oh88_ready
         map2_ps map2_ready ang_ready trig_ready trigt_ready trig_ps x_row_ready bexp_ready bias_ps bias_ready
         x_stored row_T_ps row_T_sb up_ps hidA_sb hidB_sb down_ps es_ready x2_ready xT2_ps
         xT2_sb up2_ps hid2_sb down2_ps ve2_ready rs2_ready yn_ready yo_ready c_x2a b_rr b_stats b_aggr n_yg n_yb n_rot""".split())
        gs_step = [sem(f"gs_step_{m}") for m in "UV"]
        hg_ready = [sem(f"hg_ready{i}") for i in range(RING)]
        es_stored = [sem(f"es_stored{i}") for i in range(2)]
        xg_ready = [sem(f"xg_ready{i}") for i in range(2)]
        eg_ready = [sem(f"eg_ready{i}") for i in range(RING)]
        w1_ready = [sem(f"w1_ready{i}") for i in range(RING)]
        b2_ready = [sem(f"b2_ready{i}") for i in range(RING)]
        wi_ready = [sem(f"wi_ready{i}") for i in range(RING)]
        yo_stored = [sem(f"yo_stored{i}") for i in range(RING)]

        block = ctx.enter_context(nc.Block())

        def blocks(n, step):
            for j in range(n):
                step(j, j % RING)

        def g128(t, g):
            return t[:, g * GT:(g + 1) * GT]

        def up_weights2(e):
            return Wi[bass.ds(e, 1), :, :].rearrange("e d f -> (e d) f")

        def samples_out(eng, name, j, r, places_):
            _, samples = nc.values_load_multi_w_load_instructions(
                samp[0:1, SPT * j + places_[0]:SPT * j + places_[-1] + 1], engines=[name])
            eng.wait_ge(yo_ready, j + 1)
            for sample, q in zip(samples, places_):
                eng.dma_start(out[bass.ds(sample, 1), :, :].rearrange("s t d -> (s t) d"),
                              yo[q * T:(q + 1) * T, r, :], bounds_check="skip_entire_dma").then_inc(yo_stored[r], 16)

        def over_tokens(g):
            return hT[:, g * GW:(g + 1) * GW].rearrange("p (s t) -> p s t", t=T), slice(g * SPG, (g + 1) * SPG)

        def spread(t, ss):
            return t[:, ss].unsqueeze(2).to_broadcast([P, SPG, T])

        @block.sync
        def _(sp):
            sp.dma_start(Q[:, 0, :], U).then_inc(ld_uv, 16)
            sp.dma_start(Q[:, 1, :], V).then_inc(ld_uv, 16)
            sp.dma_start(X, x.rearrange("(i s) t d -> (s t) i d", s=SPT)).then_inc(ld_x, 16)
            for dst, src in SMALL:
                sp.dma_start(dst, src).then_inc(ld_small, 16)
            sp.dma_start(w2[:], exp_w2.rearrange("e (c p) d -> p e c d", p=P)).then_inc(ld_w2, 16)
            for dst, src in ROWS:
                sp.dma_start(dst, src).then_inc(ld_rows, 16)
            sp.dma_start(wo[:], Wo.rearrange("e (c p) d -> p e c d", p=P)).then_inc(ld_wo, 16)
            sp.wait_ge(x1_ready, GROUPS)
            sp.dma_start(xdram[:, 0:D].rearrange("(i p) d -> p i d", p=P), x1r[:, :, 0:D]).then_inc(x_stored, 16)
            for g in range(GROUPS):
                sp.wait_ge(hrow_sb, g + 1)
                sp.dma_start(hdram[g * GW:(g + 1) * GW, :].rearrange("(i p) d -> p i d", p=P),
                             g128(hrow, g)).then_inc(h_stored, 16)
            def weights1(b, r):
                e = sp.value_load(bexi[0:1, b:b + 1], min_val=0, max_val=E - 1)
                if b >= RING:
                    sp.wait_ge(up_ps, b - RING + 1)
                sp.dma_start(ws[:, r, :], exp_w1[bass.ds(e, 1), :, :].rearrange("e d f -> (e d) f")).then_inc(w1_ready[r], 16)
                if b >= RING:
                    sp.wait_ge(es_ready, b - RING + 1)
                sp.dma_start(b2blk[:, r, :],
                             exp_b2[bass.ds(e, 1), :].rearrange("e d -> (e d)").partition_broadcast(P)).then_inc(b2_ready[r], 16)

            def store(b, r):
                sp.wait_ge(es_ready, b + 1)
                sp.dma_start(edram[b * P:(b + 1) * P, :], es[:, r % 2, :]).then_inc(es_stored[r % 2], 16)

            def step1(b, r):
                store(b, r)
                if b + RING < NB1:
                    weights1(b + RING, r)
            sp.wait_ge(places, 1)
            for b in range(RING):
                weights1(b, b)
            sp.wait_ge(x_row_ready, 1)
            sp.dma_start(xdram[:, D:XW].rearrange("(i p) d -> p i d", p=P), x1r[:, :, D:XW]).then_inc(x_stored, 16)
            blocks(NB1, step1)

            def out_of_block(j, r):
                samples_out(sp, mybir.EngineType.SP, j, r, range(SPT if j < NB2 - SHARED else SPT // 2))
            for j in range(RING):
                e = sp.value_load(bex2i[0:1, j:j + 1], min_val=0, max_val=E - 1)
                sp.wait_ge(up_ps, max(range(j, NB1, RING)) + 1)
                sp.dma_start(ws[:, j, :], up_weights2(e)).then_inc(wi_ready[j], 16)
            blocks(NB2, out_of_block)
            for u in range(RING):
                sp.wait_ge(yo_stored[u], 16 * SPT * len(range(u, NB2, RING)))

        @block.gpsimd
        def _(pool):
            count = [0]

            def const(ins):
                count[0] += 1
                ins.then_inc(consts, 1)
                pool.wait_ge(consts, count[0])

            const(pool.memset(gseps[:], EPS_GS))
            const(pool.memset(ones[:], 1.0))
            const(pool.memset(ident[:], 0.0))
            const(pool.affine_select(out=ident[:], in_=ident[:], compare_op=ALU.not_equal, fill=1.0, base=0,
                                     pattern=[[-1, P]], channel_multiplier=1))
            const(pool.memset(mean4[:], 1.0 / T))
            const(pool.affine_select(out=mean4[:], in_=mean4[:], compare_op=ALU.is_ge, fill=0.0, base=0,
                                     pattern=[[-T, SPT]], channel_multiplier=1))
            const(pool.affine_select(out=mean4[:], in_=mean4[:], compare_op=ALU.is_ge, fill=0.0, base=T - 1,
                                     pattern=[[T, SPT]], channel_multiplier=-1))
            const(pool.memset(tri[:], 1.0))
            const(pool.affine_select(out=tri[:], in_=tri[:], compare_op=ALU.is_gt, fill=0.0, base=0,
                                     pattern=[[1, P]], channel_multiplier=-1))
            const(pool.memset(onesrow[:], 1.0))
            const(pool.memset(tmask[:], 1.0))
            const(pool.affine_select(out=tmask[:], in_=tmask[:], compare_op=ALU.is_ge, fill=0.0, base=0,
                                     pattern=[[-SPT, TILES]], channel_multiplier=1))
            const(pool.affine_select(out=tmask[:], in_=tmask[:], compare_op=ALU.is_ge, fill=0.0, base=SPT - 1,
                                     pattern=[[SPT, TILES]], channel_multiplier=-1))
            const(pool.memset(mhalf[:], -0.5))
            const(pool.memset(ones8[:], 1.0))
            const(pool.memset(segm[:], 1.0))
            const(pool.memset(segm[:, :, 0:1], 0.0))
            for dst, pattern, base, mult in IOTAS:
                const(pool.iota(dst, pattern=pattern, base=base, channel_multiplier=mult,
                                allow_small_or_imprecise_dtypes=True))
            assert count[0] == N_CONST

            def centre(g):
                h, ss = over_tokens(g)
                pool.wait_ge(tmean_ready, g // 2 + 1)
                pool.tensor_tensor(h, h, spread(tmean, ss), ALU.subtract).then_inc(centred_even, 1)

            for g in range(GROUPS):
                pool.wait_ge(nmr_ready, g + 1)
                for t in range(g * GT + GT // 2, (g + 1) * GT):
                    last = pool.tensor_scalar(h0[:, t, :], x1r[:, t, 0:D], rstd[:, t:t + 1], nmr[:, t:t + 1], ALU.mult, ALU.add)
                last.then_inc(h0B_ready, 1)
            for g in range(0, GROUPS, 2):
                centre(g)
            for g in range(GROUPS - 1):
                h, ss = over_tokens(g)
                pool.wait_ge(h_scaled, g + 1)
                pool.tensor_tensor(h, h, spread(betaT, ss), ALU.add).then_inc(h_ready, 1)

            pool.wait_ge(slp_ready, 1)
            for n in range(POOL_OH):
                pool.tensor_scalar(ohp[:, n, :], io128[:], slp[:, n // 2, n % 2:n % 2 + 1], None, ALU.is_equal).then_inc(ohp_pool, 1)
            pool.wait_ge(eqb_ready, 1)
            pool.tensor_scalar(tokb[:, :, 1, :], eqb[:], pidx[:], 0.0, ALU.mult, ALU.add).then_inc(tok_ready, 1)

            pool.wait_ge(h_stored, 16 * GROUPS)
            pool.wait_ge(map_ready, 1)

            def power(i):
                two = slice(2 * i % RING, 2 * i % RING + 2)
                pool.wait_ge(ve2_ready, 2 * i + 2)
                if i >= RING // 2:
                    pool.wait_ge(yn_ready, 2 * i - RING + 2)
                pool.tensor_tensor(rs2[:, two], ve2[:, two], mhalf[:], ALU.pow).then_inc(rs2_ready, 2)

            def gather_x(j):
                if j == 0:
                    pool.wait_ge(x_stored, 32)
                    pool.wait_ge(map2_ready, 1)
                if j >= 2:
                    pool.wait_ge(xg_ready[j % 2], 16 * (j // 2))
                pool.indirect_dma_start(
                    out=xg[:, j, :], out_offset=None, in_=xdram,
                    in_offset=bass.IndirectOffsetOnAxis(ap=map2[:, j:j + 1], axis=0)).then_inc(xg_ready[j % 2], 16)

            for b in range(NB1):
                if b >= RING:
                    pool.wait_ge(row_T_ps, b - RING + 1)
                pool.indirect_dma_start(
                    out=hg[:, b % RING, :], out_offset=None, in_=hdram,
                    in_offset=bass.IndirectOffsetOnAxis(ap=map1[:, b:b + 1], axis=0)).then_inc(hg_ready[b % RING], 16)
                if b >= 8 and b % 2 == 0 and (b - 8) // 2 < NB2:
                    gather_x((b - 8) // 2)
            for j in range((NB1 - 8 + 1) // 2, NB2):
                gather_x(j)
            pool.wait_ge(es_stored[0], 16 * ((NB1 + 1) // 2))
            pool.wait_ge(es_stored[1], 16 * (NB1 // 2))
            pool.wait_ge(xg_ready[0], 16 * ((NB2 + 1) // 2))
            pool.wait_ge(xg_ready[1], 16 * (NB2 // 2))

            def gather_e(j):
                if j >= RING:
                    pool.wait_ge(eg_ready[j % RING], 32 * (j // RING))
                for k in range(2):
                    pool.indirect_dma_start(
                        out=eg[:, j, k, :], out_offset=None, in_=edram,
                        in_offset=bass.IndirectOffsetOnAxis(
                            ap=xg[:, j, C_SLOT + k:C_SLOT + k + 1].bitcast(I32), axis=0)).then_inc(eg_ready[j % RING], 16)

            for j in range(NB2):
                gather_e(j)
                if j >= 6 and j % 2 == 0:
                    power(j // 2 - 3)
            for i in range(NB2 // 2 - 3, NB2 // 2):
                power(i)

        @block.scalar
        def _(act):
            def token_std(g):
                ss = slice(g * SPG, (g + 1) * SPG)
                act.wait_ge(tvar_ready, g + 1)
                act.activation(trs[:, ss], tve[:, ss], ACT.Sqrt).then_inc(tstd_ready, 1)

            def square(g):
                cols = slice(g * GW, (g + 1) * GW)
                act.wait_ge(centred_odd if g % 2 else centred_even, g // 2 + 1)
                act.activation(sq[:, cols], hT[:, cols], ACT.Square).then_inc(sq_ready, 1)

            def layer_norm(g):
                act.wait_ge(nmr_ready, g + 1)
                for t in range(g * GT, g * GT + GT // 2):
                    last = act.activation(h0[:, t, :], x1r[:, t, 0:D], ACT.Identity, bias=nmr[:, t:t + 1],
                                          scale=rstd[:, t:t + 1])
                last.then_inc(h0A_ready, 1)

            def gain(g):
                act.wait_ge(h0T_ps, g + 1)
                act.activation(hT[:, g * GW:(g + 1) * GW], ps[(4, 7)[g % 2]][:], ACT.Identity,
                               bias=col[:, c_lnb:c_lnb + 1], scale=col[:, c_lng:c_lng + 1]).then_inc(hT_raw, 1)

            def side(n):
                if n < TILES:
                    act.wait_ge(xt_ps, n + 1)
                    act.activation(xT[:, n * P:(n + 1) * P], ps[1 + n % 2][:, 0:P], ACT.Copy).then_inc(xt_sb, 1)
                    return
                n -= TILES
                act.wait_ge(side_ps, n + 1)
                if n == 0:
                    act.wait_ge(pooled_ps, 1)
                    act.activation(gw1T[:], ps[6][:, 0:R], ACT.Copy)
                    act.activation(rwT[:], ps[6][0:R, P:2 * P], ACT.Copy)
                    last = act.activation(pooledT[:], ps[3][:, 0:NS], ACT.Copy)
                elif n == 1:
                    act.activation(h1T[:], ps[5][0:R, 0:NS], ACT.Relu, bias=col[0:R, c_gb1:c_gb1 + 1])
                    last = act.activation(seT[:], ps[5][0:SE, NS:2 * NS], ACT.Copy)
                elif n == 2:
                    act.activation(zs[:, 0:1], ps[6][0:NS, 0:1], ACT.Identity, bias=gb2[:])
                    act.activation(zs[:, 1:2], smp[:, 0:1], ACT.Copy)
                    last = act.activation(hypT[:], ps[6][:, NS:2 * NS], ACT.Relu, bias=col[:, c_hb1:c_hb1 + 1])
                elif n == 3:
                    last = act.activation(hyp2T[:], ps[5][:, 0:NS], ACT.Identity, bias=col[:, c_hb2:c_hb2 + 1])
                elif n == 4:
                    last = act.activation(styT[:], ps[6][0:SH // 2, 0:NS], ACT.Relu, bias=col[0:SH // 2, c_sb1:c_sb1 + 1])
                else:
                    act.activation(graw[:], ps[5][:, 0:NS], ACT.Identity, bias=col[:, c_sg:c_sg + 1])
                    act.activation(gabs[:], ps[5][:, 0:NS], ACT.Abs, bias=col[:, c_sg:c_sg + 1])
                    last = act.activation(betaT[:], ps[5][:, NS:2 * NS], ACT.Identity, bias=col[:, c_sbt:c_sbt + 1])
                last.then_inc(side_sb, 1)

            for i in range(R):
                for k in range(2):
                    act.wait_ge(gs_dots, 2 * i + k + 1)
                    last = act.activation(gsn[:, i % 2, k:k + 1], ps[4 * k][:, 0:1], ACT.Sqrt)
                last.then_inc(gs_root, 1)
                act.wait_ge(gs_root, i + 1)
                if i == 0:
                    act.wait_ge(consts, 1)
                act.activation(gsd2[:], gsn[:, i % 2, :], ACT.Square, bias=gseps[:]).then_inc(gs_norm, 1)
                if 0 <= i - GS_SIDE < N_SIDE:
                    if i == GS_SIDE + TILES:
                        act.wait_ge(ld_small, 16 * N_SMALL)
                    side(i - GS_SIDE)
            act.wait_ge(side_sb, N_SIDE - TILES)
            act.activation(zexp[:], zs[:], ACT.Exp, scale=-1.0).then_inc(z_exp, 1)
            act.activation(gexp[:], gabs[:], ACT.Exp, scale=-1.0).then_inc(act_own, 1)
            act.wait_ge(act_own, 1)
            act.activation(gln[:], gexp[:], ACT.Ln, bias=1.0).then_inc(style_exp, 1)
            for g in range(GROUPS):
                act.wait_ge(var_ready, g + 1)
                act.activation(g128(rs, g), g128(ve, g), ACT.Sqrt).then_inc(std_ready, 1)
                if g >= 1:
                    layer_norm(g - 1)
                if g >= 2:
                    gain(g - 2)
            layer_norm(GROUPS - 1)
            gain(GROUPS - 2)
            gain(GROUPS - 1)
            for g in range(GROUPS):
                square(g)
                if g:
                    token_std(g - 1)
            token_std(GROUPS - 1)
            act.wait_ge(logit_shift, 1)
            act.activation(rex[:], rsh[:], ACT.Exp).then_inc(logit_exp, 1)
            act.wait_ge(ang_ready, 1)
            act.activation(trig[:], angw[:], ACT.Sin).then_inc(trig_ready, 1)
            for g in range(GROUPS):
                act.wait_ge(hrow_ps, g + 1)
                act.activation(g128(hrow, g), ps[4 + g % 2][:].rearrange("p (i d) -> p i d", d=D),
                               ACT.Copy).then_inc(hrow_sb, 1)

            expert2 = []

            def hidden(b, r):
                u = r % 2
                act.wait_ge(up_ps, b + 1)
                if b >= 2:
                    act.wait_ge(down_ps, b - 1)
                for c in range(FC // 2):
                    last = act.activation(hid[:, u, c, :], ps[2 + u][:, c * P:(c + 1) * P], ACT.Relu,
                                          bias=bh1[:, c, b:b + 1])
                last.then_inc(hidA_sb, 1)
                if 0 <= b - FIRST2 < NB2 - RING:
                    expert2.append(act.value_load(bex2i[0:1, RING + b - FIRST2:RING + b - FIRST2 + 1], min_val=0, max_val=E - 1))
            act.wait_ge(eqb_ready, 1)
            for i in range(TILES):
                last = act.activation(tokb[:, 2 * i:2 * i + 2, 0, :], eqb[:, 2 * i:2 * i + 2, :], ACT.Copy, scale=float(i))
            last.then_inc(tile_ready, 1)
            act.wait_ge(bias_ps, 1)
            act.activation(bh1[:].rearrange("p c b -> p (c b)"), ps[6][:, 0:FC * NB1], ACT.Copy)
            act.activation(bh2[:].rearrange("p c b -> p (c b)"), ps[6][:, FC * NB1:FC * (NB1 + NB2)], ACT.Copy).then_inc(bias_ready, 1)
            act.wait_ge(bias_ready, 1)
            blocks(NB1, hidden)

            def columns2(j, r):
                act.wait_ge(xT2_ps, j + 1)
                act.activation(hgT[:, r % 2, :], ps[r % 2][:, 0:P], ACT.Copy).then_inc(xT2_sb, 1)

            def hidden2(j, r):
                u = r % 2
                act.wait_ge(up2_ps, j + 1)
                if j >= 2:
                    act.wait_ge(down2_ps, j - 1)
                for c in range(FC):
                    last = act.activation(hid[:, u, c, :], ps[2 + 2 * (c // 2) + u][:, c % 2 * P:(c % 2 + 1) * P], ACT.Gelu,
                                          bias=bh2[:, c, j:j + 1])
                last.then_inc(hid2_sb, 1)
                if j + RING < NB2:
                    act.dma_start(ws[:, r, :], up_weights2(expert2[j])).then_inc(wi_ready[r], 16)

            def norm2(n, rn):
                act.wait_ge(rs2_ready, n + 1)
                if n >= 2:
                    act.wait_ge(n_yb, n - 1)
                act.wait_ge(n_yg, n + 1)
                act.activation(yn[:, rn % 2, :], rr[:, rn, :], ACT.Copy, scale=rs2[:, rn:rn + 1]).then_inc(yn_ready, 1)

            def step2(j, r):
                if j >= NLAG:
                    norm2(j - NLAG, (r - NLAG) % RING)
                if j < NB2:
                    hidden2(j, r)
                if j + 2 < NB2:
                    columns2(j + 2, r + 2)
            act.wait_ge(down_ps, NB1)
            columns2(0, 0)
            columns2(1, 1)
            blocks(NB2 + NLAG, step2)
            for j in range(NB2 - SHARED, NB2):
                samples_out(act, mybir.EngineType.Activation, j, j % RING, range(SPT // 2, SPT))

        @block.tensor
        def _(pe):
            mm = pe.matmul

            def side(n):
                if n < TILES:
                    if n >= 2:
                        pe.wait_ge(xt_sb, n - 1)
                    pe.transpose(ps[1 + n % 2][:, 0:P], X[:, n, :], ident[:]).then_inc(xt_ps, 1)
                    m = mm(ps[3][:, n * SPT:(n + 1) * SPT], X[:, n, :], mean4[:], start=True, stop=True)
                    if n == TILES - 1:
                        m.then_inc(pooled_ps, 1)
                    return
                n -= TILES
                if n:
                    pe.wait_ge(side_sb, n)
                if n == 0:
                    pe.wait_ge(ld_small, 16 * N_SMALL)
                    pe.transpose(ps[6][:, 0:R], gw1[:], ident[0:R, 0:R])
                    last = pe.transpose(ps[6][0:R, P:2 * P], rw[:], ident[:])
                elif n == 1:
                    pe.wait_ge(sid_ready, 1)
                    mm(ps[5][0:R, 0:NS], gw1T[:], pooledT[:], start=True, stop=True)
                    last = mm(ps[5][0:SE, NS:2 * NS], emb[:], sid[:], start=True, stop=True)
                elif n == 2:
                    mm(ps[6][0:NS, 0:1], h1T[:], col[0:R, c_gw2:c_gw2 + 1], start=True, stop=True)
                    last = mm(ps[6][:, NS:2 * NS], hw1[:], seT[:], start=True, stop=True)
                elif n == 3:
                    last = mm(ps[5][:, 0:NS], hw2[:], hypT[:], start=True, stop=True)
                elif n == 4:
                    last = mm(ps[6][0:SH // 2, 0:NS], sw1[:], hyp2T[:], start=True, stop=True)
                else:
                    mm(ps[5][:, 0:NS], sw2[:, 0:D], styT[:], start=True, stop=True)
                    last = mm(ps[5][:, NS:2 * NS], sw2[:, D:2 * D], styT[:], start=True, stop=True)
                last.then_inc(side_ps, 1)

            def busy(n, bank=7):
                for _ in range(n):
                    mm(ps[bank][:], ones[:], ones[:].unsqueeze(1).to_broadcast([P, 4, P]), start=True, stop=True)

            pe.wait_ge(ld_uv, 32)
            for i in range(R):
                for k in range(2):
                    if i:
                        pe.wait_ge(gs_step[k], i)
                    mm(ps[4 * k][:, 0:R - i], Q[:, k, i:i + 1].to_broadcast([P, P]), Q[:, k, i:R],
                       start=True, stop=True).then_inc(gs_dots, 1)
                if 0 <= i - GS_SIDE < N_SIDE:
                    if i == GS_SIDE:
                        pe.wait_ge(consts, N_CONST)
                        pe.wait_ge(ld_x, 16)
                    side(i - GS_SIDE)
                if i == 1:
                    pe.wait_ge(consts, 2)
                if 0 < i < R - 1:
                    busy(GS_BUSY - 4 * (i in GS_RESP) + 3 * (i - 1 in GS_LONG))
                if i in GS_RESP:
                    if i == GS_RESP[0]:
                        pe.wait_ge(side_sb, N_SIDE - TILES)
                        pe.wait_ge(xt_sb, TILES)
                        pe.wait_ge(crow_ready, 1)
                    mm(ps[RESP_BANK[GS_RESP.index(i)]][:], onesrow[:], crow4[:].rearrange("o i d -> o (i d)"), start=True, stop=False)
                if i == GS_RANK2:
                    pe.wait_ge(a2_ready, 1)
                    mm(ps[3][0:NS, 0:E], tri[0:NS, 0:NS], a2[:], start=True, stop=True)
                    mm(ps[3][:, E:2 * E], ones[0:NS, :], a2[:], start=True, stop=True).then_inc(rank2_ps, 1)
                if i == GS_MAP2:
                    pe.wait_ge(oh88_ready, 1)
                    for q in range(SPT):
                        mm(ps[3][q * T:(q + 1) * T, NB2:2 * NB2], tokv[:], oh88[:, q, :], start=True, stop=True)
                    mm(ps[3][0:1, P:P + NB2 * SPT], sback[:], oh88[:].rearrange("s q b -> s b q"),
                       start=True, stop=True).then_inc(map2_ps, 1)
            pe.wait_ge(q_ready, 1)
            mm(ps[0][0:R, 0:R], Q[:, 1, :], Q[:, 1, :], start=True, stop=True)
            mm(ps[0][0:R, P:2 * P], Q[0:R, 0, :], rwT[:], start=True, stop=True)
            pe.transpose(ps[0][0:R, 2 * P:3 * P], Q[:, 0, :], ident[:]).then_inc(fold_ps, 1)
            pe.wait_ge(fold_sb, 1)
            mm(ps[4][0:R, 0:D], fold[:, 0, 0:R], fold[:, 1, :], start=True, stop=True).then_inc(fold_ps, 1)
            pe.wait_ge(fold_sb, 2)
            mm(ps[7][:, 0:D], fold[:, 2, :], fold[:, 3, :], start=True, stop=True).then_inc(fold_ps, 1)
            pe.wait_ge(str_in, 1)
            mm(ps[3][:, 0:TILES], smod[:].rearrange("s q t -> s (q t)"), strtile[:], start=True, stop=True).then_inc(str_ps, 1)
            pe.wait_ge(fold_sb, 3)
            for g in range(GROUPS):
                bank = ps[RESP_BANK[g]]
                for j in range(GT):
                    t = g * GT + j
                    last = mm(bank[:, j * D:(j + 1) * D], xT[:, t * P:(t + 1) * P], M[:], start=False, stop=(j == GT - 1))
                last.then_inc(resp_ps, 1)
            for g in range(GROUPS):
                pe.wait_ge(h0A_ready, g + 1)
                pe.wait_ge(h0B_ready, g + 1)
                if g >= 2:
                    pe.wait_ge(hT_raw, g - 1)
                for j in range(GT):
                    last = pe.transpose(ps[(4, 7)[g % 2]][:, j * P:(j + 1) * P], h0[:, g * GT + j, :], ident[:])
                last.then_inc(h0T_ps, 1)
            pe.wait_ge(tstd_ready, 1)
            busy(LOGIT_BUSY, 6)
            for g in range(GROUPS):
                busy(STYLE_BUSY, 6)
                if g < GROUPS - 1:
                    pe.wait_ge(h_ready, g + 1)
                else:
                    pe.wait_ge(last_ready, 1)
                for t in range(g * GT, (g + 1) * GT):
                    last = mm(ps[7][:, t * E:(t + 1) * E], hT[:, t * P:(t + 1) * P], rout[:], start=True, stop=True)
                last.then_inc(logit_ps, 1)
            for g in range(GROUPS):
                if g >= 2:
                    pe.wait_ge(hrow_sb, g - 1)
                for j in range(GT):
                    t = g * GT + j
                    last = pe.transpose(ps[4 + g % 2][:, j * D:(j + 1) * D], hT[:, t * P:(t + 1) * P], ident[:])
                last.then_inc(hrow_ps, 1)
            pe.wait_ge(onehots, 1)
            mm(ps[3][:, 0:P], tri[:], both[:].rearrange("p i e -> p (i e)"), start=True, stop=True)
            mm(ps[3][:, P:2 * P], ones[:], both[:].rearrange("p i e -> p (i e)"), start=True, stop=True).then_inc(rank_ps, 1)
            pe.wait_ge(ld_rows, 16 * N_ROWS)
            pe.wait_ge(bexp_ready, 1)
            for k, (oh, n) in enumerate(((bexp1, NB1), (bexp2, NB2))):
                for c in range(FC):
                    at = k * FC * NB1 + c * n
                    last = mm(ps[6][:, at:at + n], brow[:, k, c * P:(c + 1) * P], oh[:], start=True, stop=True)
            last.then_inc(bias_ps, 1)
            pe.wait_ge(tok_ready, 1)
            pe.wait_ge(tile_ready, 1)
            pe.wait_ge(ohp_pool, POOL_OH)
            for n in range(2 * TILES):
                if n >= POOL_OH:
                    pe.wait_ge(map_in, n - POOL_OH + 1)
                last = mm(ps[1][:, 0:2 * NB1], ohp[:, n, :], tokb[:, n, :, :].rearrange("p k b -> p (k b)"),
                          start=(n == 0), stop=(n == 2 * TILES - 1))
            last.then_inc(map_ps, 1)
            pe.wait_ge(trigt_ready, 1)
            mm(ps[3][:, 2 * P:3 * P], smod[:].rearrange("s q t -> s (q t)"), trigt[:].rearrange("s k i -> s (k i)"),
               start=True, stop=True).then_inc(trig_ps, 1)

            def rows_T(b, r):
                pe.wait_ge(hg_ready[r % RING], 16 * (b // RING + 1))
                if b >= 2:
                    pe.wait_ge(row_T_sb, b - 1)
                pe.transpose(ps[r % 2][:, 0:P], hg[:, r % RING, :], ident[:]).then_inc(row_T_ps, 1)

            def up_product(u, w):
                for c in range(FC):
                    last = mm(ps[2 + 2 * (c // 2) + u][:, c % 2 * P:(c % 2 + 1) * P], ws[:, w, c * P:(c + 1) * P],
                              hgT[:, u, :], start=True, stop=True)
                return last

            def up(b, r):
                pe.wait_ge(row_T_sb, b + 1)
                pe.wait_ge(w1_ready[r % RING], 16 * (b // RING + 1))
                if b >= 2:
                    pe.wait_ge(hidA_sb, b - 1)
                    pe.wait_ge(hidB_sb, b - 1)
                up_product(r % 2, r % RING).then_inc(up_ps, 1)

            def down(b, r):
                u = r % 2
                e = pe.value_load(bexi[0:1, b:b + 1], min_val=0, max_val=E - 1)
                pe.wait_ge(hidA_sb, b + 1)
                pe.wait_ge(hidB_sb, b + 1)
                if b >= 2:
                    pe.wait_ge(es_ready, b - 1)
                for c in range(FC):
                    last = mm(ps[6 + u][:, 0:D], hid[:, u, c, :], w2[:, bass.ds(e, 1), c, :], start=(c == 0), stop=(c == FC - 1))
                last.then_inc(down_ps, 1)

            def step1(b, r):
                if b + 2 < NB1:
                    rows_T(b + 2, r + 2)
                if b + 1 < NB1:
                    up(b + 1, r + 1)
                down(b, r)

            pe.wait_ge(ld_w2, 16)
            busy(GATHER_BUSY)
            rows_T(0, 0)
            rows_T(1, 1)
            up(0, 0)
            blocks(NB1, step1)

            def rows_T2(j, r):
                pe.wait_ge(x2_ready, j + 1)
                if j >= 2:
                    pe.wait_ge(xT2_sb, j - 1)
                pe.transpose(ps[r % 2][:, 0:P], x2[:, r % RING, :], ident[:]).then_inc(xT2_ps, 1)

            def up2(j, r):
                pe.wait_ge(xT2_sb, j + 1)
                pe.wait_ge(wi_ready[r % RING], 16 * (j // RING + 1))
                if j >= 2:
                    pe.wait_ge(hid2_sb, j - 1)
                up_product(r % 2, r % RING).then_inc(up2_ps, 1)

            def down2(j, r):
                u = r % 2
                e = pe.value_load(bex2i[0:1, j:j + 1], min_val=0, max_val=E - 1)
                if j >= 2:
                    pe.wait_ge(b_rr, j - 1)
                mm(ps[6 + u][:, 0:D], onesrow[:], bor[:, bass.ds(e, 1), :], start=True, stop=False)
                pe.wait_ge(hid2_sb, j + 1)
                for c in range(FC):
                    last = mm(ps[6 + u][:, 0:D], hid[:, u, c, :], wo[:, bass.ds(e, 1), c, :], start=False, stop=(c == FC - 1))
                last.then_inc(down2_ps, 1)

            def step2(j, r):
                if j + 2 < NB2:
                    rows_T2(j + 2, r + 2)
                if j + 1 < NB2:
                    up2(j + 1, r + 1)
                down2(j, r)

            pe.wait_ge(ld_wo, 16)
            pe.wait_ge(es_ready, NB1)
            rows_T2(0, 0)
            rows_T2(1, 1)
            up2(0, 0)
            blocks(NB2, step2)

        @block.vector
        def _(dve):
            count = [0]

            def link(ins):
                count[0] += 1
                ins.then_inc(dve_own, 1)
                dve.wait_ge(dve_own, count[0])

            def masks():
                dve.wait_ge(consts, N_CONST)
                dve.wait_ge(ld_small, 16 * N_SMALL)
                link(dve.tensor_scalar(smodi[:], pidxi[0:NS, :], SPT - 1, None, ALU.bitwise_and))
                link(dve.tensor_scalar(pmodi[:], pidxi[:], T - 1, None, ALU.bitwise_and))
                link(dve.tensor_copy(smodf[:], smodi[:]))
                link(dve.tensor_copy(pmod[:], pmodi[:]))
                link(dve.tensor_scalar(smod[:], qio[:], smodf[:], None, ALU.is_equal))
                link(dve.tensor_copy(idf[:], id1[:]))
                dve.tensor_scalar(sid[:], idf[:], pidx[0:SUBJ, :], None, ALU.is_equal).then_inc(sid_ready, 1)
                link(dve.tensor_add(crow[:], biasrow[:, 0, :], biasrow[:, 1, :]))
                dve.tensor_copy(crow4[:], crow[:].unsqueeze(1).to_broadcast([1, GT, D])).then_inc(crow_ready, 1)

            def blocks_of(counts, steps, cmp, n, upto, before):
                link(dve.tensor_tensor(cmp[:], counts.unsqueeze(2).to_broadcast([P, E, TILES]),
                                       steps[:].unsqueeze(1).to_broadcast([P, E, TILES]), ALU.is_gt))
                link(dve.tensor_reduce(n[:], cmp[:], AX.X, ALU.add))
                link(dve.tensor_tensor_scan(upto[:], ones8[:], n[:], 0.0, ALU.mult, ALU.add))
                link(dve.tensor_tensor(before[:], upto[:], n[:], ALU.subtract))

            def expert_of_block(cmp, upto, asfloat, asint, n):
                link(dve.tensor_tensor(cmp[:], iob[:, 0:n].unsqueeze(2).to_broadcast([P, n, E]),
                                       upto[:].unsqueeze(1).to_broadcast([P, n, E]), ALU.is_ge))
                link(dve.tensor_reduce(asfloat[:], cmp[:], AX.X, ALU.add))
                return dve.tensor_scalar_min(asint[:], asfloat[:], float(E - 1))

            two = slice(0, 2)

            def turns():
                link(dve.tensor_scalar(angk[:, two], smp[:, 1:3], 1.0 / (2 * PI), ROUND, ALU.mult, ALU.add))
                link(dve.tensor_scalar_add(angk[:, two], angk[:, two], -ROUND))
                link(dve.scalar_tensor_tensor(ang[:, two], angk[:, two], -PI2_HI, smp[:, 1:3], ALU.mult, ALU.add))

            def reduced():
                link(dve.scalar_tensor_tensor(angr[:, two], angk[:, two], -PI2_LO, ang[:, two], ALU.mult, ALU.add))
                link(dve.tensor_scalar_add(angr[:, 2:4], angr[:, two], PI / 2))
                link(dve.tensor_scalar(angk[:], angr[:], PI, -2 * PI, ALU.is_gt, ALU.mult))

            def clamped():
                link(dve.tensor_tensor(ang[:], angr[:], angk[:], ALU.add))
                dve.tensor_scalar(angw[:], ang[:], 3.1415925, -3.1415925, ALU.min, ALU.max).then_inc(ang_ready, 1)

            ANGLES = [turns, reduced, clamped]

            dve.wait_ge(ld_uv, 32)
            for i in range(R):
                dve.wait_ge(gs_norm, i + 1)
                link(dve.reciprocal(gsr[:], gsd2[:]))
                link(dve.tensor_tensor(gss[:], Q[:, :, i], gsr[:], ALU.mult))
                if i < R - 1:
                    for k in range(2):
                        dve.scalar_tensor_tensor(Q[:, k, i + 1:R], ps[4 * k][:, 1:R - i], gss[:, k:k + 1],
                                                 Q[:, k, i + 1:R], ALU.mult, ALU.subtract, reverse1=True).then_inc(gs_step[k], 1)
                link(dve.tensor_scalar_add(gsd[:], gsn[:, i % 2, :], EPS_GS))
                q = dve.tensor_tensor(Q[:, :, i], gss[:], gsd[:], ALU.mult)
                if i == R - 1:
                    q.then_inc(q_ready, 1)
                    break
                if i == GS_MASKS:
                    masks()
                elif i == GS_A2:
                    link(dve.tensor_copy(id2f[:], id2[:]))
                    link(dve.tensor_scalar(a2f[:], iob[0:NS, 0:E], id2f[:], None, ALU.is_equal))
                    dve.tensor_copy(a2[:], a2f[:]).then_inc(a2_ready, 1)
                elif GS_ANGLES <= i < GS_ANGLES + len(ANGLES):
                    ANGLES[i - GS_ANGLES]()
                elif i == GS_RANK2:
                    dve.wait_ge(rank2_ps, 1)
                    link(dve.tensor_copy(cnt2[:], ps[3][:, E:2 * E]))
                    blocks_of(cnt2[:], sstep, cmp2, nb2, cb2, cbe2)
                elif i == GS_RANK2 + 1:
                    link(expert_of_block(cmpb2, cb2, bex2f, bex2i, NB2))
                    link(dve.scalar_tensor_tensor(slot2e[:], cbe2[0:NS, :], float(SPT), ps[3][0:NS, 0:E], ALU.mult, ALU.add))
                elif i == GS_RANK2 + 2:
                    link(dve.tensor_tensor(a2f[:], a2f[:], slot2e[:], ALU.mult))
                    link(dve.tensor_reduce(slot2[:], a2f[:], AX.X, ALU.add))
                    dve.tensor_scalar(oh88[:], io88[:], slot2[:], None, ALU.is_equal).then_inc(oh88_ready, 1)
                elif i == GS_MAP2:
                    dve.wait_ge(map2_ps, 1)
                    dve.tensor_scalar(samp[:], ps[3][0:1, P:P + NB2 * SPT], float(NS), None, ALU.add)
                    dve.tensor_scalar(map2[:], ps[3][:, NB2:2 * NB2], pmod[:], None, ALU.add).then_inc(map2_ready, 1)

            dve.wait_ge(fold_ps, 1)
            dve.tensor_copy(fold[:, 0, 0:R], ps[0][0:R, 0:R])
            dve.tensor_copy(fold[:, 1:3, :], ps[0][0:R, P:3 * P].rearrange("p (k d) -> p k d", d=D)).then_inc(fold_sb, 1)
            dve.wait_ge(z_exp, 1)
            link(dve.tensor_scalar_add(zden[:], zexp[:], 1.0))
            link(dve.reciprocal(zsig[:], zden[:]))
            link(dve.tensor_tensor(stren[:], zsig[:, 0:1], zsig[:, 1:2], ALU.mult))
            dve.tensor_scalar(strtile[:], tmask[:], stren[:], None, ALU.mult).then_inc(str_in, 1)
            dve.wait_ge(fold_ps, 2)
            dve.tensor_copy(fold[:, 3, :], ps[4][0:R, 0:D]).then_inc(fold_sb, 1)
            dve.wait_ge(fold_ps, 3)
            dve.tensor_copy(M[:], ps[7][:, 0:D]).then_inc(fold_sb, 1)
            dve.wait_ge(str_ps, 1)
            link(dve.tensor_copy(strT[:], ps[3][:, 0:TILES]))
            dve.wait_ge(style_exp, 1)
            link(dve.tensor_scalar_max(gpos[:], graw[:], 0.0))
            link(dve.scalar_tensor_tensor(gammaT[:], gpos[:], EPS_SP, gln[:], ALU.add, ALU.add))

            def x1_of(g):
                dve.wait_ge(resp_ps, g + 1)
                for j in range(GT):
                    t = g * GT + j
                    last = dve.scalar_tensor_tensor(x1r[:, t, 0:D], ps[RESP_BANK[g]][:, j * D:(j + 1) * D], strT[:, t:t + 1],
                                                    X[:, t, :], ALU.mult, ALU.add)
                last.then_inc(x1_ready, 1)
                dve.wait_ge(x1_ready, g + 1)
                for t in range(g * GT, (g + 1) * GT):
                    last = dve.bn_stats(bst[:, t, :], x1r[:, t, 0:D])
                link(last)
                for t in range(g * GT, (g + 1) * GT):
                    last = dve.bn_aggr(mv[:, t, :], bst[:, t, :])
                link(last)
                dve.tensor_scalar_add(g128(ve, g), g128(mv, g)[:, :, 1], EPS_LN).then_inc(var_ready, 1)

            def shift_of(g):
                dve.wait_ge(std_ready, g + 1)
                link(dve.reciprocal(g128(rstd, g), g128(rs, g)))
                dve.scalar_tensor_tensor(g128(nmr, g), g128(mv, g)[:, :, 0], -1.0, g128(rstd, g), ALU.mult,
                                         ALU.mult).then_inc(nmr_ready, 1)

            for g in range(GROUPS):
                x1_of(g)
                if g:
                    shift_of(g - 1)
            shift_of(GROUPS - 1)

            for g in range(GROUPS):
                h, ss = over_tokens(g)
                dve.wait_ge(hT_raw, g + 1)
                link(dve.tensor_reduce(tsum[:, ss], h, AX.X, ALU.add))
                if g % 2 == 0:
                    dve.tensor_scalar_mul(tmean[:, ss], tsum[:, ss], 1.0 / T).then_inc(tmean_ready, 1)
                else:
                    dve.scalar_tensor_tensor(h, spread(tsum, ss), -1.0 / T, h, ALU.mult, ALU.add).then_inc(centred_odd, 1)
            for g in range(GROUPS):
                h, ss = over_tokens(g)
                dve.wait_ge(sq_ready, g + 1)
                link(dve.tensor_reduce(tvar[:, ss], sq[:, g * GW:(g + 1) * GW].rearrange("p (s t) -> p s t", t=T),
                                       AX.X, ALU.add))
                dve.tensor_scalar(tve[:, ss], tvar[:, ss], 1.0 / T, EPS_T, ALU.mult, ALU.add).then_inc(tvar_ready, 1)
            for g in range(GROUPS):
                h, ss = over_tokens(g)
                dve.wait_ge(tstd_ready, g + 1)
                link(dve.reciprocal(trr[:, ss], trs[:, ss]))
                link(dve.tensor_tensor(tsc[:, ss], trr[:, ss], gammaT[:, ss], ALU.mult))
                dve.tensor_tensor(h, h, spread(tsc, ss), ALU.mult).then_inc(h_scaled, 1)
            dve.wait_ge(h_scaled, GROUPS)
            dve.tensor_tensor(h, h, spread(betaT, ss), ALU.add).then_inc(last_ready, 1)

            def wide(t):
                return t[:].unsqueeze(2).to_broadcast([P, TILES, E])

            dve.wait_ge(logit_ps, GROUPS)
            logits = ps[7][:, 0:P].rearrange("p (i e) -> p i e", e=E)
            link(dve.tensor_reduce(rmx[:], logits, AX.X, ALU.max))
            dve.tensor_tensor(rsh[:], logits, wide(rmx), ALU.subtract).then_inc(logit_shift, 1)
            dve.wait_ge(logit_exp, 1)
            link(dve.tensor_reduce(rsum[:], rex[:], AX.X, ALU.add))
            link(dve.reciprocal(rrec[:], rsum[:]))
            link(dve.tensor_tensor(rp[:], rex[:], wide(rrec), ALU.mult))
            for probs, m, mm, o in ((rp, m1, mm1, o1), (rp2, m2, mm2, o2)):
                link(dve.tensor_reduce(m[:], probs[:], AX.X, ALU.max))
                link(dve.tensor_tensor(req[:], probs[:], wide(m), ALU.is_equal))
                link(dve.tensor_tensor(rwt[:], req[:], down8[:], ALU.mult))
                link(dve.tensor_reduce(mm[:], rwt[:], AX.X, ALU.max))
                link(dve.tensor_tensor(o[:], rwt[:], wide(mm), ALU.is_equal))
                if o is o1:
                    link(dve.scalar_tensor_tensor(rp2[:], o1[:], -2.0, rp[:], ALU.mult, ALU.add))
            dve.tensor_tensor(both[:], o1[:], o2[:], ALU.add).then_inc(onehots, 1)
            link(dve.tensor_tensor(gsum[:], m1[:], m2[:], ALU.add))
            link(dve.reciprocal(grec[:], gsum[:]))
            dve.tensor_tensor(x1r[:, :, C_GATE], m1[:], grec[:], ALU.mult)
            dve.tensor_tensor(x1r[:, :, C_GATE + 1], m2[:], grec[:], ALU.mult)

            dve.wait_ge(rank_ps, 1)
            link(dve.tensor_copy(tot[:], ps[3][:, P:2 * P].rearrange("p (i e) -> p e i", e=E)))
            flat = lambda t: t[:].rearrange("p e i -> p (e i)")
            link(dve.tensor_tensor_scan(flat(incl), flat(segm), flat(tot), 0.0, ALU.mult, ALU.add))

            blocks_of(incl[:, :, TILES - 1], bstep, cmp8, nb, cb, cbe)
            expert_of_block(cmpb, cb, bexf, bexi, NB1).then_inc(places, 1)
            for oh, of in ((bexp1, bexf), (bexp2, bex2f)):
                last = dve.tensor_scalar(oh[:], of[0:E, :], pidx[0:E, :], None, ALU.is_equal)
            last.then_inc(bexp_ready, 1)
            link(dve.tensor_tensor(texc[:], incl[:], tot[:], ALU.subtract))
            link(dve.scalar_tensor_tensor(tbase[:], cbe[:].unsqueeze(2).to_broadcast([P, E, TILES]), float(P), texc[:],
                                          ALU.mult, ALU.add))
            link(dve.tensor_tensor(slots[:], ps[3][:, 0:P].rearrange("p (i e) -> p i e", e=E),
                                   tbase[:].rearrange("p e i -> p i e"), ALU.add))
            for k, o in enumerate((o1, o2)):
                link(dve.tensor_tensor(pick[:], o[:], slots[:], ALU.mult))
                link(dve.tensor_reduce(slotf[:, :, k], pick[:], AX.X, ALU.add))
            link(dve.tensor_copy(sloti[:], slotf[:]))
            dve.tensor_copy(x1r[:, :, C_SLOT:C_SLOT + 2].bitcast(I32), sloti[:])
            dve.tensor_scalar(slpi[:], sloti[:], P - 1, None, ALU.bitwise_and)
            link(dve.tensor_scalar(slbi[:], sloti[:], 7, None, ALU.logical_shift_right))
            dve.tensor_copy(slp[:], slpi[:]).then_inc(slp_ready, 1)
            link(dve.tensor_copy(slb[:], slbi[:]))
            dve.tensor_tensor(eqb[:], iob16[:].unsqueeze(1).to_broadcast([P, 2 * TILES, NB1]),
                              slb[:].rearrange("p i k -> p (i k)").unsqueeze(2).to_broadcast([P, 2 * TILES, NB1]),
                              ALU.is_equal).then_inc(eqb_ready, 1)
            for n in range(POOL_OH, 2 * TILES):
                dve.tensor_scalar(ohp[:, n, :], io128[:], slp[:, n // 2, n % 2:n % 2 + 1], None, ALU.is_equal).then_inc(map_in, 1)
            dve.wait_ge(trig_ready, 1)
            for k in range(4):
                dve.tensor_copy(trig8[:, k:k + 1], trig[:, 2 + k // 2:3 + k // 2])
                last = dve.tensor_scalar_mul(trig8[:, 4 + k:5 + k], trig[:, k // 2:k // 2 + 1], -1.0 if k % 2 else 1.0)
            link(last)
            dve.tensor_tensor(trigt[:], trig8[:].unsqueeze(2).to_broadcast([NS, 8, TILES]),
                              tmask[:].unsqueeze(1).to_broadcast([NS, 8, TILES]), ALU.mult).then_inc(trigt_ready, 1)
            dve.wait_ge(map_ps, 1)
            link(dve.tensor_copy(hilo[:], ps[1][:, 0:2 * NB1].rearrange("p (k b) -> p k b", k=2)))
            dve.scalar_tensor_tensor(map1[:], hilo[:, 0, :], float(P), hilo[:, 1, :], ALU.mult, ALU.add).then_inc(map_ready, 1)
            dve.wait_ge(trig_ps, 1)
            dve.tensor_copy(x1r[:, :, C_COS:C_COS + 8],
                            ps[3][:, 2 * P:3 * P].rearrange("p (k i) -> p i k", i=TILES)).then_inc(x_row_ready, 1)

            def expert(table, b):
                return dve.value_load(table[0:1, b:b + 1], min_val=0, max_val=E - 1)

            def columns(b, r):
                dve.wait_ge(row_T_ps, b + 1)
                if b >= 2:
                    dve.wait_ge(up_ps, b - 1)
                dve.tensor_copy(hgT[:, r % 2, :], ps[r % 2][:, 0:P]).then_inc(row_T_sb, 1)

            def hidden(b, r):
                u = r % 2
                dve.wait_ge(up_ps, b + 1)
                if b >= 2:
                    dve.wait_ge(down_ps, b - 1)
                for c in range(FC // 2, FC):
                    last = dve.tensor_scalar(hid[:, u, c, :], ps[4 + u][:, (c - FC // 2) * P:(c - FC // 2 + 1) * P],
                                             bh1[:, c, b:b + 1], 0.0, ALU.add, ALU.max)
                last.then_inc(hidB_sb, 1)

            def rows_out(b, r):
                u = r % 2
                dve.wait_ge(down_ps, b + 1)
                dve.wait_ge(b2_ready[r % RING], 16 * (b // RING + 1))
                if b >= 2:
                    dve.wait_ge(es_stored[u], 16 * (b // 2))
                dve.tensor_tensor(es[:, u, :], ps[6 + u][:, 0:D], b2blk[:, r % RING, :], ALU.add).then_inc(es_ready, 1)

            def row_of(t, e):
                return t[:, bass.ds(e, 1), :].rearrange("p o d -> p (o d)")

            expert2 = []

            def step1(b, r):
                if b + 2 < NB1:
                    columns(b + 2, r + 2)
                if b + 1 < NB1:
                    hidden(b + 1, r + 1)
                rows_out(b, r)
                if 0 <= b - FIRST2 < NB2:
                    expert2.append(expert(bex2i, b - FIRST2))

            dve.wait_ge(bias_ready, 1)
            columns(0, 0)
            columns(1, 1)
            hidden(0, 0)
            blocks(NB1, step1)

            dve.wait_ge(ld_rows, 16 * N_ROWS)
            def of_block(j, a, b):
                return xg[:, j, a:b]

            def wait2(s_, j):
                dve.wait_ge(s_, j + 1)

            def step2(j, r):
                comb = j + LAG < NB2
                meas = 0 <= j < NB2
                norm = j >= LAG
                c, rc, n, rn = j + LAG, (r + LAG) % RING, j - LAG, (r - LAG) % RING
                if comb:
                    if c >= 1:
                        dve.wait_ge(x2_ready, c)
                    dve.wait_ge(eg_ready[rc], 32 * (c // RING + 1))
                    dve.scalar_tensor_tensor(x2a[:], one(eg, c, 0), of_block(c, C_GATE, C_GATE + 1), of_block(c, 0, D),
                                             ALU.mult, ALU.add).then_inc(c_x2a, 1)
                if comb:
                    wait2(c_x2a, c)
                    dve.scalar_tensor_tensor(x2[:, rc, :], one(eg, c, 1), of_block(c, C_GATE + 1, C_GATE + 2), x2a[:],
                                             ALU.mult, ALU.add).then_inc(x2_ready, 1)
                if 0 <= j - 1 < NB2:
                    rp = (r - 1) % RING
                    dve.scalar_tensor_tensor(rr[:, rp, :], rr[:, rp, :], mv2[:, rp, 0:1], row_of(g2r, expert2[j - 1]),
                                             ALU.subtract, ALU.mult).then_inc(n_yg, 1)
                if meas:
                    wait2(down2_ps, j)
                    wait2(x2_ready, j)
                    dve.tensor_tensor(rr[:, r, :], ps[6 + r % 2][:, 0:D], x2[:, r, :], ALU.add).then_inc(b_rr, 1)
                if norm:
                    wait2(yn_ready, n)
                    dve.tensor_tensor(yb[:], yn[:, rn % 2, :], row_of(be2r, expert2[n]), ALU.add).then_inc(n_yb, 1)
                if meas:
                    wait2(b_rr, j)
                    dve.bn_stats(st2[:], rr[:, r, :]).then_inc(b_stats, 1)
                if norm:
                    wait2(n_yb, n)
                    y4 = yb[:].rearrange("p (a c) -> p a c", c=4)
                    s4 = ysn[:].rearrange("p (a c) -> p a c", c=4)
                    cos = xg[:, n:n + 1, C_COS:C_COS + 4].to_broadcast([P, D // 4, 4])
                    sin = xg[:, n:n + 1, C_SIN:C_SIN + 4].to_broadcast([P, D // 4, 4])
                    dve.tensor_tensor(yc[:].rearrange("p (a c) -> p a c", c=4), y4, cos, ALU.mult)
                if norm:
                    for k in range(2):
                        if meas and k == 1:
                            wait2(b_stats, j)
                        last = dve.tensor_tensor(s4[:, :, k::2], y4[:, :, 1 - k::2], sin[:, :, k::2], ALU.mult)
                    last.then_inc(n_rot, 1)
                elif meas:
                    wait2(b_stats, j)
                if meas:
                    dve.bn_aggr(mv2[:, r, :], st2[:]).then_inc(b_aggr, 1)
                if norm:
                    wait2(n_rot, n)
                    if n >= RING:
                        dve.wait_ge(yo_stored[rn], 16 * SPT * (n // RING))
                    dve.tensor_tensor(yo[:, rn, :], yc[:], ysn[:], ALU.add).then_inc(yo_ready, 1)
                if meas:
                    wait2(b_aggr, j)
                    dve.tensor_scalar_add(ve2[:, r:r + 1], mv2[:, r, 1:2], EPS_L2).then_inc(ve2_ready, 1)

            def one(t, j, k):
                return t[:, j, k, :]

            for j in range(-LAG, 0):
                step2(j, j % RING)
            blocks(NB2 + LAG, step2)


_INS = ["x", "condB_safetyscore", "itok_B_6_14", "itok_B_0_7", "condB_theta", "condB_phi"] + [
    f"L0_cond_{n}" for n in ("U", "V", "safety_bias", "gate_w1", "gate_b1", "gate_w2", "gate_b2", "resp_w", "resp_b")] + [
    f"L1_cond_{n}" for n in ("ln_g", "ln_b", "subj_emb", "hyp_w1", "hyp_b1", "hyp_w2", "hyp_b2", "sty_w1", "sty_b1",
                             "sty_w2", "sty_b2", "router_w", "exp_w1", "exp_b1", "exp_w2", "exp_b2")] + [
    f"L2_cond_{n}" for n in ("Wi", "bi", "Wo", "bo", "gamma", "beta")]
_OUTS = [((NS, T, D), "float32")]


def kernel(**inputs):
    import numpy as _np
    import concourse.bacc as _bacc
    from concourse import mybir as _mybir
    from concourse.bass_utils import run_bass_kernel_spmd as _run

    nc = _bacc.Bacc("TRN2", target_bir_lowering=False, num_devices=1)
    arrays, args = {}, []
    for name in _INS:
        a = _np.ascontiguousarray(inputs[name])
        arrays[f"in_{name}_dram"] = a
        args.append(nc.dram_tensor(f"in_{name}_dram", a.shape, _mybir.dt.from_np(a.dtype), kind="ExternalInput").ap())
    for i, (shape, dtype) in enumerate(_OUTS):
        dt = _mybir.dt.from_np(_np.dtype(dtype))
        args.append(nc.dram_tensor(f"out_{i}_dram", shape, dt, kind="ExternalOutput").ap())
    cond_seq_kernel(nc, *args)
    r = _run(nc, [arrays], core_ids=[0])
    got = tuple(r.results[0][f"out_{i}_dram"] for i in range(len(_OUTS)))
    return got[0]
```
